# Optimizing a Trainium2 kernel written in Bass

```python
import numpy as np
import jax
import jax.numpy as jnp

def _softmax(x, axis=-1):
    return jax.nn.softmax(x, axis=axis)

def _gelu(x):
    return jax.nn.gelu(x, approximate=True)

def _silu(x):
    return jax.nn.silu(x)

def _sigmoid(x):
    return jax.nn.sigmoid(x)

def _layernorm(x, axis=-1, eps=1e-05):
    m = jnp.mean(x, axis=axis, keepdims=True)
    v = jnp.var(x, axis=axis, keepdims=True)
    return (x - m) / jnp.sqrt(v + eps)

def _scatter_add(tgt, idx, src, axis=0):
    return tgt.at[idx].add(src)

def _segment_sum(src, seg, n):
    return jax.ops.segment_sum(src, seg, n)
kernel_name = 'mk_adj_preln_d2_adj_r2_a7f0e6'

def setup_inputs(seed: int=0):
    np.random.seed(seed)
    _w = jnp.asarray

    def _rec_inputs():
        import jax
        import jax.numpy as jnp
        _gk = jax.random.key(seed)
        x = -0.001547 + 1.001 * jax.random.normal(jax.random.fold_in(_gk, 1), (64, 128, 128), jnp.float32)
        _w = (1.0 + jnp.arange(128, dtype=jnp.float32)) ** (-0.5)
        _w = _w / _w.mean()
        _pij = jnp.clip(0.03125 * _w[:, None] * _w[None, :], 0.0, 1.0)
        _a = jax.random.uniform(jax.random.fold_in(_gk, 2), (64, 128, 128)) < _pij
        _a = jnp.logical_or(_a, jnp.swapaxes(_a, -1, -2))
        _a = jnp.logical_or(_a, jnp.eye(128, dtype=bool))
        _af = _a.astype(jnp.float32)
        _af = _af * jax.random.uniform(jax.random.fold_in(_gk, 3), (64, 128, 128), jnp.float32, 0.05, 4.99997)
        adj = _af
        return (x, adj)
    x, adj = _rec_inputs()

    def _L0_gnn_setup():
        import jax, jax.numpy as jnp
        import numpy as np
        B, N, NAB, NF, NG = (8, 128, 128, 128, 64)
        CUTOFF = 5.0
        LN2 = float(np.log(2.0))

        def ssp(x):
            return jax.nn.softplus(x) - LN2
        key = jax.random.key(seed)
        ks = jax.random.split(key, 12)
        r = jax.random.normal(ks[0], (B, N, NAB), dtype=jnp.float32)
        e = jax.random.uniform(ks[1], (B, N, N), dtype=jnp.float32) * CUTOFF
        A = (jax.random.uniform(ks[2], (B, N, N)) < 0.3).astype(jnp.float32)
        s = 0.05
        W1 = jax.random.normal(ks[3], (NF, NG), dtype=jnp.float32) * s
        b1 = jnp.zeros((NF,), jnp.float32)
        W2 = jax.random.normal(ks[4], (NF, NF), dtype=jnp.float32) * s
        b2 = jnp.zeros((NF,), jnp.float32)
        Wa = jax.random.normal(ks[5], (NF, NAB), dtype=jnp.float32) * s
        Wd1 = jax.random.normal(ks[6], (NAB, NF), dtype=jnp.float32) * s
        bd1 = jnp.zeros((NAB,), jnp.float32)
        Wd2 = jax.random.normal(ks[7], (NAB, NAB), dtype=jnp.float32) * s
        bd2 = jnp.zeros((NAB,), jnp.float32)
        return {'r': r, 'e': e, 'A': A, 'W1': W1, 'b1': b1, 'W2': W2, 'b2': b2, 'Wa': Wa, 'Wd1': Wd1, 'bd1': bd1, 'Wd2': Wd2, 'bd2': bd2}
    _L0_gnn_all = _L0_gnn_setup()
    _L0_gnn_in = {k: v for k, v in _L0_gnn_all.items() if k in ('W1', 'b1', 'W2', 'b2', 'Wa', 'Wd1', 'bd1', 'Wd2', 'bd2')}
    del _L0_gnn_all

    def _L1_gnn_setup():
        import jax, jax.numpy as jnp
        import numpy as np
        B, N, U = (8, 2048, 128)
        AVG_DEG = 32.0
        key = jax.random.key(seed)
        k1, k2, k3 = jax.random.split(key, 3)
        x = jax.random.normal(k1, (B, N, U), dtype=jnp.float32)
        adj = (jax.random.uniform(k2, (B, N, N)) < AVG_DEG / N).astype(jnp.float32)
        W = jax.random.normal(k3, (U, U), dtype=jnp.float32) * 0.05
        b = jnp.zeros((U,), dtype=jnp.float32)
        return {'x': x, 'adj': adj, 'W': W, 'b': b}
    _L1_gnn_all = _L1_gnn_setup()
    _L1_gnn_in = {k: v for k, v in _L1_gnn_all.items() if k in ('W', 'b')}
    del _L1_gnn_all
    return {'x': x, 'adj': adj, 'L0_gnn_W1': _L0_gnn_in['W1'], 'L0_gnn_b1': _L0_gnn_in['b1'], 'L0_gnn_W2': _L0_gnn_in['W2'], 'L0_gnn_b2': _L0_gnn_in['b2'], 'L0_gnn_Wa': _L0_gnn_in['Wa'], 'L0_gnn_Wd1': _L0_gnn_in['Wd1'], 'L0_gnn_bd1': _L0_gnn_in['bd1'], 'L0_gnn_Wd2': _L0_gnn_in['Wd2'], 'L0_gnn_bd2': _L0_gnn_in['bd2'], 'L1_gnn_W': _L1_gnn_in['W'], 'L1_gnn_b': _L1_gnn_in['b']}

def reference(x, adj, L0_gnn_W1, L0_gnn_b1, L0_gnn_W2, L0_gnn_b2, L0_gnn_Wa, L0_gnn_Wd1, L0_gnn_bd1, L0_gnn_Wd2, L0_gnn_bd2, L1_gnn_W, L1_gnn_b):
    import jax
    import jax.numpy as jnp

    def _L0_gnn_ref(r, e, A, W1, b1, W2, b2, Wa, Wd1, bd1, Wd2, bd2):
        import jax, jax.numpy as jnp
        import numpy as np
        B, N, NAB, NF, NG = (8, 128, 128, 128, 64)
        CUTOFF = 5.0
        LN2 = float(np.log(2.0))

        def ssp(x):
            return jax.nn.softplus(x) - LN2
        offsets = jnp.linspace(0.0, CUTOFF, NG, dtype=jnp.float32)
        width = offsets[1] - offsets[0]
        coeff = -0.5 / (width * width)
        diff = e[:, :, :, None] - offsets
        g = jnp.exp(coeff * diff * diff)
        h = ssp(jnp.einsum('bijg,fg->bijf', g, W1) + b1)
        Wf = jnp.einsum('bijf,gf->bijg', h, W2) + b2
        rf = jnp.einsum('bjd,fd->bjf', r, Wa)
        Am = A[:, :, :, None]
        Wf = Wf * Am
        y = jnp.einsum('bjf,bijf->bif', rf, Wf * Am)
        y = ssp(jnp.einsum('bif,df->bid', y, Wd1) + bd1)
        y = jnp.einsum('bid,ed->bie', y, Wd2) + bd2
        return y

    def _L1_gnn_ref(x, adj, W, b):
        import jax, jax.numpy as jnp
        import numpy as np
        B, N, U = (8, 2048, 128)
        AVG_DEG = 32.0
        adj = jax.lax.stop_gradient(adj)

        def step(h):
            hn = jnp.einsum('bij,bjd->bid', adj, h)
            return jax.nn.swish(hn @ W + b)
        return step(step(x))
    h = jnp.maximum(_layernorm(x, axis=-1), 0.0)
    x = x + _L0_gnn_ref(h, adj, adj, L0_gnn_W1, L0_gnn_b1, L0_gnn_W2, L0_gnn_b2, L0_gnn_Wa, L0_gnn_Wd1, L0_gnn_bd1, L0_gnn_Wd2, L0_gnn_bd2)
    h = jnp.maximum(_layernorm(x, axis=-1), 0.0)
    x = x + _L1_gnn_ref(h, adj, L1_gnn_W, L1_gnn_b)
    return x

_drawn_inputs = setup_inputs


def setup_inputs(seed=0):
    import zlib

    import numpy as np

    out = dict(_drawn_inputs(seed))
    spreads = {'L0_gnn_b1': (0.0, 0.1),
     'L0_gnn_b2': (0.0, 0.1),
     'L0_gnn_bd1': (0.0, 0.1),
     'L0_gnn_bd2': (0.0, 0.1),
     'L1_gnn_b': (0.0, 0.529)}
    factors = {}
    for name, (base, spread) in spreads.items():
        noise = np.random.default_rng([zlib.crc32(name.encode()), seed]).standard_normal(out[name].shape)
        drawn = base * np.exp(spread * noise) if base else spread * noise
        out[name] = jnp.asarray(drawn.astype(out[name].dtype))
    for name, factor in factors.items():
        out[name] = (out[name] * factor).astype(out[name].dtype)
    return out
```

```python
from contextlib import ExitStack

import concourse.bass as bass
from concourse import mybir

ALU = mybir.AluOpType
ACT = mybir.ActivationFunctionType
F32 = mybir.dt.float32
BF16 = mybir.dt.bfloat16
F16 = mybir.dt.float16
I32 = mybir.dt.int32
AX = mybir.AxisListType

P = 128
NG = 64
TILES = 10
T = TILES * P
HALF = T // 2
CUTOFF = 5.0
WIDTH = CUTOFF / (NG - 1)
COEFF = -0.5 / (WIDTH * WIDTH)
EPS = 1e-5
SAFE = 40.0
ROWS = 4
LIMIT = T

C_ID, C_U, C_US, C_TC, C_NO, C_IO = 0, P, 2 * P, 3 * P, 3 * P + TILES, 3 * P + TILES + 1
C_ALL = C_IO + T


class Batch:

    def __init__(self, k, c):
        self.k, self.c = (0, 4 * k + c) if isinstance(k, int) else (k, c)
        self.static = isinstance(k, int)

    def __add__(self, d):
        return Batch(self.k, self.c + d)

    @property
    def n(self):
        return self.c if self.static else 4 * self.k + self.c

    @property
    def pair(self):
        return self.c // 2 if self.static else 2 * self.k + self.c // 2

    @property
    def half(self):
        return self.c // 4 if self.static else self.k + self.c // 4

    @property
    def p4(self):
        return self.c % 4

    @property
    def p2(self):
        return self.c % 2

    @property
    def pp(self):
        return (self.c // 2) % 2

    def within(self, nb):
        return not self.static or 0 <= self.c < nb


def wait(eng, sem, count):
    if not (isinstance(count, int) and count <= 0):
        eng.wait_ge(sem, count)


def settle(eng, S):
    eng.sem_inc(S["settled"], 1)


def build(nc, x, adj, W1, b1, W2, b2, Wa, Wd1, bd1, Wd2, bd2, LW, Lb, consts, out):
    NB = x.shape[0]
    assert NB % 4 == 0 and NB >= 12

    ctx = ExitStack()
    with ctx:
        def sb(name, shape, dt=F32):
            return ctx.enter_context(nc.sbuf_tensor(name, shape, dt))

        def ps(name, shape):
            return ctx.enter_context(nc.psum_tensor(name, shape, F32))

        def sem(name):
            return ctx.enter_context(nc.semaphore(name))

        e_dram = nc.dram_tensor("edge_values", (NB, TILES, P), F32).ap()

        cst = sb("cst", [P, C_ALL])
        ident = cst[:, C_ID:C_ID + P]
        tcol = cst[:, C_TC:C_TC + TILES]
        neg_off = cst[:, C_NO:C_NO + 1]
        upper = sb("upper", [P, P], BF16)
        upper_s = sb("upper_s", [P, P], BF16)
        iota = sb("iota", [P, T], F16)
        wraw = sb("wraw", [P, 5, P])
        wT = sb("wT", [P, 5, P])
        lw = sb("lw", [P, P])
        cols = sb("cols", [P, 2])
        bd2_bc = sb("bd2_bc", [P, P])
        W1T, W2T, WaT, Wd1T, Wd2T = (wT[:, k, :] for k in range(5))
        b1c, bd1c = (cols[:, k:k + 1] for k in range(2))
        half_c = sb("half_c", [P, 1])
        mhalf = sb("mhalf", [P, 2])
        ones = sb("ones", [P, P], BF16)
        b2row = sb("b2row", [P, P], BF16)
        lbrow = sb("lbrow", [P, 2, P], BF16)
        raw_bc = sb("raw_bc", [P, 2, P])
        spl_r = sb("spl_r", [P, 2, P])
        spl = sb("spl", [P, 3, 2, P], BF16)
        acc_b = sb("acc_b", [P, 2, 2, P])

        xin = [sb(f"xin{k}", [P, 2, P]) for k in range(2)]
        adjin = [sb(f"adjin{k}", [P, 2, P]) for k in range(2)]
        bn1 = sb("bn1", [P, 2, 6])
        mv1 = sb("mv1", [P, 2, 2])
        rs1 = sb("rs1", [P, 2])
        tt1 = sb("tt1", [P, 2, 2])
        nm1 = sb("nm1", [P, 2])
        h1 = sb("h1", [P, 2, P])
        h1T = sb("h1T", [P, 2, P])
        rf = [sb(f"rf{k}", [P, 2, P]) for k in range(2)]
        rfr = sb("rfr", [P, 2, P])
        rfS = [sb(f"rfS{k}", [P, 3, 2, P], BF16) for k in range(2)]
        adjT = [sb(f"adjT{k}", [P, 2, P]) for k in range(2)]
        adjr = sb("adjr", [P, 2, P])
        adjS = [sb(f"adjS{k}", [P, 3, 2, P], BF16) for k in range(2)]
        rank = sb("rank", [P, 2, P], F16)
        maskN = sb("maskN", [P, 2, P], BF16)
        maskT = sb("maskT", [P, 2, P], BF16)
        deg = sb("deg", [P, 2], BF16)
        oo = [sb(f"oo{k}", [P, 2, 2]) for k in range(2)]
        key = [sb(f"key{k}", [P, 2, P], F16) for k in range(2)]
        most = sb("most", [P, 2])

        Qend = sb("Qend", [P, T], F16)
        Qbeg = sb("Qbeg", [P, T], F16)
        Q = [sb(f"Q{k}", [P, T], F16) for k in range(4)]
        Ksb = sb("Ksb", [P, 2, 2, P])
        Gsb = sb("Gsb", [P, 2, 2, P])
        Wsc = [sb(f"Wsc{k}", [P, T]) for k in range(4)]
        eT = [sb(f"eT{k}", [P, TILES]) for k in range(4)]
        erow = [sb(f"erow{k}", [TILES, P]) for k in range(2)]
        eb = [sb(f"eb{k}", [P, HALF]) for k in range(2)]
        dsq = sb("dsq", [P, HALF])
        gau = sb("gau", [P, HALF])
        ex = sb("ex", [P, T])
        hid = [sb(f"hid{k}", [P, T]) for k in range(2)]
        msg = sb("msg", [P, 4, P])

        xpost = [sb(f"xpost{k}", [P, 2, P]) for k in range(2)]
        xb = sb("xb", [P, 2, P])
        adjL = [sb(f"adjL{k}", [P, 2, P]) for k in range(2)]
        adjM = [sb(f"adjM{k}", [P, 2, P]) for k in range(2)]
        yT = sb("yT", [P, 2, P])
        dabs = sb("dabs", [P, 2, P])
        drel = sb("drel", [P, 2, P])
        dexp = sb("dexp", [P, 2, P])
        dln = sb("dln", [P, 2, P])
        dsp = sb("dsp", [P, 2, P])
        cols2 = sb("cols2", [P, ROWS])
        x2 = [sb(f"x2_{k}", [P, 2, P]) for k in range(2)]
        bn2 = sb("bn2", [P, 2, 6])
        mv2 = sb("mv2", [P, 2, 2])
        rs2 = sb("rs2", [P, 2])
        tt2 = sb("tt2", [P, 2, 2])
        nm2 = sb("nm2", [P, 2])
        hs = [sb(f"hs{k}", [P, 2, P]) for k in range(3)]
        hnT = sb("hnT", [P, 2, P])
        zex = sb("zex", [P, 2, P])
        zcl = sb("zcl", [P, 2, P])
        zden = sb("zden", [P, 2, P])
        zrec = sb("zrec", [P, 2, P])
        res = [sb(f"res{k}", [P, 2, P]) for k in range(2)]

        psKV = ps("psKV", [P, 2, 2, 2, P])
        psGF = ps("psGF", [P, 2, 2, 2, P])
        psY = ps("psY", [P, 4, P])
        psX = ps("psX", [P, 2, 512])
        psM = ps("psM", [P, 4, P])
        psA = psM[:, 0:2, :]
        psW = psGF[:, 0, :, :, :].rearrange("p a b c -> p (a b) c")
        psE = psX[0:TILES, 1, 0:P]
        psO = psX[:, 1, P:P + 4]

        names = """w_in w_tr w_tr2 w_cast w_done c_in split_b rows_b
            x_in0 x_in1 a_in0 a_in1 xp_in0 xp_in1 e_out eb_in0 eb_in1 o_out0 o_out1
            bn1_d mv1_d rs1_d nm1_d h1_d h1Tp h1T_d rfp rf_d rfhi rfr_d rfmid rfS_d
            adjTp adjT_d ahi adjr_d amid adjS_d maskN_d maskT_d rank_d rank_c deg_d offs_d oo_d key_d most_d
            Qe_d Qb_d Q_d kx_d kc_d w_d et_d erow_d dsq_d gau_d x_d ex_d hid_d gw_d gc_d msg_d y_mm
            yT_d dp abs_d rel_d dexp_d dln_d dsp_d ep xb_d adjL_d adjM_d x2_d bn2_d mv2_d rs2_d nm2_d h2_d
            ve1_d ng1_d ve2_d ng2_d settled zc_d1 zc_d2 zden_d zrec_d hn_p1 hn_c1 z_p1 zex_d1 st_d1 hn_p2 hn_c2 z_p2 zex_d2 st_d2 res_d""".split()
        S = {k: sem(k) for k in names}
        W_LOADS = 16 * 12

        block = nc.Block()
        block.__enter__()

        def filter_tile(b, t):
            return (b + -2, t - 4) if t >= 4 else (b + -3, t + TILES - 4)

        def scatter_tile(b, t):
            return (b + -2, t - 7) if t >= 7 else (b + -3, t + TILES - 7)

        def prep_pair(b):
            return b + 2 if b.p2 == 0 else b + 1

        def rest_pair(b):
            return b + -5 if b.p2 == 1 else b + -6

        def steps(eng, step):
            for n in range(-3, 8):
                step(Batch(0, n))
            with eng.Fori(2, NB // 4 - 1) as k:
                for c in range(4):
                    step(Batch(k, c))
            for n in range(NB - 4, NB + 6):
                step(Batch(0, n))

        BANK_USES = [[("adjT", prep_pair, "adjT_d"), ("hn1", rest_pair, "hn_c1"), ("rank", prep_pair, "rank_c"),
                      ("z1", rest_pair, "st_d1"), ("hn2", rest_pair, "hn_c2"), ("z2", rest_pair, "st_d2")],
                     [("h1T", prep_pair, "h1T_d"), ("d", rest_pair, "rel_d"), ("rf", prep_pair, "rf_d"),
                      ("e", rest_pair, "x2_d")]]

        def bank_free(pe, b, use):
            at = [u[0] for u in BANK_USES[b.p2]].index(use) - 1
            for _ in range(20):
                if at < 0:
                    b = b + -1
                    at = len(BANK_USES[b.p2]) - 1
                _, pair_of, read = BANK_USES[b.p2][at]
                if pair_of(b).within(NB):
                    pe.wait_ge(S[read], pair_of(b).pair + 1)
                    return
                at -= 1

        ROUNDS = [slice(0, 3 * P), slice(3 * P, HALF)]
        ROUND_SLOT = [0, 2]

        @block.sync
        def _(sp):
            for k, w in enumerate((W1, W2, Wa, Wd1, Wd2)):
                sp.dma_start(wraw[:, k, 0:w.shape[1]], w).then_inc(S["w_in"], 16)
            sp.dma_start(wraw[:, 0, NG:2 * NG], W1).then_inc(S["w_in"], 16)
            sp.dma_start(cst[:, 0:C_IO], consts[:, 0:C_IO]).then_inc(S["c_in"], 16)
            sp.dma_start(cst[:, C_IO:], consts[0:1, C_IO:].to_broadcast((P, T))).then_inc(S["c_in"], 16)
            sp.dma_start(lw[:, :], LW).then_inc(S["w_in"], 16)
            for k, v in enumerate((b1, bd1)):
                sp.dma_start(cols[:, k:k + 1], v.rearrange("(p a) -> p a", a=1)).then_inc(S["w_in"], 16)
            for dst, v in ((bd2_bc[:, :], bd2), (raw_bc[:, 0, :], b2), (raw_bc[:, 1, :], Lb)):
                sp.dma_start(dst, v.rearrange("(a p) -> a p", a=1).to_broadcast((P, P))).then_inc(S["w_in"], 16)

            def load(q):
                wait(sp, S["h1_d"], 2 * q.pair - 2)
                settle(sp, S)
                sp.dma_start(xin[q.pp][:, :, :], x[bass.ds(q.n, 2)].rearrange("b n d -> n b d"))\
                  .then_inc(S[f"x_in{q.pp}"], 16)
                wait(sp, S["adjTp"], q.pair - 1)
                wait(sp, S["maskN_d"], q.pair - 1)
                settle(sp, S)
                sp.dma_start(adjin[q.pp][:, :, :], adj[bass.ds(q.n, 2)].rearrange("b n d -> n b d"))\
                  .then_inc(S[f"a_in{q.pp}"], 16)

            def step(b):
                if b.static and b.c == -3:
                    load(Batch(0, 0))
                    return
                if b.p2 == 0 and (b + 4).within(NB):
                    load(b + 4)
                if b.p2 == 1 and (b + -3).within(NB):
                    q = b + -3
                    wait(sp, S["xb_d"], q.pair - 1)
                    settle(sp, S)
                    sp.dma_start(xpost[q.pp][:, :, :], x[bass.ds(q.n, 2)].rearrange("b n d -> n b d"))\
                      .then_inc(S[f"xp_in{q.pp}"], 16)
                o = b + -7
                if b.p2 == 1 and o.within(NB):
                    sp.wait_ge(S["res_d"], o.pair + 1)
                    settle(sp, S)
                    sp.dma_start(out[bass.ds(o.n, 2)].rearrange("b n d -> n b d"), res[o.pp][:, :, :])\
                      .then_inc(S[f"o_out{o.pp}"], 16)
                m = b + -1
                if m.within(NB):
                    sp.wait_ge(S["erow_d"], m.n + 1)
                    settle(sp, S)
                    sp.dma_start(e_dram[bass.ds(m.n, 1)].rearrange("b t p -> (b t) p"), erow[m.p2][:, :])\
                      .then_inc(S["e_out"], 16)
                    sp.wait_ge(S["e_out"], 16 * m.n + 16)
                    settle(sp, S)
                    wait(sp, S["dsq_d"], m.n - 1)
                    settle(sp, S)
                    for s in range(2):
                        src = e_dram[bass.ds(m.n, 1), s * TILES // 2:(s + 1) * TILES // 2]
                        sp.dma_start(eb[m.p2][s * NG:(s + 1) * NG, :],
                                     src.rearrange("b t p -> b (t p)").to_broadcast((NG, HALF)))\
                          .then_inc(S[f"eb_in{m.p2}"], 16)

            steps(sp, step)
            for k in range(2):
                sp.wait_ge(S[f"o_out{k}"], 16 * NB // 4)

        @block.tensor
        def _(pe):
            def mm(o, a, b, start=True, stop=True):
                return nc.tensor.matmul(o, a, b, start=start, stop=stop)

            pe.wait_ge(S["c_in"], 32)
            pe.wait_ge(S["w_in"], W_LOADS)
            for k in range(4):
                nc.tensor.transpose(psW[:, k, :], wraw[:, k, :], ident).then_inc(S["w_tr"], 1)
            nc.tensor.transpose(psA[:, 0, :], wraw[:, 4, :], ident).then_inc(S["w_tr2"], 1)
            pe.wait_ge(S["w_done"], 2)
            pe.wait_ge(S["w_cast"], 7)
            pe.wait_ge(S["rows_b"], 6)

            def first_product(e, c):
                if c == 0:
                    pe.wait_ge(S["gau_d"], e.n + 1)
                    pe.wait_ge(S["erow_d"], e.n + 1)
                    pairs = e.pair + 2
                    pe.wait_ge(S["oo_d"], min(pairs, NB // 2) if e.static else pairs)
                wait(pe, S["ex_d"], 2 * e.n + c)
                for s in range(2):
                    part = ROUNDS[c]
                    last = mm(psX[:, s, 0:part.stop - part.start], W1T[s * NG:(s + 1) * NG, :],
                              gau[s * NG:(s + 1) * NG, part])
                    last.then_inc(S["x_d"], 1)

            def expand(b, t):
                if t == 0:
                    pe.wait_ge(S["Q_d"], b.n + 1)
                    pe.wait_ge(S["key_d"], 2 * b.pair + 2)
                    pe.wait_ge(S["adjS_d"], b.pair + 1)
                c, k2 = t // 2, (b.p2 + t // 2) % 2
                if t % 2 == 0:
                    wait(pe, S["kc_d"], TILES // 2 * b.n + c - 1)
                    wait(pe, S["w_d"], TILES * b.n + 2 * (c - 1))
                q = Q[b.p4][:, t * P:(t + 1) * P]
                mm(psKV[:, k2, 0, t % 2, :], q, key[b.pp][:, b.p2, :])
                for k in range(3):
                    last = mm(psKV[:, k2, 1, t % 2, :], q, adjS[b.pp][:, k, b.p2, :], k == 0, k == 2)
                last.then_inc(S["kx_d"], 1)

            def filters(e, t):
                if t == 0:
                    pe.wait_ge(S["rfS_d"], e.pair + 1)
                if t in (0, 3):
                    pe.wait_ge(S["hid_d"], 2 * e.n + (2 if t else 1))
                c, k2 = t // 2, (e.p2 + t // 2) % 2
                if t % 2 == 0:
                    wait(pe, S["gc_d"], TILES // 2 * e.n + c - 1)
                    wait(pe, S["msg_d"], TILES * e.n + 2 * (c - 1))
                for k in range(3):
                    mm(psGF[:, k2, 0, t % 2, :], Q[e.p4][:, t * P:(t + 1) * P], rfS[e.pp][:, k, e.p2, :],
                       k == 0, k == 2)
                mm(psGF[:, k2, 1, t % 2, :], hid[e.p2][:, t * P:(t + 1) * P], W2T, True, False)
                mm(psGF[:, k2, 1, t % 2, :], ones[:, :], b2row[:, :], False, True).then_inc(S["gw_d"], 1)

            def scatter(e, t):
                if t == 0:
                    wait(pe, S["yT_d"], e.n)
                pe.wait_ge(S["msg_d"], TILES * e.n + t + 1)
                mm(psY[:, 0, :], msg[:, (TILES * e.c + t) % 4, :], Wsc[e.p4][:, t * P:(t + 1) * P],
                   t == 0, t == TILES - 1).then_inc(S["y_mm"], 1)

            def both(f):
                for k in range(2):
                    last = f(k)
                return last

            def rows_and_offsets(b):
                m, q = b + -1, prep_pair(b)
                wait(pe, S["oo_d"], min(q.pair, NB // 2) if b.static else q.pair)
                if m.within(NB):
                    pe.wait_ge(S["w_d"], TILES * m.n + TILES)
                    wait(pe, S["ex_d"], 2 * m.n)
                    nc.tensor.transpose(psE, eT[m.p4][:, :], ident).then_inc(S["et_d"], 1)
                if q.within(NB) and b.p2 == 1:
                    pe.wait_ge(S["deg_d"], q.pair + 1)
                    wait(pe, S["ex_d"], 2 * (b.n - 1))
                    mm(psO[:, 0:2], upper_s[:, :], deg[:, :])
                    mm(psO[:, 2:4], upper[:, :], deg[:, :]).then_inc(S["offs_d"], 1)

            def prep_products(b, t):
                q = prep_pair(b)
                c = q.pair
                if not q.within(NB):
                    return
                if b.p2 == 0 and t == 0:
                    pe.wait_ge(S[f"a_in{q.pp}"], 16 * q.half + 16)
                    bank_free(pe, b, "adjT")
                    both(lambda k: nc.tensor.transpose(psA[:, k, :], adjin[q.pp][:, k, :], ident))\
                        .then_inc(S["adjTp"], 1)
                if b.p2 == 0 and t == 2:
                    pe.wait_ge(S["maskN_d"], c + 1)
                    bank_free(pe, b, "rank")
                    both(lambda k: mm(psA[:, k, :], maskN[:, k, :], upper[:, :])).then_inc(S["rank_d"], 1)
                if b.p2 == 1 and t == 1:
                    pe.wait_ge(S["h1_d"], 2 * c + 2)
                    bank_free(pe, b, "h1T")
                    both(lambda k: nc.tensor.transpose(psA[:, k, :], h1[:, k, :], ident))\
                        .then_inc(S["h1Tp"], 1)
                if b.p2 == 1 and t == 5:
                    pe.wait_ge(S["h1T_d"], c + 1)
                    bank_free(pe, b, "rf")
                    both(lambda k: mm(psA[:, k, :], h1T[:, k, :], WaT)).then_inc(S["rfp"], 1)

            def rest_products(b, t):
                s = rest_pair(b)
                d = s.pair
                if not s.within(NB):
                    return
                if b.p2 == 1 and t == 3:
                    pe.wait_ge(S["yT_d"], 2 * d + 2)
                    bank_free(pe, b, "d")
                    mm(psA, Wd1T, yT[:, :, :]).then_inc(S["dp"], 1)
                if b.p2 == 1 and t == 7:
                    pe.wait_ge(S["dsp_d"], d + 1)
                    bank_free(pe, b, "e")
                    both(lambda k: mm(psA[:, k, :], dsp[:, k, :], Wd2T)).then_inc(S["ep"], 1)
                if b.p2 == 0:
                    for n, t_adj, t_w in ((1, 1, 3), (2, 6, 8)):
                        if t == t_adj:
                            if n == 1:
                                pe.wait_ge(S["h2_d"], 2 * d + 2)
                                pe.wait_ge(S["adjM_d"], d + 1)
                            else:
                                pe.wait_ge(S["st_d1"], d + 1)
                            bank_free(pe, b, f"hn{n}")
                            both(lambda k: mm(psA[:, k, :], hs[n - 1][:, k, :], adjM[s.pp][:, k, :]))\
                                .then_inc(S[f"hn_p{n}"], 1)
                        if t == t_w:
                            pe.wait_ge(S[f"hn_c{n}"], d + 1)
                            bank_free(pe, b, f"z{n}")
                            for k in range(2):
                                mm(psA[:, k, :], hnT[:, k, :], lw[:, :], True, False)
                                last = mm(psA[:, k, :], ones[:, :], lbrow[:, 0, :], False, True)
                            last.then_inc(S[f"z_p{n}"], 1)

            def step(b):
                for t in range(TILES):
                    if t in ROUND_SLOT and (b + -2).within(NB):
                        first_product(b + -2, ROUND_SLOT.index(t))
                    if b.within(NB):
                        expand(b, t)
                    e, u = filter_tile(b, t)
                    if e.within(NB):
                        filters(e, u)
                    if t == 3:
                        rows_and_offsets(b)
                    prep_products(b, t)
                    rest_products(b, t)
                    e, u = scatter_tile(b, t)
                    if e.within(NB):
                        scatter(e, u)

            steps(pe, step)

        @block.vector
        def _(dve):
            v = nc.vector
            dve.wait_ge(S["c_in"], 32)
            v.tensor_copy(upper[:, :], cst[:, C_U:C_U + P]).then_inc(S["w_cast"], 1)
            v.tensor_copy(upper_s[:, :], cst[:, C_US:C_US + P]).then_inc(S["w_cast"], 1)
            v.tensor_copy(iota[:, :], cst[:, C_IO:C_IO + T]).then_inc(S["w_cast"], 1)
            v.memset(most[:, :], 0.0).then_inc(S["w_cast"], 1)
            v.memset(half_c[:, :], 0.5).then_inc(S["w_cast"], 1)
            v.memset(mhalf[:, :], -0.5).then_inc(S["w_cast"], 1)
            v.memset(ones[:, :], 1.0).then_inc(S["w_cast"], 1)
            dve.wait_ge(S["w_in"], W_LOADS)
            v.tensor_copy(spl[:, 0], raw_bc[:, :, :]).then_inc(S["split_b"], 1)
            dve.wait_ge(S["split_b"], 1)
            v.tensor_tensor(spl_r[:, :, :], raw_bc[:, :, :], spl[:, 0], ALU.subtract).then_inc(S["split_b"], 1)
            dve.wait_ge(S["split_b"], 2)
            v.tensor_copy(spl[:, 1], spl_r[:, :, :]).then_inc(S["split_b"], 1)
            dve.wait_ge(S["split_b"], 3)
            v.tensor_tensor(spl[:, 2], spl_r[:, :, :], spl[:, 1], ALU.subtract).then_inc(S["split_b"], 1)
            dve.wait_ge(S["split_b"], 4)
            v.tensor_scalar(acc_b[:, 0], spl[:, 0], ident[:, 0:1], None, ALU.mult).then_inc(S["rows_b"], 1)
            dve.wait_ge(S["rows_b"], 1)
            v.scalar_tensor_tensor(acc_b[:, 1], spl[:, 1], ident[:, 1:2], acc_b[:, 0], ALU.mult, ALU.add)\
             .then_inc(S["rows_b"], 1)
            dve.wait_ge(S["rows_b"], 2)
            v.scalar_tensor_tensor(acc_b[:, 0], spl[:, 2], ident[:, 2:3], acc_b[:, 1], ALU.mult, ALU.add)\
             .then_inc(S["rows_b"], 1)
            dve.wait_ge(S["rows_b"], 3)
            v.tensor_copy(b2row[:, :], acc_b[:, 0, 0, :]).then_inc(S["rows_b"], 1)
            v.tensor_copy(lbrow[:, 0, :], acc_b[:, 0, 1, :]).then_inc(S["rows_b"], 1)
            v.tensor_copy(lbrow[:, 1, :], acc_b[:, 0, 1, :]).then_inc(S["rows_b"], 1)
            dve.wait_ge(S["w_tr"], 4)
            v.tensor_copy(wT[:, 0:4, :], psW).then_inc(S["w_done"], 1)
            dve.wait_ge(S["w_tr2"], 1)
            v.tensor_copy(wT[:, 4, :], psA[:, 0, :]).then_inc(S["w_done"], 1)
            dve.wait_ge(S["w_cast"], 7)

            def moments(c, xt, bn, mv, s_bn, s_mv, stage):
                if stage == 0:
                    for k in range(2):
                        v.bn_stats(bn[:, k, :], xt[:, k, :]).then_inc(s_bn, 1)
                if stage == 1:
                    dve.wait_ge(s_bn, 2 * c + 2)
                    settle(dve, S)
                    for k in range(2):
                        v.bn_aggr(mv[:, k, :], bn[:, k, :]).then_inc(s_mv, 1)

            def list_edges(b, t):
                c, k2 = t // 2, (b.p2 + t // 2) % 2
                dve.wait_ge(S["kc_d"], TILES // 2 * b.n + c + 1)
                if t == 0:
                    wait(dve, S["y_mm"], TILES * b.n - 3 * TILES)
                    wait(dve, S["et_d"], b.n - 3)
                v.scalar_tensor_tensor(Wsc[b.p4][:, t * P:(t + 1) * P], Ksb[:, k2, t % 2, :],
                                       tcol[:, t:t + 1], psKV[:, k2, 1, t % 2, :], ALU.is_equal, ALU.mult,
                                       accum_out=eT[b.p4][:, t:t + 1]).then_inc(S["w_d"], 1)

            def message(e, t):
                c, k2 = t // 2, (e.p2 + t // 2) % 2
                dve.wait_ge(S["gc_d"], TILES // 2 * e.n + c + 1)
                wait(dve, S["y_mm"], TILES * e.n + t - 3)
                v.scalar_tensor_tensor(msg[:, (TILES * e.c + t) % 4, :], psGF[:, k2, 1, t % 2, :], eT[e.p4][:, t:t + 1],
                                       Gsb[:, k2, t % 2, :], ALU.mult, ALU.mult).then_inc(S["msg_d"], 1)

            def owners(m, t):
                if t == 6:
                    dve.wait_ge(S["oo_d"], m.pair + 1)
                    wait(dve, S["Q_d"], m.n)
                    v.tensor_scalar(Qend[:, :], iota[:, :], oo[m.pp][:, 1, m.p2:m.p2 + 1], None, ALU.is_gt)\
                     .then_inc(S["Qe_d"], 1)
                if t == 7:
                    v.tensor_scalar(Qbeg[:, :], iota[:, :], oo[m.pp][:, 0, m.p2:m.p2 + 1], None, ALU.is_gt)\
                     .then_inc(S["Qb_d"], 1)
                if t == 8:
                    dve.wait_ge(S["Qe_d"], m.n + 1)
                    dve.wait_ge(S["Qb_d"], m.n + 1)
                    wait(dve, S["gw_d"], TILES * m.n - 3 * TILES)
                    v.tensor_tensor(Q[m.p4][:, :], Qbeg[:, :], Qend[:, :], ALU.subtract)\
                     .then_inc(S["Q_d"], 1)

            def sum_out(e):
                dve.wait_ge(S["y_mm"], TILES * e.n + TILES)
                if e.p2 == 0:
                    wait(dve, S["dp"], e.pair)
                v.tensor_copy(yT[:, e.p2, :], psY[:, 0, :]).then_inc(S["yT_d"], 1)

            def clamped(d, n):
                dve.wait_ge(S[f"z_p{n}"], d + 1)
                wait(dve, S["zex_d2"], d) if n == 1 else dve.wait_ge(S["zex_d1"], d + 1)
                v.tensor_scalar(zcl[:, :, :], psA, -88.0, None, ALU.max).then_inc(S[f"zc_d{n}"], 1)

            def gated(d, n):
                dve.wait_ge(S[f"zex_d{n}"], d + 1)
                wait(dve, S["st_d2"], d) if n == 1 else dve.wait_ge(S["st_d1"], d + 1)
                if n == 1:
                    wait(dve, S["hn_p2"], d)
                else:
                    wait(dve, S["res_d"], d)
                v.tensor_scalar(zden[:, :, :], zex[:, :, :], 1.0, None, ALU.add).then_inc(S["zden_d"], 1)
                dve.wait_ge(S["zden_d"], 2 * d + n)
                v.reciprocal(zrec[:, :, :], zden[:, :, :]).then_inc(S["zrec_d"], 1)
                dve.wait_ge(S["zrec_d"], 2 * d + n)
                v.tensor_tensor(hs[n][:, :, :], psA, zrec[:, :, :], ALU.mult)\
                 .then_inc(S[f"st_d{n}"], 1)

            def prep_vectors(b, t):
                q = prep_pair(b)
                c = q.pair
                if not q.within(NB):
                    return
                if b.p2 == 0:
                    if t == 0:
                        dve.wait_ge(S[f"x_in{q.pp}"], 16 * q.half + 16)
                        moments(c, xin[q.pp], bn1, mv1, S["bn1_d"], S["mv1_d"], 0)
                    if t == 1:
                        wait(dve, S["nm1_d"], c)
                        moments(c, xin[q.pp], bn1, mv1, S["bn1_d"], S["mv1_d"], 1)
                    if t == 1:
                        dve.wait_ge(S["adjTp"], c + 1)
                        wait(dve, S["adjL_d"], c - 1)
                        wait(dve, S["adjS_d"], c - 1)
                        wait(dve, S["maskT_d"], c - 1)
                        v.tensor_copy(adjT[q.pp][:, :, :], psA).then_inc(S["adjT_d"], 1)
                    if t == 3:
                        dve.wait_ge(S["rank_d"], c + 1)
                        wait(dve, S["key_d"], 2 * c)
                        v.tensor_copy(rank[:, :, :], psA).then_inc(S["rank_c"], 1)
                    if t == 4:
                        dve.wait_ge(S["rank_c"], c + 1)
                        wait(dve, S["offs_d"], c)
                        v.tensor_copy(deg[:, :], rank[:, :, P - 1]).then_inc(S["deg_d"], 1)
                else:
                    if t == 4:
                        dve.wait_ge(S["offs_d"], c + 1)
                        if (b + -1).within(NB):
                            dve.wait_ge(S["erow_d"], b.n)
                        wait(dve, S["key_d"], 2 * c - 2)
                        wait(dve, S["Qb_d"], 2 * c - 2)
                        wait(dve, S["Qe_d"], 2 * c - 2)
                        wait(dve, S["most_d"], c - 1)
                        v.tensor_copy(oo[q.pp][:, :, :], psO).then_inc(S["oo_d"], 1)
                    if t == 5:
                        dve.wait_ge(S["oo_d"], c + 1)
                        dve.wait_ge(S["maskT_d"], c + 1)
                        wait(dve, S["kx_d"], 2 * TILES * (c - 1))
                        for k in range(2):
                            v.scalar_tensor_tensor(key[q.pp][:, k, :], rank[:, k, :],
                                                   oo[q.pp][:, 0, k:k + 1], maskT[:, k, :],
                                                   ALU.add, ALU.mult).then_inc(S["key_d"], 1)
                    if t == 6:
                        wait(dve, S["most_d"], c)
                        v.tensor_tensor(most[:, :], most[:, :], oo[q.pp][:, 1, :], ALU.max)\
                         .then_inc(S["most_d"], 1)

            def rest_vectors(b, t):
                s = rest_pair(b)
                d = s.pair
                if s.within(NB) and b.p2 == 1:
                    if t == 4:
                        dve.wait_ge(S["abs_d"], d + 1)
                        wait(dve, S["dsp_d"], d)
                        v.tensor_scalar(drel[:, :, :], psA, bd1c, 0.0, ALU.add, ALU.max)\
                         .then_inc(S["rel_d"], 1)
                    if t == 6:
                        dve.wait_ge(S["dln_d"], d + 1)
                        dve.wait_ge(S["rel_d"], d + 1)
                        wait(dve, S["ep"], d)
                        v.tensor_tensor(dsp[:, :, :], drel[:, :, :], dln[:, :, :], ALU.add)\
                         .then_inc(S["dsp_d"], 1)
                    if t == 8:
                        dve.wait_ge(S["ep"], d + 1)
                        dve.wait_ge(S["xb_d"], d + 1)
                        wait(dve, S["res_d"], d - 1)
                        wait(dve, S["h2_d"], 2 * d - 2)
                        v.tensor_tensor(x2[s.pp][:, :, :], psA, xb[:, :, :], ALU.add)\
                         .then_inc(S["x2_d"], 1)
                    if t == 9:
                        dve.wait_ge(S["x2_d"], d + 1)
                        moments(d, x2[s.pp], bn2, mv2, S["bn2_d"], S["mv2_d"], 0)
                    if t == 9:
                        wait(dve, S["nm2_d"], d)
                        moments(d, x2[s.pp], bn2, mv2, S["bn2_d"], S["mv2_d"], 1)
                if s.within(NB) and b.p2 == 0:
                    if t == 3:
                        clamped(d, 1)
                    if t == 5:
                        gated(d, 1)
                    if t == 8:
                        clamped(d, 2)
                if (b + -7).within(NB) and b.p2 == 1 and t == 0:
                    gated((b + -7).pair, 2)
                if (b + -3).within(NB) and t == 6:
                    sum_out(b + -3)

            def step(b):
                for t in range(TILES):
                    e, u = filter_tile(b, t)
                    if t % 2 == 1:
                        for k in (1, 0):
                            if b.within(NB):
                                list_edges(b, t - k)
                        for k in (1, 0):
                            if e.within(NB):
                                message(e, u - k)
                    if (b + 1).within(NB):
                        owners(b + 1, t)
                    prep_vectors(b, t)
                    rest_vectors(b, t)

            steps(dve, step)

        @block.scalar
        def _(act):
            a = nc.scalar.activation
            nc.scalar.preload_act_table_set("natural_log_exp_and_others")
            act.wait_ge(S["w_in"], W_LOADS)
            act.wait_ge(S["c_in"], 32)
            act.wait_ge(S["w_cast"], 7)

            def hidden(e, c):
                part = ROUNDS[c]
                exp_at = ex[:, :].rearrange("p (s n) -> p s n", s=2)[:, :, part]
                hid_at = hid[e.p2][:, :].rearrange("p (s n) -> p s n", s=2)[:, :, part]
                act.wait_ge(S["x_d"], 4 * e.n + 2 * c + 2)
                wait(act, S["hid_d"], 2 * e.n + c - 1)
                a(exp_at, psX[:, :, 0:part.stop - part.start], ACT.Exp, bias=b1c).then_inc(S["ex_d"], 1)
                act.wait_ge(S["ex_d"], 2 * e.n + c + 1)
                wait(act, S["gw_d"], TILES * e.n - TILES)
                a(hid_at, exp_at, ACT.Ln, bias=half_c[:, :], scale=0.5).then_inc(S["hid_d"], 1)

            def step(b):
                q, s = prep_pair(b), rest_pair(b)
                c, d = q.pair, s.pair
                prep, rest = q.within(NB), s.within(NB)
                for t in range(TILES):
                    if t in ROUND_SLOT and (b + -2).within(NB):
                        hidden(b + -2, ROUND_SLOT.index(t))
                    if t == 0 and rest and b.p2 == 0:
                        act.wait_ge(S["nm2_d"], d + 1)
                        wait(act, S["hn_p1"], d)
                        for k in range(2):
                            a(hs[0][:, k, :], x2[s.pp][:, k, :], ACT.Relu, bias=nm2[:, k:k + 1],
                              scale=rs2[:, k:k + 1]).then_inc(S["h2_d"], 1)
                    if t % 2 == 1:
                        h = t // 2
                        if b.within(NB):
                            act.wait_ge(S["kx_d"], TILES * b.n + 2 * h + 2)
                            wait(act, S["w_d"], TILES * b.n + 2 * (h - 1))
                            a(Ksb[:, (b.p2 + h) % 2], psKV[:, (b.p2 + h) % 2, 0], ACT.Copy).then_inc(S["kc_d"], 1)
                        e, u = filter_tile(b, t)
                        h = u // 2
                        if e.within(NB):
                            act.wait_ge(S["gw_d"], TILES * e.n + 2 * h + 2)
                            wait(act, S["msg_d"], TILES * e.n + 2 * (h - 1))
                            a(Gsb[:, (e.p2 + h) % 2], psGF[:, (e.p2 + h) % 2, 0], ACT.Copy).then_inc(S["gc_d"], 1)
                    m = b + -1
                    if m.within(NB) and t == 4:
                        act.wait_ge(S["et_d"], m.n + 1)
                        if b.p2 == 1 and prep:
                            act.wait_ge(S["offs_d"], c + 1)
                        wait(act, S["e_out"], 16 * (m.n - 1))
                        a(erow[m.p2][:, :], psE, ACT.Copy).then_inc(S["erow_d"], 1)
                    if prep:
                        if t == 3 and b.p2 == 0:
                            act.wait_ge(S["nm1_d"], c + 1)
                            wait(act, S["h1Tp"], c)
                            for k in range(2):
                                a(h1[:, k, :], xin[q.pp][:, k, :], ACT.Relu, bias=nm1[:, k:k + 1],
                                  scale=rs1[:, k:k + 1]).then_inc(S["h1_d"], 1)
                        if t == 1 and b.p2 == 1:
                            act.wait_ge(S["h1Tp"], c + 1)
                            wait(act, S["rfp"], c)
                            a(h1T[:, :, :], psA, ACT.Copy).then_inc(S["h1T_d"], 1)
                        if t == 5 and b.p2 == 1:
                            act.wait_ge(S["rfp"], c + 1)
                            wait(act, S["rfr_d"], c - 1)
                            wait(act, S["rfhi"], c - 1)
                            a(rf[q.pp][:, :, :], psA, ACT.Copy).then_inc(S["rf_d"], 1)
                    if rest and b.p2 == 1:
                        if t == 3:
                            act.wait_ge(S["dp"], d + 1)
                            wait(act, S["dexp_d"], d)
                            a(dabs[:, :, :], psA, ACT.Abs, bias=bd1c).then_inc(S["abs_d"], 1)
                        if t == 4:
                            act.wait_ge(S["abs_d"], d + 1)
                            wait(act, S["dln_d"], d)
                            a(dexp[:, :, :], dabs[:, :, :], ACT.Exp, scale=-1.0).then_inc(S["dexp_d"], 1)
                        if t == 5:
                            act.wait_ge(S["dexp_d"], d + 1)
                            wait(act, S["dsp_d"], d)
                            a(dln[:, :, :], dexp[:, :, :], ACT.Ln, bias=half_c[:, :], scale=0.5)\
                                .then_inc(S["dln_d"], 1)
                    if rest and b.p2 == 0:
                        for n, t0, t1 in ((1, 1, 3), (2, 6, 8)):
                            if t == t0:
                                act.wait_ge(S[f"hn_p{n}"], d + 1)
                                wait(act, S["z_p2"], d) if n == 1 else act.wait_ge(S["z_p1"], d + 1)
                                a(hnT[:, :, :], psA, ACT.Copy).then_inc(S[f"hn_c{n}"], 1)
                            if t == t1:
                                act.wait_ge(S[f"zc_d{n}"], d + 1)
                                wait(act, S["st_d2"], d) if n == 1 else act.wait_ge(S["st_d1"], d + 1)
                                a(zex[:, :, :], zcl[:, :, :], ACT.Exp, scale=-1.0).then_inc(S[f"zex_d{n}"], 1)
                    if m.within(NB) and t == 9:
                        act.wait_ge(S[f"eb_in{m.p2}"], 32 * (2 * m.half + m.p4 // 2) + 32)
                        wait(act, S["gau_d"], m.n)
                        a(dsq[:, :], eb[m.p2][:, :], ACT.Square, bias=neg_off).then_inc(S["dsq_d"], 1)
                        act.wait_ge(S["dsq_d"], m.n + 1)
                        wait(act, S["x_d"], 4 * m.n)
                        a(gau[:, :], dsq[:, :], ACT.Exp, scale=COEFF).then_inc(S["gau_d"], 1)

            steps(act, step)

        @block.gpsimd
        def _(pool):
            g = nc.gpsimd
            pool.wait_ge(S["w_in"], W_LOADS)
            pool.wait_ge(S["w_cast"], 7)

            def split(part, rest, src, s_hi, s_rest, s_mid, s_all, c, read):
                read()
                settle(pool, S)
                g.tensor_copy(part[:, 0], src).then_inc(s_hi, 1)
                pool.wait_ge(s_hi, c + 1)
                wait(pool, s_all, c)
                g.tensor_tensor(rest, src, part[:, 0], ALU.subtract).then_inc(s_rest, 1)
                pool.wait_ge(s_rest, c + 1)
                settle(pool, S)
                g.tensor_copy(part[:, 1], rest).then_inc(s_mid, 1)
                pool.wait_ge(s_mid, c + 1)
                g.tensor_tensor(part[:, 2], rest, part[:, 1], ALU.subtract).then_inc(s_all, 1)

            def deviations(c, mv, tt, rs, nm, names, read):
                s_mv, s_ve, s_ng, s_rs, s_nm = (S[k] for k in names)
                pool.wait_ge(s_mv, 2 * c + 2)
                wait(pool, s_nm, c)
                settle(pool, S)
                g.tensor_scalar(tt[:, 0], mv[:, :, 1], EPS, None, ALU.add).then_inc(s_ve, 1)
                g.tensor_scalar(tt[:, 1], mv[:, :, 0], -1.0, None, ALU.mult).then_inc(s_ng, 1)
                pool.wait_ge(s_ve, c + 1)
                wait(pool, read, 2 * c)
                g.tensor_tensor(rs[:, :], tt[:, 0], mhalf[:, :], ALU.pow).then_inc(s_rs, 1)
                pool.wait_ge(s_ng, c + 1)
                pool.wait_ge(s_rs, c + 1)
                g.tensor_tensor(nm[:, :], tt[:, 1], rs[:, :], ALU.mult).then_inc(s_nm, 1)

            def step(b):
                q, r, o = prep_pair(b), b + -1, b + -7
                c = q.pair
                if q.within(NB) and b.p2 == 0:
                    deviations(c, mv1, tt1, rs1, nm1, ("mv1_d", "ve1_d", "ng1_d", "rs1_d", "nm1_d"), S["h1_d"])
                if q.within(NB) and b.p2 == 0:
                    pool.wait_ge(S[f"a_in{q.pp}"], 16 * q.half + 16)
                    wait(pool, S["rank_d"], c)
                    settle(pool, S)
                    g.tensor_scalar(maskN[:, :, :], adjin[q.pp][:, :, :], 0.0, 0.0, ALU.is_equal, ALU.is_equal)\
                     .then_inc(S["maskN_d"], 1)
                    pool.wait_ge(S["adjT_d"], c + 1)
                    aT = adjT[q.pp][:, :, :]
                    wait(pool, S["key_d"], 2 * c)
                    settle(pool, S)
                    g.tensor_scalar(maskT[:, :, :], aT, 0.0, 0.0, ALU.is_equal, ALU.is_equal).then_inc(S["maskT_d"], 1)
                    split(adjS[q.pp], adjr[:, :, :], aT, S["ahi"], S["adjr_d"], S["amid"], S["adjS_d"], c,
                          lambda: wait(pool, S["kx_d"], 2 * TILES * (c - 1)))
                if b.within(NB) and b.p2 == 0:
                    c = b.pair
                    pool.wait_ge(S["rf_d"], c + 1)
                    split(rfS[b.pp], rfr[:, :, :], rf[b.pp][:, :, :], S["rfhi"], S["rfr_d"], S["rfmid"],
                          S["rfS_d"], c, lambda: wait(pool, S["gw_d"], 2 * TILES * (c - 1)))
                if b.p2 == 1 and o.within(NB):
                    u = o.pair
                    pool.wait_ge(S["st_d2"], u + 1)
                    wait(pool, S[f"o_out{o.pp}"], 16 * o.half)
                    g.tensor_tensor(res[o.pp][:, :, :], x2[o.pp][:, :, :], hs[2][:, :, :], ALU.add)\
                     .then_inc(S["res_d"], 1)
                if b.p2 == 1 and r.within(NB):
                    wait(pool, S["adjM_d"], r.pair - 1)
                    settle(pool, S)
                    g.tensor_copy(adjL[r.pp][:, :, :], adjT[r.pp][:, :, :]).then_inc(S["adjL_d"], 1)
                r = b + -3
                if b.p2 == 1 and r.within(NB):
                    u = r.pair
                    pool.wait_ge(S["adjL_d"], u + 1)
                    wait(pool, S["hn_p2"], u - 1)
                    settle(pool, S)
                    g.tensor_copy(adjM[r.pp][:, :, :], adjL[r.pp][:, :, :]).then_inc(S["adjM_d"], 1)
                    pool.wait_ge(S[f"xp_in{r.pp}"], 16 * r.half + 16)
                    wait(pool, S["x2_d"], u)
                    for k in range(2):
                        last = g.tensor_tensor(xb[:, k, :], xpost[r.pp][:, k, :], bd2_bc[:, :], ALU.add)
                    last.then_inc(S["xb_d"], 1)

                s = rest_pair(b)
                if b.p2 == 1 and s.within(NB):
                    deviations(s.pair, mv2, tt2, rs2, nm2, ("mv2_d", "ve2_d", "ng2_d", "rs2_d", "nm2_d"),
                               S["h2_d"])

            steps(pool, step)

        block.__exit__(None, None, None)

        ORDER = {
            "pe": ("count", "hT rf aT", "xp f y", "d e hn1 z1 hn2 z2"),
            "act": ("", "h hTc rfc", "dsq gau abs exp ln", "dabs dexp dln h2 hc1 ze1 hc2 ze2"),
            "dve": ("bound bneg babs wide most isw flags flag", "bn mv aTc sq", "rel sum col msg ysb",
                    "drel dsp x2 bn2 mv2 zc1 zd1 zr1 st1 zc2 zd2 zr2 st2"),
            "pool": ("", "ve ng rs nm xb", "", "ve2 ng2 rs2 nm2 res"),
        }
        NQ = P // ROWS
        G = {k: sem("g_" + k) for k in ("pe", "act", "dve", "pool", "x", "adj", "eb", "out")}

        def after(eng, name, b=None, q=None):
            for owner, parts in ORDER.items():
                once, head, rows, tail = (p.split() for p in parts)
                graph = len(head) + NQ * len(rows) + len(tail)
                if name in once:
                    eng.wait_ge(G[owner], once.index(name) + 1)
                if name in head:
                    eng.wait_ge(G[owner], b * graph + (len(once) + head.index(name) + 1))
                if name in rows:
                    eng.wait_ge(G[owner], b * graph + q * len(rows) + (len(once) + len(head) + rows.index(name) + 1))
                if name in tail:
                    eng.wait_ge(G[owner], b * graph + (graph - len(tail) + len(once) + tail.index(name) + 1))

        flag = sb("flag", [P, 1], I32)
        bound = sb("bound", [P, 4])
        flags = sb("flags", [P, 1], BF16)
        gx, gadj, gsq = xin[0][:, 0, :], adjin[0][:, 0, :], xin[0][:, 1, :]
        geb, gdsq, ggau = eb[0][0:NG, 0:512], dsq[0:NG, 0:512], gau[0:NG, 0:512]
        gcol, gy, gmsg = cols2[:, :], yT[:, 0, :], msg[:, :, :]
        ps0, ps1, ps2, ps3 = psM[:, 0, :], psX[:, 0, :], psY[:, :, :], psX[:, 1, 0:ROWS]
        with nc.Block() as general:
            def needed(eng):
                return eng.value_load(flag[0:1, 0:1], min_val=0, max_val=2 * P)

            @general.sync
            def _(sp):
                after(sp, "flag")
                with sp.If(needed(sp) > 0):
                    with sp.Fori(0, NB) as b:
                        sp.wait_ge(G["out"], 16 * b)
                        settle(sp, S)
                        sp.dma_start(gx, x[bass.ds(b, 1)].rearrange("b n d -> (b n) d")).then_inc(G["x"], 16)
                        sp.dma_start(gadj, adj[bass.ds(b, 1)].rearrange("b n d -> (b n) d"))\
                          .then_inc(G["adj"], 16)
                        with sp.Fori(0, NQ) as q:
                            n = b * NQ + q
                            once, head, rows, tail = (len(p.split()) for p in ORDER["dve"])
                            sp.wait_ge(G["dve"], b * (head + NQ * rows + tail) + q * rows + once + head)
                            settle(sp, S)
                            src = adj[bass.ds(b, 1), bass.ds(q * ROWS, ROWS), :].rearrange("b i j -> b (i j)")
                            sp.dma_start(geb, src.to_broadcast((NG, 512))).then_inc(G["eb"], 16)
                        after(sp, "res", b)
                        settle(sp, S)
                        sp.dma_start(out[bass.ds(b, 1)].rearrange("b n d -> (b n) d"), res[0][:, 0, :])\
                          .then_inc(G["out"], 16)
                    sp.wait_ge(G["out"], 16 * NB)

            @general.tensor
            def _(pe):
                def mm(o, a, b, start=True, stop=True):
                    return nc.tensor.matmul(o, a, b, start=start, stop=stop)

                after(pe, "flags")
                mm(ps0[:, 0:1], ones[:, :], flags[:, :]).then_inc(G["pe"], 1)
                after(pe, "flag")
                with pe.If(needed(pe) > 0):
                    with pe.Fori(0, NB) as b:
                        after(pe, "h", b)
                        nc.tensor.transpose(ps0, h1[:, 0, :], ident).then_inc(G["pe"], 1)
                        after(pe, "hTc", b)
                        mm(ps0, h1T[:, 0, :], WaT).then_inc(G["pe"], 1)
                        after(pe, "rfc", b)
                        pe.wait_ge(G["adj"], 16 * b + 16)
                        nc.tensor.transpose(ps0, gadj, ident).then_inc(G["pe"], 1)
                        with pe.Fori(0, NQ) as q:
                            n = b * NQ + q
                            after(pe, "gau", b, q)
                            mm(ps1, W1T[0:NG, :], ggau).then_inc(G["pe"], 1)
                            after(pe, "sum", b, q)
                            for r in range(ROWS):
                                mm(ps2[:, r, :], hid[0][:, r * P:(r + 1) * P], W2T, True, False)
                                last = mm(ps2[:, r, :], ones[:, :], b2row[:, :], False, True)
                            last.then_inc(G["pe"], 1)
                            after(pe, "msg", b, q)
                            after(pe, "col", b, q)
                            for r in range(ROWS):
                                last = mm(ps3[:, r:r + 1], gmsg[:, r, :], gcol[:, r:r + 1])
                            last.then_inc(G["pe"], 1)
                        after(pe, "ysb", b, NQ - 1)
                        mm(ps0, Wd1T, gy).then_inc(G["pe"], 1)
                        after(pe, "dsp", b)
                        mm(ps0, dsp[:, 0, :], Wd2T).then_inc(G["pe"], 1)
                        for k in (1, 2):
                            after(pe, "h2" if k == 1 else "st1", b)
                            mm(ps0, hs[k - 1][:, 0, :], adjT[0][:, 0, :]).then_inc(G["pe"], 1)
                            after(pe, f"hc{k}", b)
                            mm(ps0, hnT[:, 0, :], lw[:, :], True, False)
                            mm(ps0, ones[:, :], lbrow[:, 0, :], False, True).then_inc(G["pe"], 1)

            @general.vector
            def _(dve):
                v = nc.vector
                v.tensor_reduce(bound[:, 0:1], wraw[:, 0, 0:NG], AX.X, ALU.add, apply_absolute_value=True)\
                 .then_inc(G["dve"], 1)
                v.tensor_scalar(bound[:, 1:2], b1c, -1.0, None, ALU.mult).then_inc(G["dve"], 1)
                after(dve, "bneg")
                v.tensor_tensor(bound[:, 1:2], bound[:, 1:2], b1c, ALU.max).then_inc(G["dve"], 1)
                after(dve, "bound")
                after(dve, "babs")
                v.tensor_tensor(bound[:, 2:3], bound[:, 0:1], bound[:, 1:2], ALU.add).then_inc(G["dve"], 1)
                v.tensor_tensor(bound[:, 3:4], most[:, 0:1], most[:, 1:2], ALU.max).then_inc(G["dve"], 1)
                after(dve, "most")
                v.tensor_scalar(bound[:, 2:3], bound[:, 2:3], SAFE, None, ALU.is_gt).then_inc(G["dve"], 1)
                after(dve, "isw")
                v.scalar_tensor_tensor(flags[:, :], bound[:, 3:4], float(LIMIT), bound[:, 2:3],
                                       ALU.is_gt, ALU.add).then_inc(G["dve"], 1)
                after(dve, "count")
                v.tensor_copy(flag[:, :], ps0[:, 0:1]).then_inc(G["dve"], 1)
                after(dve, "flag")
                with dve.If(needed(dve) > 0):
                    with dve.Fori(0, NB) as b:
                        dve.wait_ge(G["x"], 16 * b + 16)
                        v.bn_stats(bn1[:, 0, :], gx).then_inc(G["dve"], 1)
                        after(dve, "bn", b)
                        settle(dve, S)
                        v.bn_aggr(mv1[:, 0, :], bn1[:, 0, :]).then_inc(G["dve"], 1)
                        after(dve, "aT", b)
                        v.tensor_copy(adjT[0][:, 0, :], ps0).then_inc(G["dve"], 1)
                        after(dve, "aTc", b)
                        v.tensor_tensor(gsq, adjT[0][:, 0, :], adjT[0][:, 0, :], ALU.mult).then_inc(G["dve"], 1)
                        after(dve, "sq", b)
                        settle(dve, S)
                        with dve.Fori(0, NQ) as q:
                            n = b * NQ + q
                            after(dve, "ln", b, q)
                            v.tensor_scalar(ex[:, 512:1024], ps1, b1c, 0.0, ALU.add, ALU.max)\
                             .then_inc(G["dve"], 1)
                            after(dve, "rel", b, q)
                            v.tensor_tensor(hid[0][:, 0:512], ex[:, 0:512], ex[:, 512:1024], ALU.add)\
                             .then_inc(G["dve"], 1)
                            v.tensor_copy(gcol, xin[0][:, 1, bass.ds(q * ROWS, ROWS)]).then_inc(G["dve"], 1)
                            after(dve, "f", b, q)
                            for r in range(ROWS):
                                last = v.tensor_tensor(gmsg[:, r, :], ps2[:, r, :], rf[0][:, 0, :], ALU.mult)
                            last.then_inc(G["dve"], 1)
                            after(dve, "y", b, q)
                            v.tensor_copy(yT[:, 0, bass.ds(q * ROWS, ROWS)], ps3).then_inc(G["dve"], 1)
                        after(dve, "dln", b)
                        v.tensor_scalar(drel[:, 0, :], ps0, bd1c, 0.0, ALU.add, ALU.max).then_inc(G["dve"], 1)
                        after(dve, "drel", b)
                        v.tensor_tensor(dsp[:, 0, :], drel[:, 0, :], dln[:, 0, :], ALU.add)\
                         .then_inc(G["dve"], 1)
                        after(dve, "xb", b)
                        after(dve, "e", b)
                        v.tensor_tensor(x2[0][:, 0, :], ps0, xb[:, 0, :], ALU.add).then_inc(G["dve"], 1)
                        after(dve, "x2", b)
                        v.bn_stats(bn2[:, 0, :], x2[0][:, 0, :]).then_inc(G["dve"], 1)
                        after(dve, "bn2", b)
                        settle(dve, S)
                        v.bn_aggr(mv2[:, 0, :], bn2[:, 0, :]).then_inc(G["dve"], 1)
                        for k in (1, 2):
                            after(dve, f"z{k}", b)
                            v.tensor_scalar(zcl[:, 0, :], ps0, -88.0, None, ALU.max).then_inc(G["dve"], 1)
                            after(dve, f"ze{k}", b)
                            v.tensor_scalar(zden[:, 0, :], zex[:, 0, :], 1.0, None, ALU.add)\
                             .then_inc(G["dve"], 1)
                            after(dve, f"zd{k}", b)
                            v.reciprocal(zrec[:, 0, :], zden[:, 0, :]).then_inc(G["dve"], 1)
                            after(dve, f"zr{k}", b)
                            v.tensor_tensor(hs[k][:, 0, :], ps0, zrec[:, 0, :], ALU.mult)\
                             .then_inc(G["dve"], 1)

            @general.scalar
            def _(act):
                a = nc.scalar.activation
                after(act, "flag")
                with act.If(needed(act) > 0):
                    nc.scalar.preload_act_table_set("natural_log_exp_and_others")
                    with act.Fori(0, NB) as b:
                        after(act, "nm", b)
                        a(h1[:, 0, :], gx, ACT.Relu, bias=nm1[:, 0:1], scale=rs1[:, 0:1]).then_inc(G["act"], 1)
                        after(act, "hT", b)
                        a(h1T[:, 0, :], ps0, ACT.Copy).then_inc(G["act"], 1)
                        after(act, "rf", b)
                        a(rf[0][:, 0, :], ps0, ACT.Copy).then_inc(G["act"], 1)
                        after(act, "sq", b)
                        with act.Fori(0, NQ) as q:
                            n = b * NQ + q
                            act.wait_ge(G["eb"], 16 * n + 16)
                            a(gdsq, geb, ACT.Square, bias=cst[0:NG, C_NO:C_NO + 1]).then_inc(G["act"], 1)
                            after(act, "dsq", b, q)
                            a(ggau, gdsq, ACT.Exp, scale=COEFF).then_inc(G["act"], 1)
                            after(act, "xp", b, q)
                            a(ex[:, 0:512], ps1, ACT.Abs, bias=b1c).then_inc(G["act"], 1)
                            after(act, "abs", b, q)
                            a(ex[:, 512:1024], ex[:, 0:512], ACT.Exp, scale=-1.0).then_inc(G["act"], 1)
                            after(act, "exp", b, q)
                            a(ex[:, 0:512], ex[:, 512:1024], ACT.Ln, bias=half_c[:, :], scale=0.5)\
                                .then_inc(G["act"], 1)
                        after(act, "d", b)
                        a(dabs[:, 0, :], ps0, ACT.Abs, bias=bd1c).then_inc(G["act"], 1)
                        after(act, "dabs", b)
                        a(dexp[:, 0, :], dabs[:, 0, :], ACT.Exp, scale=-1.0).then_inc(G["act"], 1)
                        after(act, "dexp", b)
                        a(dln[:, 0, :], dexp[:, 0, :], ACT.Ln, bias=half_c[:, :], scale=0.5)\
                            .then_inc(G["act"], 1)
                        after(act, "nm2", b)
                        a(hs[0][:, 0, :], x2[0][:, 0, :], ACT.Relu, bias=nm2[:, 0:1], scale=rs2[:, 0:1])\
                            .then_inc(G["act"], 1)
                        for k in (1, 2):
                            after(act, f"hn{k}", b)
                            a(hnT[:, 0, :], ps0, ACT.Copy).then_inc(G["act"], 1)
                            after(act, f"zc{k}", b)
                            a(zex[:, 0, :], zcl[:, 0, :], ACT.Exp, scale=-1.0).then_inc(G["act"], 1)

            @general.gpsimd
            def _(pool):
                g = nc.gpsimd

                def deviation(b, mv, tt, rs, nm, names):
                    s_mv, s_ve, s_ng, s_rs = names
                    after(pool, s_mv, b)
                    settle(pool, S)
                    g.tensor_scalar(tt[:, 0, 0:1], mv[:, 0, 1:2], EPS, None, ALU.add).then_inc(G["pool"], 1)
                    g.tensor_scalar(tt[:, 1, 0:1], mv[:, 0, 0:1], -1.0, None, ALU.mult).then_inc(G["pool"], 1)
                    after(pool, s_ve, b)
                    g.tensor_tensor(rs[:, 0:1], tt[:, 0, 0:1], mhalf[:, 0:1], ALU.pow).then_inc(G["pool"], 1)
                    after(pool, s_ng, b)
                    after(pool, s_rs, b)
                    g.tensor_tensor(nm[:, 0:1], tt[:, 1, 0:1], rs[:, 0:1], ALU.mult).then_inc(G["pool"], 1)

                after(pool, "flag")
                with pool.If(needed(pool) > 0):
                    with pool.Fori(0, NB) as b:
                        deviation(b, mv1, tt1, rs1, nm1, ("mv", "ve", "ng", "rs"))
                        pool.wait_ge(G["x"], 16 * b + 16)
                        g.tensor_tensor(xb[:, 0, :], gx, bd2_bc[:, :], ALU.add).then_inc(G["pool"], 1)
                        deviation(b, mv2, tt2, rs2, nm2, ("mv2", "ve2", "ng2", "rs2"))
                        after(pool, "st2", b)
                        g.tensor_tensor(res[0][:, 0, :], x2[0][:, 0, :], hs[2][:, 0, :], ALU.add)\
                         .then_inc(G["pool"], 1)


def edge_constants():
    import numpy as np
    c = np.zeros((P, C_ALL), np.float32)
    k, m = np.arange(P)[:, None], np.arange(P)[None, :]
    c[:, C_ID:C_ID + P] = k == m
    c[:, C_U:C_U + P] = k <= m
    c[:, C_US:C_US + P] = k < m
    c[:, C_TC:C_TC + TILES] = k + P * np.arange(TILES)[None, :] + 1
    c[:, C_NO] = -np.tile(np.linspace(0.0, CUTOFF, NG, dtype=np.float32), P // NG)
    c[:, C_IO:] = np.arange(1, T + 1)
    return c


_INS = ["x", "adj", "L0_gnn_W1", "L0_gnn_b1", "L0_gnn_W2", "L0_gnn_b2", "L0_gnn_Wa", "L0_gnn_Wd1",
        "L0_gnn_bd1", "L0_gnn_Wd2", "L0_gnn_bd2", "L1_gnn_W", "L1_gnn_b"]


def kernel(**inputs):
    import numpy as np
    import concourse.bacc as bacc
    from concourse.bass_utils import run_bass_kernel_spmd

    nc = bacc.Bacc("TRN2", target_bir_lowering=False, num_devices=1)
    given = {name: np.ascontiguousarray(inputs[name]) for name in _INS}
    given["consts"] = edge_constants()
    arrays = {f"in_{name}": a for name, a in given.items()}
    args = [nc.dram_tensor(f"in_{name}", a.shape, mybir.dt.from_np(a.dtype), kind="ExternalInput").ap()
            for name, a in given.items()]
    out = nc.dram_tensor("out", given["x"].shape, F32, kind="ExternalOutput").ap()
    build(nc, *args, out)
    r = run_bass_kernel_spmd(nc, [arrays], core_ids=[0])
    return r.results[0]["out"]
```

```python
from contextlib import ExitStack

import concourse.bass as bass
from concourse import mybir

ALU = mybir.AluOpType
ACT = mybir.ActivationFunctionType
F32 = mybir.dt.float32
BF16 = mybir.dt.bfloat16
F16 = mybir.dt.float16
I32 = mybir.dt.int32
AX = mybir.AxisListType

P = 128
NG = 64
TILES = 10
T = TILES * P
HALF = T // 2
CUTOFF = 5.0
WIDTH = CUTOFF / (NG - 1)
COEFF = -0.5 / (WIDTH * WIDTH)
EPS = 1e-5
SAFE = 40.0
ROWS = 4
LIMIT = T

C_ID, C_U, C_US, C_TC, C_NO, C_IO = 0, P, 2 * P, 3 * P, 3 * P + TILES, 3 * P + TILES + 1
C_ALL = C_IO + T


class Batch:

    def __init__(self, k, c):
        self.k, self.c = (0, 4 * k + c) if isinstance(k, int) else (k, c)
        self.static = isinstance(k, int)

    def __add__(self, d):
        return Batch(self.k, self.c + d)

    @property
    def n(self):
        return self.c if self.static else 4 * self.k + self.c

    @property
    def pair(self):
        return self.c // 2 if self.static else 2 * self.k + self.c // 2

    @property
    def half(self):
        return self.c // 4 if self.static else self.k + self.c // 4

    @property
    def p4(self):
        return self.c % 4

    @property
    def p2(self):
        return self.c % 2

    @property
    def pp(self):
        return (self.c // 2) % 2

    def within(self, nb):
        return not self.static or 0 <= self.c < nb


def wait(eng, sem, count):
    if not (isinstance(count, int) and count <= 0):
        eng.wait_ge(sem, count)


def settle(eng, S):
    eng.sem_inc(S["settled"], 1)


def build(nc, x, adj, W1, b1, W2, b2, Wa, Wd1, bd1, Wd2, bd2, LW, Lb, consts, out):
    NB = x.shape[0]
    assert NB % 4 == 0 and NB >= 16

    ctx = ExitStack()
    with ctx:
        def sb(name, shape, dt=F32):
            return ctx.enter_context(nc.sbuf_tensor(name, shape, dt))

        def ps(name, shape):
            return ctx.enter_context(nc.psum_tensor(name, shape, F32))

        def sem(name):
            return ctx.enter_context(nc.semaphore(name))

        e_dram = nc.dram_tensor("edge_values", (NB, TILES, P), F32).ap()

        cst = sb("cst", [P, C_ALL])
        ident = cst[:, C_ID:C_ID + P]
        tcol = cst[:, C_TC:C_TC + TILES]
        neg_off = cst[:, C_NO:C_NO + 1]
        upper = sb("upper", [P, P], BF16)
        upper_s = sb("upper_s", [P, P], BF16)
        iota = sb("iota", [P, T], F16)
        wraw = sb("wraw", [P, 5, P])
        wT = sb("wT", [P, 5, P])
        lw = sb("lw", [P, P])
        cols = sb("cols", [P, 2])
        bd2_bc = sb("bd2_bc", [P, P])
        W1T, W2T, WaT, Wd1T, Wd2T = (wT[:, k, :] for k in range(5))
        b1c, bd1c = (cols[:, k:k + 1] for k in range(2))
        half_c = sb("half_c", [P, 1])
        mhalf = sb("mhalf", [P, 2])
        ones = sb("ones", [P, P], BF16)
        b2row = sb("b2row", [P, P], BF16)
        b2_bc = sb("b2_bc", [P, P])
        lb_bc = sb("lb_bc", [P, 2, P])
        b2_left = sb("b2_left", [P, P])
        b2_part = sb("b2_part", [P, 3, P], BF16)
        b2_acc = sb("b2_acc", [P, 2, P])
        one_c = sb("one_c", [P, 1])

        xin = [sb(f"xin{k}", [P, 2, P]) for k in range(2)]
        adjin = [sb(f"adjin{k}", [P, 2, P]) for k in range(2)]
        bn1 = sb("bn1", [P, 2, 6])
        mv1 = sb("mv1", [P, 2, 2])
        rs1 = sb("rs1", [P, 2])
        tt1 = sb("tt1", [P, 2, 2])
        nm1 = sb("nm1", [P, 2])
        h1 = sb("h1", [P, 2, P])
        h1T = sb("h1T", [P, 2, P])
        rf = [sb(f"rf{k}", [P, 2, P]) for k in range(2)]
        rfr = sb("rfr", [P, 2, P])
        rfS = [sb(f"rfS{k}", [P, 3, 2, P], BF16) for k in range(2)]
        adjT = [sb(f"adjT{k}", [P, 2, P]) for k in range(2)]
        adjr = sb("adjr", [P, 2, P])
        adjS = [sb(f"adjS{k}", [P, 3, 2, P], BF16) for k in range(2)]
        rank = sb("rank", [P, 2, P], F16)
        maskN = sb("maskN", [P, 2, P], BF16)
        maskT = sb("maskT", [P, 2, P], BF16)
        deg = sb("deg", [P, 2], BF16)
        oo = [sb(f"oo{k}", [P, 2, 2]) for k in range(2)]
        key = [sb(f"key{k}", [P, 2, P], F16) for k in range(2)]
        most = sb("most", [P, 2])

        Qend = sb("Qend", [P, T], F16)
        Qbeg = sb("Qbeg", [P, T], F16)
        Q = [sb(f"Q{k}", [P, T], F16) for k in range(4)]
        Ksb = sb("Ksb", [P, 2, 2, P])
        Gsb = sb("Gsb", [P, 2, 2, P])
        Wsc = [sb(f"Wsc{k}", [P, T]) for k in range(4)]
        eT = [sb(f"eT{k}", [P, TILES]) for k in range(4)]
        erow = [sb(f"erow{k}", [TILES, P]) for k in range(2)]
        eb = [sb(f"eb{k}", [P, HALF]) for k in range(2)]
        dsq = sb("dsq", [P, HALF])
        gau = sb("gau", [P, HALF])
        ex = sb("ex", [P, T])
        hid = [sb(f"hid{k}", [P, T]) for k in range(2)]
        msg = sb("msg", [P, 5, P])

        xpost = [sb(f"xpost{k}", [P, 2, P]) for k in range(2)]
        xb = sb("xb", [P, 2, P])
        adjL = [sb(f"adjL{k}", [P, 2, P]) for k in range(2)]
        adjM = [sb(f"adjM{k}", [P, 2, P]) for k in range(2)]
        yT = sb("yT", [P, 2, P])
        ds = sb("ds", [P, 2, P])
        dabs = sb("dabs", [P, 2, P])
        dexp = sb("dexp", [P, 2, P])
        dln = sb("dln", [P, 2, P])
        dsp = sb("dsp", [P, 2, P])
        cols2 = sb("cols2", [P, ROWS])
        x2 = [sb(f"x2_{k}", [P, 2, P]) for k in range(2)]
        bn2 = sb("bn2", [P, 2, 6])
        mv2 = sb("mv2", [P, 2, 2])
        rs2 = sb("rs2", [P, 2])
        tt2 = sb("tt2", [P, 2, 2])
        nm2 = sb("nm2", [P, 2])
        hs = [sb(f"hs{k}", [P, 2, P]) for k in range(3)]
        hnT = sb("hnT", [P, 2, P])
        zs = sb("zs", [P, 2, P])
        zabs = sb("zabs", [P, 2, P])
        zexp = sb("zexp", [P, 2, P])
        zln = sb("zln", [P, 2, P])
        zsig = sb("zsig", [P, 2, P])
        zgate = sb("zgate", [P, 2, P])
        res = [sb(f"res{k}", [P, 2, P]) for k in range(2)]

        psKV = ps("psKV", [P, 2, 2, 2, P])
        psGF = ps("psGF", [P, 2, 2, 2, P])
        psY = ps("psY", [P, 4, P])
        psX = ps("psX", [P, 2, 512])
        psM = ps("psM", [P, 4, P])
        psA = psM[:, 0:2, :]
        psW = psGF[:, 0, :, :, :].rearrange("p a b c -> p (a b) c")
        psE = psX[0:TILES, 1, 0:P]
        psO = psX[:, 1, P:P + 4]

        names = """w_in w_tr w_tr2 w_cast w_done c_in split_b rows_b
            x_in0 x_in1 a_in0 a_in1 xp_in0 xp_in1 e_out eb_in0 eb_in1 o_out0 o_out1
            bn1_d mv1_d rs1_d nm1_d h1_d h1Tp h1T_d rfp rf_d rfhi rfr_d rfmid rfS_d
            adjTp adjT_d ahi adjr_d amid adjS_d maskN_d maskT_d rank_d rank_c deg_d offs_d oo_d key_d most_d
            Qe_d Qb_d Q_d kx_d kc_d w_d et_d erow_d dsq_d gau_d x_d ex_d hid_d gw_d gc_d msg_d y_mm
            yT_d dp ds_d abs_d dexp_d dln_d dsp_d ep xb_d adjL_d adjM_d x2_d bn2_d mv2_d rs2_d nm2_d h2_d
            ve1_d ng1_d ve2_d ng2_d settled hn_p1 hn_c1 hn_p2 hn_c2 z_p zs_d zabs_d zexp_d zln_d zsig_d zgate_d
            st_d res_d""".split()
        S = {k: sem(k) for k in names}
        W_LOADS = 16 * 13

        block = nc.Block()
        block.__enter__()

        def filter_tile(b, t):
            return (b + -2, t - 8) if t >= 8 else (b + -3, t + TILES - 8)

        def scatter_tile(b, t):
            return (b + -3, t - 2) if t >= 2 else (b + -4, t + TILES - 2)

        def prep_pair(b):
            return b + 2 if b.p2 == 0 else b + 1

        D_STEP, E_STEP, Z1_STEP, Z2_STEP = 5, 6, 7, 8

        def steps(eng, step):
            for n in range(-3, 12):
                step(Batch(0, n))
            with eng.Fori(3, NB // 4 - 1) as k:
                for c in range(4):
                    step(Batch(k, c))
            for n in range(NB - 4, NB + 8):
                step(Batch(0, n))

        BANK_USES = [[("e", lambda b: b + -E_STEP, "x2_d", 1, 1), ("z2", lambda b: b + -Z2_STEP, "zs_d", 2, 2),
                      ("adjT", prep_pair, "adjT_d", 1, 1), ("rank", prep_pair, "rank_c", 1, 1),
                      ("hn1", lambda b: b + -E_STEP, "hn_c1", 1, 1)],
                     [("z1", lambda b: b + -Z1_STEP, "zs_d", 2, 1), ("h1T", prep_pair, "h1T_d", 1, 1),
                      ("d", lambda b: b + -D_STEP, "ds_d", 1, 1), ("rf", prep_pair, "rf_d", 1, 1),
                      ("hn2", lambda b: b + -Z1_STEP, "hn_c2", 1, 1)]]

        def bank_free(pe, b, use):
            at = [u[0] for u in BANK_USES[b.p2]].index(use) - 1
            for _ in range(20):
                if at < 0:
                    b = b + -1
                    at = len(BANK_USES[b.p2]) - 1
                _, pair_of, read, per, add = BANK_USES[b.p2][at]
                if pair_of(b).within(NB):
                    pe.wait_ge(S[read], per * pair_of(b).pair + add)
                    return
                at -= 1

        ROUNDS = [slice(0, 3 * P), slice(3 * P, HALF)]
        ROUND_SLOT = [4, 6]

        @block.sync
        def _(sp):
            for k, w in enumerate((W1, W2, Wa, Wd1, Wd2)):
                sp.dma_start(wraw[:, k, 0:w.shape[1]], w).then_inc(S["w_in"], 16)
            sp.dma_start(wraw[:, 0, NG:2 * NG], W1).then_inc(S["w_in"], 16)
            sp.dma_start(cst[:, 0:C_IO], consts[:, 0:C_IO]).then_inc(S["c_in"], 16)
            sp.dma_start(cst[:, C_IO:], consts[0:1, C_IO:].to_broadcast((P, T))).then_inc(S["c_in"], 16)
            sp.dma_start(lw[:, :], LW).then_inc(S["w_in"], 16)
            for k, v in enumerate((b1, bd1)):
                sp.dma_start(cols[:, k:k + 1], v.rearrange("(p a) -> p a", a=1)).then_inc(S["w_in"], 16)
            for dst, v in ((bd2_bc[:, :], bd2), (b2_bc[:, :], b2), (lb_bc[:, 0, :], Lb), (lb_bc[:, 1, :], Lb)):
                sp.dma_start(dst, v.rearrange("(a p) -> a p", a=1).to_broadcast((P, P))).then_inc(S["w_in"], 16)

            def load(q):
                wait(sp, S["h1_d"], 2 * q.pair - 2)
                settle(sp, S)
                sp.dma_start(xin[q.pp][:, :, :], x[bass.ds(q.n, 2)].rearrange("b n d -> n b d"))\
                  .then_inc(S[f"x_in{q.pp}"], 16)
                wait(sp, S["adjTp"], q.pair - 1)
                wait(sp, S["maskN_d"], q.pair - 1)
                settle(sp, S)
                sp.dma_start(adjin[q.pp][:, :, :], adj[bass.ds(q.n, 2)].rearrange("b n d -> n b d"))\
                  .then_inc(S[f"a_in{q.pp}"], 16)

            def step(b):
                if b.static and b.c == -3:
                    load(Batch(0, 0))
                    return
                if b.p2 == 0 and (b + 4).within(NB):
                    load(b + 4)
                if b.p2 == 1 and (b + -3).within(NB):
                    q = b + -3
                    wait(sp, S["xb_d"], q.pair - 1)
                    settle(sp, S)
                    sp.dma_start(xpost[q.pp][:, :, :], x[bass.ds(q.n, 2)].rearrange("b n d -> n b d"))\
                      .then_inc(S[f"xp_in{q.pp}"], 16)
                m = b + -1
                if m.within(NB):
                    sp.wait_ge(S["erow_d"], m.n + 1)
                    settle(sp, S)
                    sp.dma_start(e_dram[bass.ds(m.n, 1)].rearrange("b t p -> (b t) p"), erow[m.p2][:, :])\
                      .then_inc(S["e_out"], 16)
                    sp.wait_ge(S["e_out"], 16 * m.n + 16)
                    settle(sp, S)
                    wait(sp, S["dsq_d"], m.n - 1)
                    settle(sp, S)
                    for s in range(2):
                        src = e_dram[bass.ds(m.n, 1), s * TILES // 2:(s + 1) * TILES // 2]
                        sp.dma_start(eb[m.p2][s * NG:(s + 1) * NG, :],
                                     src.rearrange("b t p -> b (t p)").to_broadcast((NG, HALF)))\
                          .then_inc(S[f"eb_in{m.p2}"], 16)
                o = b + -(Z2_STEP + 1)
                if b.p2 == 1 and o.within(NB):
                    sp.wait_ge(S["res_d"], o.pair + 1)
                    settle(sp, S)
                    sp.dma_start(out[bass.ds(o.n, 2)].rearrange("b n d -> n b d"), res[o.pp][:, :, :])\
                      .then_inc(S[f"o_out{o.pp}"], 16)

            steps(sp, step)
            for k in range(2):
                sp.wait_ge(S[f"o_out{k}"], 16 * NB // 4)

        @block.tensor
        def _(pe):
            def mm(o, a, b, start=True, stop=True):
                return nc.tensor.matmul(o, a, b, start=start, stop=stop)

            pe.wait_ge(S["c_in"], 32)
            pe.wait_ge(S["w_in"], W_LOADS)
            for k in range(4):
                nc.tensor.transpose(psW[:, k, :], wraw[:, k, :], ident).then_inc(S["w_tr"], 1)
            nc.tensor.transpose(psA[:, 0, :], wraw[:, 4, :], ident).then_inc(S["w_tr2"], 1)
            pe.wait_ge(S["w_done"], 2)
            pe.wait_ge(S["w_cast"], 8)
            pe.wait_ge(S["rows_b"], 4)

            def first_product(e, c):
                if c == 0:
                    pe.wait_ge(S["gau_d"], e.n + 1)
                    rows, pairs = e.n + 2, e.pair + 2 + e.p2
                    pe.wait_ge(S["erow_d"], min(rows, NB) if e.static else rows)
                    pe.wait_ge(S["oo_d"], min(pairs, NB // 2) if e.static else pairs)
                wait(pe, S["ex_d"], 2 * e.n + c)
                for s in range(2):
                    part = ROUNDS[c]
                    last = mm(psX[:, s, 0:part.stop - part.start], W1T[s * NG:(s + 1) * NG, :],
                              gau[s * NG:(s + 1) * NG, part])
                    last.then_inc(S["x_d"], 1)

            def expand(b, t):
                if t == 0:
                    pe.wait_ge(S["Q_d"], b.n + 1)
                    pe.wait_ge(S["key_d"], 2 * b.pair + 2)
                    pe.wait_ge(S["adjS_d"], b.pair + 1)
                c, k2 = t // 2, (b.p2 + t // 2) % 2
                if t % 2 == 0:
                    wait(pe, S["kc_d"], TILES // 2 * b.n + c - 1)
                    wait(pe, S["w_d"], TILES * b.n + 2 * (c - 1))
                q = Q[b.p4][:, t * P:(t + 1) * P]
                mm(psKV[:, k2, 0, t % 2, :], q, key[b.pp][:, b.p2, :])
                for k in range(3):
                    last = mm(psKV[:, k2, 1, t % 2, :], q, adjS[b.pp][:, k, b.p2, :], k == 0, k == 2)
                last.then_inc(S["kx_d"], 1)

            def filters(e, t):
                if t == 0:
                    pe.wait_ge(S["rfS_d"], e.pair + 1)
                if t in (0, 3):
                    pe.wait_ge(S["hid_d"], 2 * e.n + (2 if t else 1))
                c, k2 = t // 2, (e.p2 + t // 2) % 2
                if t % 2 == 0:
                    wait(pe, S["gc_d"], TILES // 2 * e.n + c - 1)
                    wait(pe, S["msg_d"], TILES * e.n + 2 * (c - 1))
                for k in range(3):
                    mm(psGF[:, k2, 0, t % 2, :], Q[e.p4][:, t * P:(t + 1) * P], rfS[e.pp][:, k, e.p2, :],
                       k == 0, k == 2)
                mm(psGF[:, k2, 1, t % 2, :], hid[e.p2][:, t * P:(t + 1) * P], W2T, True, False)
                mm(psGF[:, k2, 1, t % 2, :], ones[:, :], b2row[:, :], False, True).then_inc(S["gw_d"], 1)

            def scatter(e, t):
                if t == 0:
                    wait(pe, S["yT_d"], e.n)
                pe.wait_ge(S["msg_d"], TILES * e.n + t + 1)
                mm(psY[:, 0, :], msg[:, t % 5, :], Wsc[e.p4][:, t * P:(t + 1) * P],
                   t == 0, t == TILES - 1).then_inc(S["y_mm"], 1)

            def both(f):
                for k in range(2):
                    last = f(k)
                return last

            def rows_and_offsets(b):
                m, q = b + -1, prep_pair(b)
                wait(pe, S["oo_d"], min(q.pair, NB // 2) if b.static else q.pair)
                if m.within(NB):
                    pe.wait_ge(S["w_d"], TILES * m.n + TILES)
                    wait(pe, S["erow_d"], m.n)
                    wait(pe, S["ex_d"], 2 * m.n - 2)
                    nc.tensor.transpose(psE, eT[m.p4][:, :], ident).then_inc(S["et_d"], 1)
                if q.within(NB) and b.p2 == 1:
                    pe.wait_ge(S["deg_d"], q.pair + 1)
                    wait(pe, S["ex_d"], 2 * (b.n - 2))
                    mm(psO[:, 0:2], upper_s[:, :], deg[:, :])
                    mm(psO[:, 2:4], upper[:, :], deg[:, :]).then_inc(S["offs_d"], 1)

            def prep_products(b, t):
                q = prep_pair(b)
                c = q.pair
                if not q.within(NB):
                    return
                if b.p2 == 0 and t == 4:
                    pe.wait_ge(S[f"a_in{q.pp}"], 16 * q.half + 16)
                    bank_free(pe, b, "adjT")
                    both(lambda k: nc.tensor.transpose(psA[:, k, :], adjin[q.pp][:, k, :], ident))\
                        .then_inc(S["adjTp"], 1)
                if b.p2 == 0 and t == 6:
                    pe.wait_ge(S["maskN_d"], c + 1)
                    bank_free(pe, b, "rank")
                    both(lambda k: mm(psA[:, k, :], maskN[:, k, :], upper[:, :])).then_inc(S["rank_d"], 1)
                if b.p2 == 1 and t == 2:
                    pe.wait_ge(S["h1_d"], 2 * c + 2)
                    bank_free(pe, b, "h1T")
                    both(lambda k: nc.tensor.transpose(psA[:, k, :], h1[:, k, :], ident))\
                        .then_inc(S["h1Tp"], 1)
                if b.p2 == 1 and t == 6:
                    pe.wait_ge(S["h1T_d"], c + 1)
                    bank_free(pe, b, "rf")
                    both(lambda k: mm(psA[:, k, :], h1T[:, k, :], WaT)).then_inc(S["rfp"], 1)

            def rest_products(b, t):
                s, d = b + -E_STEP, (b + -E_STEP).pair
                if b.p2 == 0 and s.within(NB) and t == 0:
                    pe.wait_ge(S["dsp_d"], d + 1)
                    bank_free(pe, b, "e")
                    both(lambda k: mm(psA[:, k, :], dsp[:, k, :], Wd2T)).then_inc(S["ep"], 1)
                if b.p2 == 0 and s.within(NB) and t == 8:
                    pe.wait_ge(S["h2_d"], 2 * d + 2)
                    pe.wait_ge(S["adjM_d"], d + 1)
                    bank_free(pe, b, "hn1")
                    both(lambda k: mm(psA[:, k, :], hs[0][:, k, :], adjM[s.pp][:, k, :])).then_inc(S["hn_p1"], 1)
                s, d = b + -Z1_STEP, (b + -Z1_STEP).pair
                if b.p2 == 1 and s.within(NB) and t == 0:
                    pe.wait_ge(S["hn_c1"], d + 1)
                    bank_free(pe, b, "z1")
                    both(lambda k: mm(psA[:, k, :], hnT[:, k, :], lw[:, :])).then_inc(S["z_p"], 1)
                if b.p2 == 1 and s.within(NB) and t == 8:
                    pe.wait_ge(S["st_d"], 2 * d + 1)
                    bank_free(pe, b, "hn2")
                    both(lambda k: mm(psA[:, k, :], hs[1][:, k, :], adjM[s.pp][:, k, :])).then_inc(S["hn_p2"], 1)
                s, d = b + -Z2_STEP, (b + -Z2_STEP).pair
                if b.p2 == 0 and s.within(NB) and t == 2:
                    pe.wait_ge(S["hn_c2"], d + 1)
                    bank_free(pe, b, "z2")
                    both(lambda k: mm(psA[:, k, :], hnT[:, k, :], lw[:, :])).then_inc(S["z_p"], 1)
                s, d = b + -D_STEP, (b + -D_STEP).pair
                if b.p2 == 1 and s.within(NB) and t == 4:
                    pe.wait_ge(S["yT_d"], 2 * d + 2)
                    bank_free(pe, b, "d")
                    mm(psA, Wd1T, yT[:, :, :]).then_inc(S["dp"], 1)

            def step(b):
                for t in range(TILES):
                    if t in ROUND_SLOT and (b + -2).within(NB):
                        first_product(b + -2, ROUND_SLOT.index(t))
                    if b.within(NB):
                        expand(b, t)
                    e, u = filter_tile(b, t)
                    if e.within(NB):
                        filters(e, u)
                    if t == 2:
                        rows_and_offsets(b)
                    prep_products(b, t)
                    rest_products(b, t)
                    e, u = scatter_tile(b, t)
                    if e.within(NB):
                        scatter(e, u)

            steps(pe, step)

        @block.vector
        def _(dve):
            v = nc.vector
            dve.wait_ge(S["c_in"], 32)
            v.tensor_copy(upper[:, :], cst[:, C_U:C_U + P]).then_inc(S["w_cast"], 1)
            v.tensor_copy(upper_s[:, :], cst[:, C_US:C_US + P]).then_inc(S["w_cast"], 1)
            v.tensor_copy(iota[:, :], cst[:, C_IO:C_IO + T]).then_inc(S["w_cast"], 1)
            v.memset(most[:, :], 0.0).then_inc(S["w_cast"], 1)
            v.memset(half_c[:, :], 0.5).then_inc(S["w_cast"], 1)
            v.memset(mhalf[:, :], -0.5).then_inc(S["w_cast"], 1)
            v.memset(ones[:, :], 1.0).then_inc(S["w_cast"], 1)
            v.memset(one_c[:, :], 1.0).then_inc(S["w_cast"], 1)
            dve.wait_ge(S["w_in"], W_LOADS)
            v.tensor_copy(b2_part[:, 0], b2_bc[:, :]).then_inc(S["split_b"], 1)
            dve.wait_ge(S["split_b"], 1)
            v.tensor_tensor(b2_left[:, :], b2_bc[:, :], b2_part[:, 0], ALU.subtract).then_inc(S["split_b"], 1)
            dve.wait_ge(S["split_b"], 2)
            v.tensor_copy(b2_part[:, 1], b2_left[:, :]).then_inc(S["split_b"], 1)
            dve.wait_ge(S["split_b"], 3)
            v.tensor_tensor(b2_part[:, 2], b2_left[:, :], b2_part[:, 1], ALU.subtract).then_inc(S["split_b"], 1)
            dve.wait_ge(S["split_b"], 4)
            v.tensor_scalar(b2_acc[:, 0], b2_part[:, 0], ident[:, 0:1], None, ALU.mult).then_inc(S["rows_b"], 1)
            dve.wait_ge(S["rows_b"], 1)
            v.scalar_tensor_tensor(b2_acc[:, 1], b2_part[:, 1], ident[:, 1:2], b2_acc[:, 0], ALU.mult, ALU.add)\
             .then_inc(S["rows_b"], 1)
            dve.wait_ge(S["rows_b"], 2)
            v.scalar_tensor_tensor(b2_acc[:, 0], b2_part[:, 2], ident[:, 2:3], b2_acc[:, 1], ALU.mult, ALU.add)\
             .then_inc(S["rows_b"], 1)
            dve.wait_ge(S["rows_b"], 3)
            v.tensor_copy(b2row[:, :], b2_acc[:, 0]).then_inc(S["rows_b"], 1)
            dve.wait_ge(S["w_tr"], 4)
            v.tensor_copy(wT[:, 0:4, :], psW).then_inc(S["w_done"], 1)
            dve.wait_ge(S["w_tr2"], 1)
            v.tensor_copy(wT[:, 4, :], psA[:, 0, :]).then_inc(S["w_done"], 1)
            dve.wait_ge(S["w_cast"], 8)

            def moments(c, xt, bn, mv, s_bn, s_mv, stage):
                if stage == 0:
                    for k in range(2):
                        v.bn_stats(bn[:, k, :], xt[:, k, :]).then_inc(s_bn, 1)
                if stage == 1:
                    dve.wait_ge(s_bn, 2 * c + 2)
                    settle(dve, S)
                    for k in range(2):
                        v.bn_aggr(mv[:, k, :], bn[:, k, :]).then_inc(s_mv, 1)

            def list_edges(b, t):
                c, k2 = t // 2, (b.p2 + t // 2) % 2
                dve.wait_ge(S["kc_d"], TILES // 2 * b.n + c + 1)
                if t == 0:
                    wait(dve, S["y_mm"], TILES * b.n - 3 * TILES)
                    wait(dve, S["et_d"], b.n - 3)
                v.scalar_tensor_tensor(Wsc[b.p4][:, t * P:(t + 1) * P], Ksb[:, k2, t % 2, :],
                                       tcol[:, t:t + 1], psKV[:, k2, 1, t % 2, :], ALU.is_equal, ALU.mult,
                                       accum_out=eT[b.p4][:, t:t + 1]).then_inc(S["w_d"], 1)

            def message(e, t):
                c, k2 = t // 2, (e.p2 + t // 2) % 2
                dve.wait_ge(S["gc_d"], TILES // 2 * e.n + c + 1)
                wait(dve, S["y_mm"], TILES * e.n + t - 4)
                v.scalar_tensor_tensor(msg[:, t % 5, :], psGF[:, k2, 1, t % 2, :], eT[e.p4][:, t:t + 1],
                                       Gsb[:, k2, t % 2, :], ALU.mult, ALU.mult).then_inc(S["msg_d"], 1)

            def owners(m, t):
                if t == 5:
                    dve.wait_ge(S["oo_d"], m.pair + 1)
                    wait(dve, S["Q_d"], m.n)
                    v.tensor_scalar(Qend[:, :], iota[:, :], oo[m.pp][:, 1, m.p2:m.p2 + 1], None, ALU.is_gt)\
                     .then_inc(S["Qe_d"], 1)
                if t == 6:
                    v.tensor_scalar(Qbeg[:, :], iota[:, :], oo[m.pp][:, 0, m.p2:m.p2 + 1], None, ALU.is_gt)\
                     .then_inc(S["Qb_d"], 1)
                if t == 7:
                    dve.wait_ge(S["Qe_d"], m.n + 1)
                    dve.wait_ge(S["Qb_d"], m.n + 1)
                    wait(dve, S["gw_d"], TILES * m.n - 3 * TILES)
                    v.tensor_tensor(Q[m.p4][:, :], Qbeg[:, :], Qend[:, :], ALU.subtract)\
                     .then_inc(S["Q_d"], 1)

            def sum_out(e):
                dve.wait_ge(S["y_mm"], TILES * e.n + TILES)
                if e.p2 == 0:
                    wait(dve, S["dp"], e.pair)
                v.tensor_copy(yT[:, e.p2, :], psY[:, 0, :]).then_inc(S["yT_d"], 1)

            def silu(d, n, stage):
                at = 2 * d + n
                if stage == 0:
                    dve.wait_ge(S["z_p"], at)
                    wait(dve, S["st_d"], at - 1)
                    v.tensor_tensor(zs[:, :, :], psA, lb_bc[:, :, :], ALU.add).then_inc(S["zs_d"], 1)
                if stage == 1:
                    dve.wait_ge(S["zln_d"], at)
                    wait(dve, S["zgate_d"], at - 1)
                    v.scalar_tensor_tensor(zsig[:, :, :], zs[:, :, :], 0.0, zln[:, :, :], ALU.min, ALU.subtract)\
                     .then_inc(S["zsig_d"], 1)
                if stage == 2:
                    dve.wait_ge(S["zgate_d"], at)
                    wait(dve, S["hn_p2" if n == 1 else "res_d"], d)
                    v.tensor_tensor(hs[n][:, :, :], zs[:, :, :], zgate[:, :, :], ALU.mult).then_inc(S["st_d"], 1)

            def prep_vectors(b, t):
                q = prep_pair(b)
                c = q.pair
                if not q.within(NB):
                    return
                if b.p2 == 0:
                    if t == 0:
                        dve.wait_ge(S[f"x_in{q.pp}"], 16 * q.half + 16)
                        moments(c, xin[q.pp], bn1, mv1, S["bn1_d"], S["mv1_d"], 0)
                    if t == 1:
                        wait(dve, S["nm1_d"], c)
                        moments(c, xin[q.pp], bn1, mv1, S["bn1_d"], S["mv1_d"], 1)
                    if t == 4:
                        dve.wait_ge(S["adjTp"], c + 1)
                        wait(dve, S["adjL_d"], c - 1)
                        wait(dve, S["adjS_d"], c - 1)
                        wait(dve, S["maskT_d"], c - 1)
                        v.tensor_copy(adjT[q.pp][:, :, :], psA).then_inc(S["adjT_d"], 1)
                    if t == 6:
                        dve.wait_ge(S["rank_d"], c + 1)
                        wait(dve, S["key_d"], 2 * c)
                        v.tensor_copy(rank[:, :, :], psA).then_inc(S["rank_c"], 1)
                    if t == 7:
                        dve.wait_ge(S["rank_c"], c + 1)
                        wait(dve, S["offs_d"], c)
                        v.tensor_copy(deg[:, :], rank[:, :, P - 1]).then_inc(S["deg_d"], 1)
                else:
                    if t == 3:
                        dve.wait_ge(S["offs_d"], c + 1)
                        if (b + -1).within(NB):
                            dve.wait_ge(S["erow_d"], b.n)
                        wait(dve, S["key_d"], 2 * c - 2)
                        wait(dve, S["Qb_d"], 2 * c - 2)
                        wait(dve, S["Qe_d"], 2 * c - 2)
                        wait(dve, S["most_d"], c - 1)
                        v.tensor_copy(oo[q.pp][:, :, :], psO).then_inc(S["oo_d"], 1)
                    if t == 4:
                        dve.wait_ge(S["oo_d"], c + 1)
                        dve.wait_ge(S["maskT_d"], c + 1)
                        wait(dve, S["kx_d"], 2 * TILES * (c - 1))
                        for k in range(2):
                            v.scalar_tensor_tensor(key[q.pp][:, k, :], rank[:, k, :],
                                                   oo[q.pp][:, 0, k:k + 1], maskT[:, k, :],
                                                   ALU.add, ALU.mult).then_inc(S["key_d"], 1)
                    if t == 6:
                        wait(dve, S["most_d"], c)
                        v.tensor_tensor(most[:, :], most[:, :], oo[q.pp][:, 1, :], ALU.max)\
                         .then_inc(S["most_d"], 1)

            def rest_vectors(b, t):
                s, d = b + -D_STEP, (b + -D_STEP).pair
                if b.p2 == 1 and s.within(NB):
                    if t == 4:
                        dve.wait_ge(S["dp"], d + 1)
                        wait(dve, S["dsp_d"], d)
                        v.tensor_scalar(ds[:, :, :], psA, bd1c, None, ALU.add).then_inc(S["ds_d"], 1)
                    if t == 7:
                        dve.wait_ge(S["dln_d"], d + 1)
                        wait(dve, S["ep"], d)
                        v.scalar_tensor_tensor(dsp[:, :, :], ds[:, :, :], 0.0, dln[:, :, :], ALU.max, ALU.add)\
                         .then_inc(S["dsp_d"], 1)
                s, d = b + -E_STEP, (b + -E_STEP).pair
                if b.p2 == 0 and s.within(NB):
                    if t == 0:
                        dve.wait_ge(S["ep"], d + 1)
                        dve.wait_ge(S["xb_d"], d + 1)
                        wait(dve, S["res_d"], d - 1)
                        wait(dve, S["h2_d"], 2 * d - 2)
                        v.tensor_tensor(x2[s.pp][:, :, :], psA, xb[:, :, :], ALU.add)\
                         .then_inc(S["x2_d"], 1)
                    if t == 1:
                        dve.wait_ge(S["x2_d"], d + 1)
                        moments(d, x2[s.pp], bn2, mv2, S["bn2_d"], S["mv2_d"], 0)
                    if t == 2:
                        wait(dve, S["nm2_d"], d)
                        moments(d, x2[s.pp], bn2, mv2, S["bn2_d"], S["mv2_d"], 1)
                s = b + -Z1_STEP
                if b.p2 == 1 and s.within(NB) and t in SILU1_SLOT:
                    silu(s.pair, 1, SILU1_SLOT.index(t))
                s = b + -Z2_STEP
                if b.p2 == 0 and s.within(NB) and t in SILU2_SLOT:
                    silu(s.pair, 2, SILU2_SLOT.index(t))

            SILU1_SLOT, SILU2_SLOT = [0, 3, 5], [2, 5, 7]

            def step(b):
                for t in range(TILES):
                    e, u = filter_tile(b, t)
                    if t == 1 and (b + -4).within(NB):
                        sum_out(b + -4)
                    if t % 2 == 1:
                        for k in (1, 0):
                            if b.within(NB):
                                list_edges(b, t - k)
                        for k in (1, 0):
                            if e.within(NB):
                                message(e, u - k)
                    rest_vectors(b, t)
                    prep_vectors(b, t)
                    if (b + 1).within(NB):
                        owners(b + 1, t)

            steps(dve, step)

        @block.scalar
        def _(act):
            a = nc.scalar.activation
            nc.scalar.preload_act_table_set("natural_log_exp_and_others")
            act.wait_ge(S["w_in"], W_LOADS)
            act.wait_ge(S["c_in"], 32)
            act.wait_ge(S["w_cast"], 8)

            def hidden(e, c):
                part = ROUNDS[c]
                exp_at = ex[:, :].rearrange("p (s n) -> p s n", s=2)[:, :, part]
                hid_at = hid[e.p2][:, :].rearrange("p (s n) -> p s n", s=2)[:, :, part]
                act.wait_ge(S["x_d"], 4 * e.n + 2 * c + 2)
                wait(act, S["hid_d"], 2 * e.n + c - 1)
                a(exp_at, psX[:, :, 0:part.stop - part.start], ACT.Exp, bias=b1c).then_inc(S["ex_d"], 1)
                act.wait_ge(S["ex_d"], 2 * e.n + c + 1)
                wait(act, S["gw_d"], TILES * e.n - TILES)
                a(hid_at, exp_at, ACT.Ln, bias=half_c[:, :], scale=0.5).then_inc(S["hid_d"], 1)

            def softplus_of_d(b):
                d = (b + -D_STEP).pair
                act.wait_ge(S["ds_d"], d + 1)
                a(dabs[:, :, :], ds[:, :, :], ACT.Abs).then_inc(S["abs_d"], 1)
                act.wait_ge(S["abs_d"], d + 1)
                a(dexp[:, :, :], dabs[:, :, :], ACT.Exp, scale=-1.0).then_inc(S["dexp_d"], 1)
                act.wait_ge(S["dexp_d"], d + 1)
                wait(act, S["dsp_d"], d)
                a(dln[:, :, :], dexp[:, :, :], ACT.Ln, bias=half_c[:, :], scale=0.5).then_inc(S["dln_d"], 1)

            def silu(d, n, stage):
                at = 2 * d + n
                if stage == 0:
                    act.wait_ge(S["zs_d"], at)
                    a(zabs[:, :, :], zs[:, :, :], ACT.Abs).then_inc(S["zabs_d"], 1)
                    act.wait_ge(S["zabs_d"], at)
                    a(zexp[:, :, :], zabs[:, :, :], ACT.Exp, scale=-1.0).then_inc(S["zexp_d"], 1)
                    act.wait_ge(S["zexp_d"], at)
                    wait(act, S["zsig_d"], at - 1)
                    a(zln[:, :, :], zexp[:, :, :], ACT.Ln, bias=one_c[:, :]).then_inc(S["zln_d"], 1)
                if stage == 1:
                    act.wait_ge(S["zsig_d"], at)
                    wait(act, S["st_d"], at - 1)
                    a(zgate[:, :, :], zsig[:, :, :], ACT.Exp).then_inc(S["zgate_d"], 1)

            def normalized(dst, src, rs, nm, s_dst):
                for k in range(2):
                    a(dst[:, k, :], src[:, k, :], ACT.Relu, bias=nm[:, k:k + 1], scale=rs[:, k:k + 1])\
                        .then_inc(s_dst, 1)

            def chunk_copies(b, t):
                h = t // 2
                if b.within(NB):
                    act.wait_ge(S["kx_d"], TILES * b.n + 2 * h + 2)
                    wait(act, S["w_d"], TILES * b.n + 2 * (h - 1))
                    a(Ksb[:, (b.p2 + h) % 2], psKV[:, (b.p2 + h) % 2, 0], ACT.Copy).then_inc(S["kc_d"], 1)
                e, u = filter_tile(b, t)
                h = u // 2
                if e.within(NB):
                    act.wait_ge(S["gw_d"], TILES * e.n + 2 * h + 2)
                    wait(act, S["msg_d"], TILES * e.n + 2 * (h - 1))
                    a(Gsb[:, (e.p2 + h) % 2], psGF[:, (e.p2 + h) % 2, 0], ACT.Copy).then_inc(S["gc_d"], 1)

            def step(b):
                q, m = prep_pair(b), b + -1
                c, prep = q.pair, q.within(NB)
                s_d, s_e, s_1, s_2 = (b + -n for n in (D_STEP, E_STEP, Z1_STEP, Z2_STEP))
                for t in range(TILES):
                    if t % 2 == 1:
                        chunk_copies(b, t)
                    if t == 2:
                        if b.p2 == 1 and s_1.within(NB):
                            silu(s_1.pair, 1, 0)
                        if m.within(NB):
                            act.wait_ge(S["et_d"], m.n + 1)
                            if b.p2 == 1 and prep:
                                act.wait_ge(S["offs_d"], c + 1)
                            wait(act, S["e_out"], 16 * (m.n - 1))
                            a(erow[m.p2][:, :], psE, ACT.Copy).then_inc(S["erow_d"], 1)
                        if b.p2 == 1 and prep:
                            act.wait_ge(S["h1Tp"], c + 1)
                            wait(act, S["rfp"], c)
                            a(h1T[:, :, :], psA, ACT.Copy).then_inc(S["h1T_d"], 1)
                    if t == 3 and b.p2 == 0 and prep:
                        act.wait_ge(S["nm1_d"], c + 1)
                        wait(act, S["h1Tp"], c)
                        normalized(h1, xin[q.pp], rs1, nm1, S["h1_d"])
                    if t == 4 and b.p2 == 0 and s_2.within(NB):
                        silu(s_2.pair, 2, 0)
                    if t == 5 and b.p2 == 0 and s_e.within(NB):
                        act.wait_ge(S["nm2_d"], s_e.pair + 1)
                        wait(act, S["hn_p1"], s_e.pair)
                        normalized(hs[0], x2[s_e.pp], rs2, nm2, S["h2_d"])
                    if t == 5 and b.p2 == 1 and s_1.within(NB):
                        silu(s_1.pair, 1, 1)
                    if t == 6 and b.p2 == 1 and s_d.within(NB):
                        softplus_of_d(b)
                    if t in ROUND_SLOT and (b + -2).within(NB):
                        hidden(b + -2, ROUND_SLOT.index(t))
                    if t == 6 and b.p2 == 1 and prep:
                        act.wait_ge(S["rfp"], c + 1)
                        wait(act, S["rfr_d"], c - 1)
                        wait(act, S["rfhi"], c - 1)
                        a(rf[q.pp][:, :, :], psA, ACT.Copy).then_inc(S["rf_d"], 1)
                    if t == 7 and b.p2 == 0 and s_2.within(NB):
                        silu(s_2.pair, 2, 1)
                    if t == 8:
                        s, n = (s_e, 1) if b.p2 == 0 else (s_1, 2)
                        if s.within(NB):
                            act.wait_ge(S[f"hn_p{n}"], s.pair + 1)
                            wait(act, S["z_p"], 2 * s.pair + n - 1)
                            a(hnT[:, :, :], psA, ACT.Copy).then_inc(S[f"hn_c{n}"], 1)
                    if m.within(NB) and t == 9:
                        act.wait_ge(S[f"eb_in{m.p2}"], 32 * (2 * m.half + m.p4 // 2) + 32)
                        wait(act, S["gau_d"], m.n)
                        a(dsq[:, :], eb[m.p2][:, :], ACT.Square, bias=neg_off).then_inc(S["dsq_d"], 1)
                        act.wait_ge(S["dsq_d"], m.n + 1)
                        wait(act, S["x_d"], 4 * m.n)
                        a(gau[:, :], dsq[:, :], ACT.Exp, scale=COEFF).then_inc(S["gau_d"], 1)

            steps(act, step)

        @block.gpsimd
        def _(pool):
            g = nc.gpsimd
            pool.wait_ge(S["w_in"], W_LOADS)
            pool.wait_ge(S["w_cast"], 8)

            def split(part, rest, src, s_hi, s_rest, s_mid, s_all, c, read):
                read()
                settle(pool, S)
                g.tensor_copy(part[:, 0], src).then_inc(s_hi, 1)
                pool.wait_ge(s_hi, c + 1)
                wait(pool, s_all, c)
                g.tensor_tensor(rest, src, part[:, 0], ALU.subtract).then_inc(s_rest, 1)
                pool.wait_ge(s_rest, c + 1)
                settle(pool, S)
                g.tensor_copy(part[:, 1], rest).then_inc(s_mid, 1)
                pool.wait_ge(s_mid, c + 1)
                g.tensor_tensor(part[:, 2], rest, part[:, 1], ALU.subtract).then_inc(s_all, 1)

            def deviations(c, mv, tt, rs, nm, names, read):
                s_mv, s_ve, s_ng, s_rs, s_nm = (S[k] for k in names)
                pool.wait_ge(s_mv, 2 * c + 2)
                wait(pool, s_nm, c)
                settle(pool, S)
                g.tensor_scalar(tt[:, 0], mv[:, :, 1], EPS, None, ALU.add).then_inc(s_ve, 1)
                g.tensor_scalar(tt[:, 1], mv[:, :, 0], -1.0, None, ALU.mult).then_inc(s_ng, 1)
                pool.wait_ge(s_ve, c + 1)
                wait(pool, read, 2 * c)
                g.tensor_tensor(rs[:, :], tt[:, 0], mhalf[:, :], ALU.pow).then_inc(s_rs, 1)
                pool.wait_ge(s_ng, c + 1)
                pool.wait_ge(s_rs, c + 1)
                g.tensor_tensor(nm[:, :], tt[:, 1], rs[:, :], ALU.mult).then_inc(s_nm, 1)

            def even_step(b):
                q = prep_pair(b)
                c = q.pair
                if q.within(NB):
                    pool.wait_ge(S[f"a_in{q.pp}"], 16 * q.half + 16)
                    wait(pool, S["rank_d"], c)
                    settle(pool, S)
                    g.tensor_scalar(maskN[:, :, :], adjin[q.pp][:, :, :], 0.0, 0.0, ALU.is_equal, ALU.is_equal)\
                     .then_inc(S["maskN_d"], 1)
                    deviations(c, mv1, tt1, rs1, nm1, ("mv1_d", "ve1_d", "ng1_d", "rs1_d", "nm1_d"), S["h1_d"])
                s = b + -E_STEP
                if s.within(NB):
                    deviations(s.pair, mv2, tt2, rs2, nm2, ("mv2_d", "ve2_d", "ng2_d", "rs2_d", "nm2_d"),
                               S["h2_d"])
                if q.within(NB):
                    pool.wait_ge(S["adjT_d"], c + 1)
                    aT = adjT[q.pp][:, :, :]
                    wait(pool, S["key_d"], 2 * c)
                    settle(pool, S)
                    g.tensor_scalar(maskT[:, :, :], aT, 0.0, 0.0, ALU.is_equal, ALU.is_equal).then_inc(S["maskT_d"], 1)
                    split(adjS[q.pp], adjr[:, :, :], aT, S["ahi"], S["adjr_d"], S["amid"], S["adjS_d"], c,
                          lambda: wait(pool, S["kx_d"], 2 * TILES * (c - 1)))
                r = b + -4
                if r.within(NB):
                    pool.wait_ge(S["adjL_d"], r.pair + 1)
                    wait(pool, S["hn_p2"], r.pair - 1)
                    settle(pool, S)
                    g.tensor_copy(adjM[r.pp][:, :, :], adjL[r.pp][:, :, :]).then_inc(S["adjM_d"], 1)
                o = b + -Z2_STEP
                if o.within(NB):
                    pool.wait_ge(S["st_d"], 2 * o.pair + 2)
                    wait(pool, S[f"o_out{o.pp}"], 16 * o.half)
                    g.tensor_tensor(res[o.pp][:, :, :], x2[o.pp][:, :, :], hs[2][:, :, :], ALU.add)\
                     .then_inc(S["res_d"], 1)

            def odd_step(b):
                s = b + -D_STEP
                if s.within(NB):
                    pool.wait_ge(S[f"xp_in{s.pp}"], 16 * s.half + 16)
                    wait(pool, S["x2_d"], s.pair)
                    for k in range(2):
                        last = g.tensor_tensor(xb[:, k, :], xpost[s.pp][:, k, :], bd2_bc[:, :], ALU.add)
                    last.then_inc(S["xb_d"], 1)
                r = b + -1
                if r.within(NB):
                    wait(pool, S["adjM_d"], r.pair - 1)
                    settle(pool, S)
                    g.tensor_copy(adjL[r.pp][:, :, :], adjT[r.pp][:, :, :]).then_inc(S["adjL_d"], 1)
                    c = r.pair
                    pool.wait_ge(S["rf_d"], c + 1)
                    split(rfS[r.pp], rfr[:, :, :], rf[r.pp][:, :, :], S["rfhi"], S["rfr_d"], S["rfmid"],
                          S["rfS_d"], c, lambda: wait(pool, S["gw_d"], 2 * TILES * (c - 1)))

            def step(b):
                if b.p2 == 0:
                    even_step(b)
                else:
                    odd_step(b)

            steps(pool, step)

        block.__exit__(None, None, None)

        ORDER = {
            "pe": ("count", "hT rf aT", "xp f y", "d e hn1 z1 hn2 z2"),
            "act": ("", "h hTc rfc", "dsq gau abs exp ln",
                    "dabs dexp dln h2 hc1 za1 ze1 zl1 zg1 hc2 za2 ze2 zl2 zg2"),
            "dve": ("bound bneg babs wide most isw flags flag", "bn mv aTc sq", "rel sum col msg ysb",
                    "ds dsp x2 bn2 mv2 zs1 zt1 st1 zs2 zt2 st2"),
            "pool": ("", "ve ng rs nm xb", "", "ve2 ng2 rs2 nm2 res"),
        }
        NQ = P // ROWS
        G = {k: sem("g_" + k) for k in ("pe", "act", "dve", "pool", "x", "adj", "eb", "out")}

        def after(eng, name, b=None, q=None):
            for owner, parts in ORDER.items():
                once, head, rows, tail = (p.split() for p in parts)
                graph = len(head) + NQ * len(rows) + len(tail)
                if name in once:
                    eng.wait_ge(G[owner], once.index(name) + 1)
                if name in head:
                    eng.wait_ge(G[owner], b * graph + (len(once) + head.index(name) + 1))
                if name in rows:
                    eng.wait_ge(G[owner], b * graph + q * len(rows) + (len(once) + len(head) + rows.index(name) + 1))
                if name in tail:
                    eng.wait_ge(G[owner], b * graph + (graph - len(tail) + len(once) + tail.index(name) + 1))

        flag = sb("flag", [P, 1], I32)
        bound = sb("bound", [P, 4])
        flags = sb("flags", [P, 1], BF16)
        gx, gadj, gsq = xin[0][:, 0, :], adjin[0][:, 0, :], xin[0][:, 1, :]
        geb, gdsq, ggau = eb[0][0:NG, 0:512], dsq[0:NG, 0:512], gau[0:NG, 0:512]
        gcol, gy, gmsg = cols2[:, :], yT[:, 0, :], msg[:, 0:ROWS, :]
        ps0, ps1, ps2, ps3 = psM[:, 0, :], psX[:, 0, :], psY[:, :, :], psX[:, 1, 0:ROWS]
        with nc.Block() as general:
            def needed(eng):
                return eng.value_load(flag[0:1, 0:1], min_val=0, max_val=2 * P)

            @general.sync
            def _(sp):
                after(sp, "flag")
                with sp.If(needed(sp) > 0):
                    with sp.Fori(0, NB) as b:
                        sp.wait_ge(G["out"], 16 * b)
                        settle(sp, S)
                        sp.dma_start(gx, x[bass.ds(b, 1)].rearrange("b n d -> (b n) d")).then_inc(G["x"], 16)
                        sp.dma_start(gadj, adj[bass.ds(b, 1)].rearrange("b n d -> (b n) d"))\
                          .then_inc(G["adj"], 16)
                        with sp.Fori(0, NQ) as q:
                            n = b * NQ + q
                            once, head, rows, tail = (len(p.split()) for p in ORDER["dve"])
                            sp.wait_ge(G["dve"], b * (head + NQ * rows + tail) + q * rows + once + head)
                            settle(sp, S)
                            src = adj[bass.ds(b, 1), bass.ds(q * ROWS, ROWS), :].rearrange("b i j -> b (i j)")
                            sp.dma_start(geb, src.to_broadcast((NG, 512))).then_inc(G["eb"], 16)
                        after(sp, "res", b)
                        settle(sp, S)
                        sp.dma_start(out[bass.ds(b, 1)].rearrange("b n d -> (b n) d"), res[0][:, 0, :])\
                          .then_inc(G["out"], 16)
                    sp.wait_ge(G["out"], 16 * NB)

            @general.tensor
            def _(pe):
                def mm(o, a, b, start=True, stop=True):
                    return nc.tensor.matmul(o, a, b, start=start, stop=stop)

                after(pe, "flags")
                mm(ps0[:, 0:1], ones[:, :], flags[:, :]).then_inc(G["pe"], 1)
                after(pe, "flag")
                with pe.If(needed(pe) > 0):
                    with pe.Fori(0, NB) as b:
                        after(pe, "h", b)
                        nc.tensor.transpose(ps0, h1[:, 0, :], ident).then_inc(G["pe"], 1)
                        after(pe, "hTc", b)
                        mm(ps0, h1T[:, 0, :], WaT).then_inc(G["pe"], 1)
                        after(pe, "rfc", b)
                        pe.wait_ge(G["adj"], 16 * b + 16)
                        nc.tensor.transpose(ps0, gadj, ident).then_inc(G["pe"], 1)
                        with pe.Fori(0, NQ) as q:
                            n = b * NQ + q
                            after(pe, "gau", b, q)
                            mm(ps1, W1T[0:NG, :], ggau).then_inc(G["pe"], 1)
                            after(pe, "sum", b, q)
                            for r in range(ROWS):
                                mm(ps2[:, r, :], hid[0][:, r * P:(r + 1) * P], W2T, True, False)
                                last = mm(ps2[:, r, :], ones[:, :], b2row[:, :], False, True)
                            last.then_inc(G["pe"], 1)
                            after(pe, "msg", b, q)
                            after(pe, "col", b, q)
                            for r in range(ROWS):
                                last = mm(ps3[:, r:r + 1], gmsg[:, r, :], gcol[:, r:r + 1])
                            last.then_inc(G["pe"], 1)
                        after(pe, "ysb", b, NQ - 1)
                        mm(ps0, Wd1T, gy).then_inc(G["pe"], 1)
                        after(pe, "dsp", b)
                        mm(ps0, dsp[:, 0, :], Wd2T).then_inc(G["pe"], 1)
                        for k in (1, 2):
                            after(pe, "h2" if k == 1 else "st1", b)
                            mm(ps0, hs[k - 1][:, 0, :], adjT[0][:, 0, :]).then_inc(G["pe"], 1)
                            after(pe, f"hc{k}", b)
                            mm(ps0, hnT[:, 0, :], lw[:, :]).then_inc(G["pe"], 1)

            @general.vector
            def _(dve):
                v = nc.vector
                v.tensor_reduce(bound[:, 0:1], wraw[:, 0, 0:NG], AX.X, ALU.add, apply_absolute_value=True)\
                 .then_inc(G["dve"], 1)
                v.tensor_scalar(bound[:, 1:2], b1c, -1.0, None, ALU.mult).then_inc(G["dve"], 1)
                after(dve, "bneg")
                v.tensor_tensor(bound[:, 1:2], bound[:, 1:2], b1c, ALU.max).then_inc(G["dve"], 1)
                after(dve, "bound")
                after(dve, "babs")
                v.tensor_tensor(bound[:, 2:3], bound[:, 0:1], bound[:, 1:2], ALU.add).then_inc(G["dve"], 1)
                v.tensor_tensor(bound[:, 3:4], most[:, 0:1], most[:, 1:2], ALU.max).then_inc(G["dve"], 1)
                after(dve, "most")
                v.tensor_scalar(bound[:, 2:3], bound[:, 2:3], SAFE, None, ALU.is_gt).then_inc(G["dve"], 1)
                after(dve, "isw")
                v.scalar_tensor_tensor(flags[:, :], bound[:, 3:4], float(LIMIT), bound[:, 2:3],
                                       ALU.is_gt, ALU.add).then_inc(G["dve"], 1)
                after(dve, "count")
                v.tensor_copy(flag[:, :], ps0[:, 0:1]).then_inc(G["dve"], 1)
                after(dve, "flag")
                with dve.If(needed(dve) > 0):
                    with dve.Fori(0, NB) as b:
                        dve.wait_ge(G["x"], 16 * b + 16)
                        v.bn_stats(bn1[:, 0, :], gx).then_inc(G["dve"], 1)
                        after(dve, "bn", b)
                        settle(dve, S)
                        v.bn_aggr(mv1[:, 0, :], bn1[:, 0, :]).then_inc(G["dve"], 1)
                        after(dve, "aT", b)
                        v.tensor_copy(adjT[0][:, 0, :], ps0).then_inc(G["dve"], 1)
                        after(dve, "aTc", b)
                        v.tensor_tensor(gsq, adjT[0][:, 0, :], adjT[0][:, 0, :], ALU.mult).then_inc(G["dve"], 1)
                        after(dve, "sq", b)
                        settle(dve, S)
                        with dve.Fori(0, NQ) as q:
                            n = b * NQ + q
                            after(dve, "ln", b, q)
                            v.tensor_scalar(ex[:, 512:1024], ps1, b1c, 0.0, ALU.add, ALU.max)\
                             .then_inc(G["dve"], 1)
                            after(dve, "rel", b, q)
                            v.tensor_tensor(hid[0][:, 0:512], ex[:, 0:512], ex[:, 512:1024], ALU.add)\
                             .then_inc(G["dve"], 1)
                            v.tensor_copy(gcol, xin[0][:, 1, bass.ds(q * ROWS, ROWS)]).then_inc(G["dve"], 1)
                            after(dve, "f", b, q)
                            for r in range(ROWS):
                                last = v.tensor_tensor(gmsg[:, r, :], ps2[:, r, :], rf[0][:, 0, :], ALU.mult)
                            last.then_inc(G["dve"], 1)
                            after(dve, "y", b, q)
                            v.tensor_copy(yT[:, 0, bass.ds(q * ROWS, ROWS)], ps3).then_inc(G["dve"], 1)
                        after(dve, "d", b)
                        v.tensor_scalar(ds[:, 0, :], ps0, bd1c, None, ALU.add).then_inc(G["dve"], 1)
                        after(dve, "dln", b)
                        v.scalar_tensor_tensor(dsp[:, 0, :], ds[:, 0, :], 0.0, dln[:, 0, :], ALU.max, ALU.add)\
                         .then_inc(G["dve"], 1)
                        after(dve, "xb", b)
                        after(dve, "e", b)
                        v.tensor_tensor(x2[0][:, 0, :], ps0, xb[:, 0, :], ALU.add).then_inc(G["dve"], 1)
                        after(dve, "x2", b)
                        v.bn_stats(bn2[:, 0, :], x2[0][:, 0, :]).then_inc(G["dve"], 1)
                        after(dve, "bn2", b)
                        settle(dve, S)
                        v.bn_aggr(mv2[:, 0, :], bn2[:, 0, :]).then_inc(G["dve"], 1)
                        for k in (1, 2):
                            after(dve, f"z{k}", b)
                            v.tensor_tensor(zs[:, 0, :], ps0, lb_bc[:, 0, :], ALU.add).then_inc(G["dve"], 1)
                            after(dve, f"zl{k}", b)
                            v.scalar_tensor_tensor(zsig[:, 0, :], zs[:, 0, :], 0.0, zln[:, 0, :], ALU.min,
                                                   ALU.subtract).then_inc(G["dve"], 1)
                            after(dve, f"zg{k}", b)
                            v.tensor_tensor(hs[k][:, 0, :], zs[:, 0, :], zgate[:, 0, :], ALU.mult)\
                             .then_inc(G["dve"], 1)

            @general.scalar
            def _(act):
                a = nc.scalar.activation
                after(act, "flag")
                with act.If(needed(act) > 0):
                    nc.scalar.preload_act_table_set("natural_log_exp_and_others")
                    with act.Fori(0, NB) as b:
                        after(act, "nm", b)
                        a(h1[:, 0, :], gx, ACT.Relu, bias=nm1[:, 0:1], scale=rs1[:, 0:1]).then_inc(G["act"], 1)
                        after(act, "hT", b)
                        a(h1T[:, 0, :], ps0, ACT.Copy).then_inc(G["act"], 1)
                        after(act, "rf", b)
                        a(rf[0][:, 0, :], ps0, ACT.Copy).then_inc(G["act"], 1)
                        after(act, "sq", b)
                        with act.Fori(0, NQ) as q:
                            n = b * NQ + q
                            act.wait_ge(G["eb"], 16 * n + 16)
                            a(gdsq, geb, ACT.Square, bias=cst[0:NG, C_NO:C_NO + 1]).then_inc(G["act"], 1)
                            after(act, "dsq", b, q)
                            a(ggau, gdsq, ACT.Exp, scale=COEFF).then_inc(G["act"], 1)
                            after(act, "xp", b, q)
                            a(ex[:, 0:512], ps1, ACT.Abs, bias=b1c).then_inc(G["act"], 1)
                            after(act, "abs", b, q)
                            a(ex[:, 512:1024], ex[:, 0:512], ACT.Exp, scale=-1.0).then_inc(G["act"], 1)
                            after(act, "exp", b, q)
                            a(ex[:, 0:512], ex[:, 512:1024], ACT.Ln, bias=half_c[:, :], scale=0.5)\
                                .then_inc(G["act"], 1)
                        after(act, "ds", b)
                        a(dabs[:, 0, :], ds[:, 0, :], ACT.Abs).then_inc(G["act"], 1)
                        after(act, "dabs", b)
                        a(dexp[:, 0, :], dabs[:, 0, :], ACT.Exp, scale=-1.0).then_inc(G["act"], 1)
                        after(act, "dexp", b)
                        a(dln[:, 0, :], dexp[:, 0, :], ACT.Ln, bias=half_c[:, :], scale=0.5)\
                            .then_inc(G["act"], 1)
                        after(act, "nm2", b)
                        a(hs[0][:, 0, :], x2[0][:, 0, :], ACT.Relu, bias=nm2[:, 0:1], scale=rs2[:, 0:1])\
                            .then_inc(G["act"], 1)
                        for k in (1, 2):
                            after(act, f"hn{k}", b)
                            a(hnT[:, 0, :], ps0, ACT.Copy).then_inc(G["act"], 1)
                            after(act, f"zs{k}", b)
                            a(zabs[:, 0, :], zs[:, 0, :], ACT.Abs).then_inc(G["act"], 1)
                            after(act, f"za{k}", b)
                            a(zexp[:, 0, :], zabs[:, 0, :], ACT.Exp, scale=-1.0).then_inc(G["act"], 1)
                            after(act, f"ze{k}", b)
                            a(zln[:, 0, :], zexp[:, 0, :], ACT.Ln, bias=one_c[:, :]).then_inc(G["act"], 1)
                            after(act, f"zt{k}", b)
                            a(zgate[:, 0, :], zsig[:, 0, :], ACT.Exp).then_inc(G["act"], 1)

            @general.gpsimd
            def _(pool):
                g = nc.gpsimd

                def deviation(b, mv, tt, rs, nm, names):
                    s_mv, s_ve, s_ng, s_rs = names
                    after(pool, s_mv, b)
                    settle(pool, S)
                    g.tensor_scalar(tt[:, 0, 0:1], mv[:, 0, 1:2], EPS, None, ALU.add).then_inc(G["pool"], 1)
                    g.tensor_scalar(tt[:, 1, 0:1], mv[:, 0, 0:1], -1.0, None, ALU.mult).then_inc(G["pool"], 1)
                    after(pool, s_ve, b)
                    g.tensor_tensor(rs[:, 0:1], tt[:, 0, 0:1], mhalf[:, 0:1], ALU.pow).then_inc(G["pool"], 1)
                    after(pool, s_ng, b)
                    after(pool, s_rs, b)
                    g.tensor_tensor(nm[:, 0:1], tt[:, 1, 0:1], rs[:, 0:1], ALU.mult).then_inc(G["pool"], 1)

                after(pool, "flag")
                with pool.If(needed(pool) > 0):
                    with pool.Fori(0, NB) as b:
                        deviation(b, mv1, tt1, rs1, nm1, ("mv", "ve", "ng", "rs"))
                        pool.wait_ge(G["x"], 16 * b + 16)
                        g.tensor_tensor(xb[:, 0, :], gx, bd2_bc[:, :], ALU.add).then_inc(G["pool"], 1)
                        deviation(b, mv2, tt2, rs2, nm2, ("mv2", "ve2", "ng2", "rs2"))
                        after(pool, "st2", b)
                        g.tensor_tensor(res[0][:, 0, :], x2[0][:, 0, :], hs[2][:, 0, :], ALU.add)\
                         .then_inc(G["pool"], 1)


def edge_constants():
    import numpy as np
    c = np.zeros((P, C_ALL), np.float32)
    k, m = np.arange(P)[:, None], np.arange(P)[None, :]
    c[:, C_ID:C_ID + P] = k == m
    c[:, C_U:C_U + P] = k <= m
    c[:, C_US:C_US + P] = k < m
    c[:, C_TC:C_TC + TILES] = k + P * np.arange(TILES)[None, :] + 1
    c[:, C_NO] = -np.tile(np.linspace(0.0, CUTOFF, NG, dtype=np.float32), P // NG)
    c[:, C_IO:] = np.arange(1, T + 1)
    return c


_INS = ["x", "adj", "L0_gnn_W1", "L0_gnn_b1", "L0_gnn_W2", "L0_gnn_b2", "L0_gnn_Wa", "L0_gnn_Wd1",
        "L0_gnn_bd1", "L0_gnn_Wd2", "L0_gnn_bd2", "L1_gnn_W", "L1_gnn_b"]


def kernel(**inputs):
    import numpy as np
    import concourse.bacc as bacc
    from concourse.bass_utils import run_bass_kernel_spmd

    nc = bacc.Bacc("TRN2", target_bir_lowering=False, num_devices=1)
    given = {name: np.ascontiguousarray(inputs[name]) for name in _INS}
    given["consts"] = edge_constants()
    arrays = {f"in_{name}": a for name, a in given.items()}
    args = [nc.dram_tensor(f"in_{name}", a.shape, mybir.dt.from_np(a.dtype), kind="ExternalInput").ap()
            for name, a in given.items()]
    out = nc.dram_tensor("out", given["x"].shape, F32, kind="ExternalOutput").ap()
    build(nc, *args, out)
    r = run_bass_kernel_spmd(nc, [arrays], core_ids=[0])
    return r.results[0]["out"]
```

```python
from contextlib import ExitStack

import concourse.bass as bass
from concourse import mybir

ALU = mybir.AluOpType
ACT = mybir.ActivationFunctionType
F32 = mybir.dt.float32
BF16 = mybir.dt.bfloat16
F16 = mybir.dt.float16
F32R = mybir.dt.float32r
I32 = mybir.dt.int32
AX = mybir.AxisListType

P = 128
NG = 64
TILES = 10
T = TILES * P
HALF = T // 2
CUTOFF = 5.0
WIDTH = CUTOFF / (NG - 1)
COEFF = -0.5 / (WIDTH * WIDTH)
EPS = 1e-5
SAFE = 40.0
ROWS = 4
LIMIT = T

C_ID, C_U, C_US, C_TC, C_NO = 0, P, 2 * P, 3 * P, 3 * P + TILES
C_B1, C_BD1, C_W = C_NO + 1, C_NO + 2, C_NO + 3
C_ALL = C_W + 6 * P
R_BD2, R_B2, R_LB = 0, P, 3 * P
R_ALL = 5 * P


class Batch:

    def __init__(self, k, c):
        self.k, self.c = (0, 4 * k + c) if isinstance(k, int) else (k, c)
        self.static = isinstance(k, int)

    def __add__(self, d):
        return Batch(self.k, self.c + d)

    @property
    def n(self):
        return self.c if self.static else 4 * self.k + self.c

    @property
    def pair(self):
        return self.c // 2 if self.static else 2 * self.k + self.c // 2

    @property
    def half(self):
        return self.c // 4 if self.static else self.k + self.c // 4

    @property
    def p4(self):
        return self.c % 4

    @property
    def p2(self):
        return self.c % 2

    @property
    def pp(self):
        return (self.c // 2) % 2

    def within(self, nb):
        return not self.static or 0 <= self.c < nb


def wait(eng, sem, count):
    if not (isinstance(count, int) and count <= 0):
        eng.wait_ge(sem, count)


def settle(eng, S):
    eng.sem_inc(S["settled"], 1)


def build(nc, x, adj, packed, rows, slots, out):
    NB = x.shape[0]
    assert NB % 4 == 0 and NB >= 20

    ctx = ExitStack()
    with ctx:
        def sb(name, shape, dt=F32):
            return ctx.enter_context(nc.sbuf_tensor(name, shape, dt))

        def ps(name, shape):
            return ctx.enter_context(nc.psum_tensor(name, shape, F32))

        def sem(name):
            return ctx.enter_context(nc.semaphore(name))

        e_dram = nc.dram_tensor("edge_values", (NB, TILES, P), F32).ap()

        cst = sb("cst", [P, C_ALL])
        ident = cst[:, C_ID:C_ID + P]
        tcol = cst[:, C_TC:C_TC + TILES]
        neg_off = cst[:, C_NO:C_NO + 1]
        b1c, bd1c = cst[:, C_B1:C_B1 + 1], cst[:, C_BD1:C_BD1 + 1]
        wraw = cst[:, C_W:C_W + 5 * P].rearrange("p (k n) -> p k n", k=5)
        lw = cst[:, C_W + 5 * P:C_ALL]
        upper = sb("upper", [P, P], BF16)
        upper_s = sb("upper_s", [P, P], BF16)
        iota = sb("iota", [P, T], F16)
        wT = sb("wT", [P, 5, P])
        row_bc = sb("row_bc", [P, R_ALL])
        bd2_bc = row_bc[:, R_BD2:R_BD2 + P]
        b2_bc = row_bc[:, R_B2:R_B2 + 2 * P].rearrange("p (k n) -> p k n", k=2)
        lb_bc = row_bc[:, R_LB:R_LB + 2 * P].rearrange("p (k n) -> p k n", k=2)
        W1T, W2T, WaT, Wd1T, Wd2T = (wT[:, k, :] for k in range(5))
        half_c = sb("half_c", [P, 1])
        one_c = sb("one_c", [P, 1])
        mhalf = sb("mhalf", [P, 2])
        ones = sb("ones", [P, P], BF16)

        xin = [sb(f"xin{k}", [P, 2, P]) for k in range(2)]
        adjin = [sb(f"adjin{k}", [P, 2, P]) for k in range(2)]
        bn1 = sb("bn1", [P, 2, 6])
        mv1 = sb("mv1", [P, 2, 2])
        rs1 = sb("rs1", [P, 2])
        tt1 = sb("tt1", [P, 2, 2])
        nm1 = sb("nm1", [P, 2])
        h1 = sb("h1", [P, 2, P])
        h1T = sb("h1T", [P, 2, P])
        rf = [sb(f"rf{k}", [P, 2, P]) for k in range(2)]
        parts = [sb(f"parts{k}", [P, 2, 5, P], F32R) for k in range(2)]
        adjT = [sb(f"adjT{k}", [P, 2, P]) for k in range(2)]
        rfb = [sb(f"rfb{k}", [P, 2, P]) for k in range(2)]
        adjQ = [sb(f"adjQ{k}", [P, 2, P]) for k in range(2)]
        rank = sb("rank", [P, 2, P], F16)
        maskN = sb("maskN", [P, 2, P], BF16)
        maskT = sb("maskT", [P, 2, P], BF16)
        deg = sb("deg", [P, 2], BF16)
        oo = [sb(f"oo{k}", [P, 2, 2]) for k in range(2)]
        most = sb("most", [P, 2])

        Qend = sb("Qend", [P, T], F16)
        Qbeg = sb("Qbeg", [P, T], F16)
        Q = [sb(f"Q{k}", [P, T], F32R) for k in range(2)]
        Ksb = sb("Ksb", [P, 2, 2, P])
        Gsb = [sb(f"Gsb{k}", [P, T]) for k in range(4)]
        Wsc = [sb(f"Wsc{k}", [P, T]) for k in range(4)]
        eT = [sb(f"eT{k}", [P, TILES]) for k in range(4)]
        erow = [sb(f"erow{k}", [TILES, P]) for k in range(2)]
        eb = [sb(f"eb{k}", [P, HALF]) for k in range(2)]
        dsq = sb("dsq", [P, HALF])
        gau = sb("gau", [P, HALF])
        ex = sb("ex", [P, T])
        hid = [sb(f"hid{k}", [P, T]) for k in range(2)]
        msg = sb("msg", [P, 5, P])

        xpost = [sb(f"xpost{k}", [P, 2, P]) for k in range(2)]
        xb = sb("xb", [P, 2, P])
        adjL = [sb(f"adjL{k}", [P, 2, P]) for k in range(2)]
        adjM = [sb(f"adjM{k}", [P, 2, P]) for k in range(2)]
        yT = sb("yT", [P, 2, P])
        ds = sb("ds", [P, 2, P])
        dabs = sb("dabs", [P, 2, P])
        dexp = sb("dexp", [P, 2, P])
        dln = sb("dln", [P, 2, P])
        dsp = sb("dsp", [P, 2, P])
        cols2 = sb("cols2", [P, ROWS])
        x2 = [sb(f"x2_{k}", [P, 2, P]) for k in range(2)]
        bn2 = sb("bn2", [P, 2, 6])
        mv2 = sb("mv2", [P, 2, 2])
        rs2 = sb("rs2", [P, 2])
        tt2 = sb("tt2", [P, 2, 2])
        nm2 = sb("nm2", [P, 2])
        hs = [sb(f"hs{k}", [P, 2, P]) for k in range(3)]
        hnT = sb("hnT", [P, 2, P])
        zs = sb("zs", [P, 2, P])
        zabs = sb("zabs", [P, 2, P])
        zexp = sb("zexp", [P, 2, P])
        zln = sb("zln", [P, 2, P])
        zsig = sb("zsig", [P, 2, P])
        zgate = sb("zgate", [P, 2, P])
        res = [sb(f"res{k}", [P, 2, P]) for k in range(2)]

        flag = sb("flag", [P, 1], I32)
        bound = sb("bound", [P, 4])
        flags = sb("flags", [P, 1], BF16)

        psT = ps("psT", [P, 4, 4, P])
        psY = ps("psY", [P, 4, P])
        psX = ps("psX", [P, 2, 512])
        psM = ps("psM", [P, 4, P])
        psA = psM[:, 0:2, :]
        psW = psT[:, 0]
        psE = psX[0:TILES, 1, 0:P]
        psO = psX[:, 1, P:P + 4]

        names = """w_in w_tr w_tr2 w_cast w_done iota_in row_in
            x_in0 x_in1 a_in0 a_in1 xp_in0 xp_in1 e_out eb_in0 eb_in1 o_out0 o_out1
            bn1_d mv1_d rs1_d nm1_d h1_d h1Tp h1T_d rfp rf_d rfhi rfS_d rfb_d adjQ_d
            adjTp adjT_d ahi adjS_d maskN_d maskT_d rank_d rank_c deg_d offs_d oo_d key_d most_d
            Qe_d Qb_d Q_d kx_d w_d et_d erow_d dsq_d gau_d x_d ex_d hid_d gw_d gc_d msg_d y_mm
            yT_d dp ds_d abs_d dexp_d dln_d dsp_d ep xb_d adjL_d adjM_d x2_d bn2_d mv2_d rs2_d nm2_d h2_d
            ve1_d ng1_d ve2_d ng2_d settled hn_p1 hn_c1 hn_p2 hn_c2 z_p zs_d zabs_d zexp_d zln_d zsig_d zgate_d
            st_d res_d bound_d flags_d count_d flag_d""".split()
        S = {k: sem(k) for k in names}

        block = nc.Block()
        block.__enter__()

        def filter_tile(b, t):
            return (b + -2, t - 8) if t >= 8 else (b + -3, t + TILES - 8)

        def scatter_tile(b, t):
            return (b + -3, t - 2) if t >= 2 else (b + -4, t + TILES - 2)

        def prep_pair(b):
            return b + 2 if b.p2 == 0 else b + 1

        def rf_pair(b):
            return b + 4 if b.p2 == 0 else b + 3

        def bank(b, t):
            return (2 * b.p2 + t) % 4

        D_STEP, E_STEP, Z1_STEP, Z2_STEP = 5, 6, 7, 8
        FLAGS_STEP = NB + 3

        def last_pair(o):
            return o.static and o.c == NB - 2

        def steps(eng, step):
            for n in range(-5, 12):
                step(Batch(0, n))
            with eng.Fori(3, NB // 4 - 2) as k:
                for c in range(4):
                    step(Batch(k, c))
            for n in range(NB - 8, NB + 8):
                step(Batch(0, n))

        BANK_USES = [[("e", lambda b: b + -E_STEP, "x2_d", 1, 1), ("z2", lambda b: b + -Z2_STEP, "zs_d", 2, 2),
                      ("adjT", prep_pair, "adjT_d", 1, 1), ("rank", prep_pair, "rank_c", 1, 1),
                      ("hn1", lambda b: b + -E_STEP, "hn_c1", 1, 1)],
                     [("z1", lambda b: b + -Z1_STEP, "zs_d", 2, 1), ("h1T", rf_pair, "h1T_d", 1, 1),
                      ("d", lambda b: b + -D_STEP, "ds_d", 1, 1), ("rf", rf_pair, "rf_d", 1, 1),
                      ("hn2", lambda b: b + -Z1_STEP, "hn_c2", 1, 1)]]

        def bank_free(pe, b, use):
            at = [u[0] for u in BANK_USES[b.p2]].index(use) - 1
            for _ in range(20):
                if at < 0:
                    b = b + -1
                    at = len(BANK_USES[b.p2]) - 1
                _, pair_of, read, per, add = BANK_USES[b.p2][at]
                if pair_of(b).within(NB):
                    pe.wait_ge(S[read], per * pair_of(b).pair + add)
                    return
                at -= 1

        ROUNDS = [slice(0, 3 * P), slice(3 * P, HALF)]
        ROUND_SLOT = [4, 6]

        @block.sync
        def _(sp):
            def load_x(q):
                wait(sp, S["h1_d"], 2 * q.pair - 2)
                settle(sp, S)
                sp.dma_start(xin[q.pp][:, :, :], x[bass.ds(q.n, 2)].rearrange("b n d -> n b d"))\
                  .then_inc(S[f"x_in{q.pp}"], 16)

            def load_adj(q):
                wait(sp, S["adjTp"], q.pair - 1)
                wait(sp, S["maskN_d"], q.pair - 1)
                settle(sp, S)
                sp.dma_start(adjin[q.pp][:, :, :], adj[bass.ds(q.n, 2)].rearrange("b n d -> n b d"))\
                  .then_inc(S[f"a_in{q.pp}"], 16)

            def step(b):
                if b.static and b.c == -5:
                    load_x(Batch(0, 0))
                    sp.dma_start(cst[:, :], packed).then_inc(S["w_in"], 16)
                if b.p2 == 0 and (b + 4).within(NB):
                    load_adj(b + 4)
                if b.static and b.c == -4:
                    sp.dma_start(iota[:, :], slots.to_broadcast((P, T))).then_inc(S["iota_in"], 16)
                if b.p2 == 0 and (b + 6).within(NB):
                    load_x(b + 6)
                if b.static and b.c == -4:
                    sp.dma_start(row_bc[:, :], rows.to_broadcast((P, R_ALL))).then_inc(S["row_in"], 16)
                if b.p2 == 1 and (b + -3).within(NB):
                    q = b + -3
                    wait(sp, S["xb_d"], q.pair - 1)
                    settle(sp, S)
                    sp.dma_start(xpost[q.pp][:, :, :], x[bass.ds(q.n, 2)].rearrange("b n d -> n b d"))\
                      .then_inc(S[f"xp_in{q.pp}"], 16)
                m = b + -1
                if m.within(NB):
                    sp.wait_ge(S["erow_d"], m.n + 1)
                    settle(sp, S)
                    sp.dma_start(e_dram[bass.ds(m.n, 1)].rearrange("b t p -> (b t) p"), erow[m.p2][:, :])\
                      .then_inc(S["e_out"], 16)
                    sp.wait_ge(S["e_out"], 16 * m.n + 16)
                    settle(sp, S)
                    wait(sp, S["dsq_d"], m.n - 1)
                    settle(sp, S)
                    for s in range(2):
                        src = e_dram[bass.ds(m.n, 1), s * TILES // 2:(s + 1) * TILES // 2]
                        sp.dma_start(eb[m.p2][s * NG:(s + 1) * NG, :],
                                     src.rearrange("b t p -> b (t p)").to_broadcast((NG, HALF)))\
                          .then_inc(S[f"eb_in{m.p2}"], 16)
                o = b + -(Z2_STEP + 1)
                if b.p2 == 1 and o.within(NB):
                    sp.wait_ge(S["res_d"], o.pair + 1)
                    settle(sp, S)
                    sp.dma_start(out[bass.ds(o.n, 2)].rearrange("b n d -> n b d"), res[o.pp][:, :, :])\
                      .then_inc(S[f"o_out{o.pp}"], 16)

            steps(sp, step)
            for k in range(2):
                sp.wait_ge(S[f"o_out{k}"], 16 * NB // 4)

        @block.tensor
        def _(pe):
            def mm(o, a, b, start=True, stop=True):
                return nc.tensor.matmul(o, a, b, start=start, stop=stop)

            pe.wait_ge(S["w_in"], 16)
            for k in range(4):
                nc.tensor.transpose(psW[:, k, :], wraw[:, k, :], ident).then_inc(S["w_tr"], 1)
            nc.tensor.transpose(psA[:, 0, :], wraw[:, 4, :], ident).then_inc(S["w_tr2"], 1)
            pe.wait_ge(S["w_done"], 2)
            pe.wait_ge(S["w_cast"], 7)

            def first_product(e, c):
                if c == 0:
                    pe.wait_ge(S["gau_d"], e.n + 1)
                    rows, pairs = e.n + 2, e.pair + 2 + e.p2
                    pe.wait_ge(S["erow_d"], min(rows, NB) if e.static else rows)
                    pe.wait_ge(S["oo_d"], min(pairs, NB // 2) if e.static else pairs)
                wait(pe, S["ex_d"], 2 * e.n + c)
                for s in range(2):
                    part = ROUNDS[c]
                    last = mm(psX[:, s, 0:part.stop - part.start], W1T[s * NG:(s + 1) * NG, :],
                              gau[s * NG:(s + 1) * NG, part])
                    last.then_inc(S["x_d"], 1)

            def operands(b, t):
                if t in (0, 4):
                    pe.wait_ge(S["Q_d"], 2 * b.n + (2 if t else 1))
                if t == 0:
                    pe.wait_ge(S["key_d"], 2 * b.pair + 2)
                    pe.wait_ge(S["adjS_d"], b.pair + 1)
                    pe.wait_ge(S["rfS_d"], b.pair + 1)

            def expand(b, t):
                q = Q[b.p2][:, t * P:(t + 1) * P]
                mm(psT[:, bank(b, t), 0:3, :], q, parts[b.pp][:, b.p2, 0:3, :], True, False)
                mm(psT[:, bank(b, t), 1:3, :], q, parts[b.pp][:, b.p2, 3:5, :], False, True).then_inc(S["kx_d"], 1)

            def filters(b, t, e, u):
                if u in (0, 3):
                    pe.wait_ge(S["hid_d"], 2 * e.n + (2 if u else 1))
                mm(psT[:, bank(b, t), 3, :], hid[e.p2][:, u * P:(u + 1) * P], W2T).then_inc(S["gw_d"], 1)

            def scatter(e, t):
                if t == 0:
                    wait(pe, S["yT_d"], e.n)
                    pe.wait_ge(S["rfb_d"], e.pair + 1)
                    pe.wait_ge(S["adjQ_d"], e.pair + 1)
                    mm(psY[:, 0, :], rfb[e.pp][:, e.p2, :], adjQ[e.pp][:, e.p2, :], True, False)
                pe.wait_ge(S["msg_d"], TILES * e.n + t + 1)
                mm(psY[:, 0, :], msg[:, t % 5, :], Wsc[e.p4][:, t * P:(t + 1) * P],
                   False, t == TILES - 1).then_inc(S["y_mm"], 1)

            def both(f):
                for k in range(2):
                    last = f(k)
                return last

            def rows_and_offsets(b):
                m, q = b + -1, prep_pair(b)
                wait(pe, S["oo_d"], min(q.pair, NB // 2) if b.static else q.pair)
                if m.within(NB):
                    pe.wait_ge(S["w_d"], TILES * m.n + TILES)
                    wait(pe, S["erow_d"], m.n)
                    wait(pe, S["ex_d"], 2 * m.n - 2)
                    nc.tensor.transpose(psE, eT[m.p4][:, :], ident).then_inc(S["et_d"], 1)
                if q.within(NB) and b.p2 == 1:
                    pe.wait_ge(S["deg_d"], q.pair + 1)
                    wait(pe, S["ex_d"], 2 * (b.n - 2))
                    mm(psO[:, 0:2], upper_s[:, :], deg[:, :])
                    mm(psO[:, 2:4], upper[:, :], deg[:, :]).then_inc(S["offs_d"], 1)

            def prep_products(b, t):
                q = prep_pair(b)
                c = q.pair
                if b.p2 == 0 and t == 4 and q.within(NB):
                    pe.wait_ge(S[f"a_in{q.pp}"], 16 * q.half + 16)
                    bank_free(pe, b, "adjT")
                    both(lambda k: nc.tensor.transpose(psA[:, k, :], adjin[q.pp][:, k, :], ident))\
                        .then_inc(S["adjTp"], 1)
                if b.p2 == 0 and t == 6 and q.within(NB):
                    pe.wait_ge(S["maskN_d"], c + 1)
                    bank_free(pe, b, "rank")
                    both(lambda k: mm(psA[:, k, :], maskN[:, k, :], upper[:, :])).then_inc(S["rank_d"], 1)
                q = rf_pair(b)
                c = q.pair
                if b.p2 == 1 and t == 2 and q.within(NB):
                    pe.wait_ge(S["h1_d"], 2 * c + 2)
                    bank_free(pe, b, "h1T")
                    both(lambda k: nc.tensor.transpose(psA[:, k, :], h1[:, k, :], ident))\
                        .then_inc(S["h1Tp"], 1)
                if b.p2 == 1 and t == 6 and q.within(NB):
                    pe.wait_ge(S["h1T_d"], c + 1)
                    bank_free(pe, b, "rf")
                    both(lambda k: mm(psA[:, k, :], h1T[:, k, :], WaT)).then_inc(S["rfp"], 1)

            def rest_products(b, t):
                s, d = b + -E_STEP, (b + -E_STEP).pair
                if b.p2 == 0 and s.within(NB) and t == 0:
                    pe.wait_ge(S["dsp_d"], d + 1)
                    bank_free(pe, b, "e")
                    both(lambda k: mm(psA[:, k, :], dsp[:, k, :], Wd2T)).then_inc(S["ep"], 1)
                if b.p2 == 0 and s.within(NB) and t == 8:
                    pe.wait_ge(S["h2_d"], 2 * d + 2)
                    pe.wait_ge(S["adjM_d"], d + 1)
                    bank_free(pe, b, "hn1")
                    both(lambda k: mm(psA[:, k, :], hs[0][:, k, :], adjM[s.pp][:, k, :])).then_inc(S["hn_p1"], 1)
                s, d = b + -Z1_STEP, (b + -Z1_STEP).pair
                if b.p2 == 1 and s.within(NB) and t == 0:
                    pe.wait_ge(S["hn_c1"], d + 1)
                    bank_free(pe, b, "z1")
                    both(lambda k: mm(psA[:, k, :], hnT[:, k, :], lw)).then_inc(S["z_p"], 1)
                if b.p2 == 1 and s.within(NB) and t == 8:
                    pe.wait_ge(S["st_d"], 2 * d + 1)
                    bank_free(pe, b, "hn2")
                    both(lambda k: mm(psA[:, k, :], hs[1][:, k, :], adjM[s.pp][:, k, :])).then_inc(S["hn_p2"], 1)
                s, d = b + -Z2_STEP, (b + -Z2_STEP).pair
                if b.p2 == 0 and s.within(NB) and t == 2:
                    pe.wait_ge(S["hn_c2"], d + 1)
                    bank_free(pe, b, "z2")
                    both(lambda k: mm(psA[:, k, :], hnT[:, k, :], lw)).then_inc(S["z_p"], 1)
                s, d = b + -D_STEP, (b + -D_STEP).pair
                if b.p2 == 1 and s.within(NB) and t == 4:
                    pe.wait_ge(S["yT_d"], 2 * d + 2)
                    bank_free(pe, b, "d")
                    mm(psA, Wd1T, yT[:, :, :]).then_inc(S["dp"], 1)

            def step(b):
                if b.static and b.c == FLAGS_STEP + 1:
                    pe.wait_ge(S["flags_d"], 1)
                    pe.wait_ge(S["ex_d"], 2 * NB)
                    mm(psX[:, 0, 0:1], ones[:, :], flags[:, :]).then_inc(S["count_d"], 1)
                for t in range(0, TILES, 2):
                    e, u = filter_tile(b, t)
                    if b.within(NB):
                        operands(b, t)
                    if b.within(NB) or e.within(NB):
                        read = TILES * b.n + t - 2
                        wait(pe, S["w_d"], min(read, TILES * NB) if b.static else read)
                    if e.within(NB):
                        wait(pe, S["msg_d"], TILES * e.n + u - 2)
                    if b.within(NB):
                        expand(b, t)
                        expand(b, t + 1)
                    if t in ROUND_SLOT and (b + -2).within(NB):
                        first_product(b + -2, ROUND_SLOT.index(t))
                    if e.within(NB):
                        filters(b, t, e, u)
                        filters(b, t + 1, e, u + 1)
                    if t == 2:
                        rows_and_offsets(b)
                    prep_products(b, t)
                    rest_products(b, t)
                    e, u = scatter_tile(b, t)
                    if e.within(NB):
                        scatter(e, u)
                        scatter(e, u + 1)

            steps(pe, step)

        @block.vector
        def _(dve):
            v = nc.vector
            v.memset(most[:, :], 0.0).then_inc(S["w_cast"], 1)
            v.memset(half_c[:, :], 0.5).then_inc(S["w_cast"], 1)
            v.memset(mhalf[:, :], -0.5).then_inc(S["w_cast"], 1)
            v.memset(ones[:, :], 1.0).then_inc(S["w_cast"], 1)
            v.memset(one_c[:, :], 1.0).then_inc(S["w_cast"], 1)
            dve.wait_ge(S["w_in"], 16)
            v.tensor_copy(upper[:, :], cst[:, C_U:C_U + P]).then_inc(S["w_cast"], 1)
            v.tensor_copy(upper_s[:, :], cst[:, C_US:C_US + P]).then_inc(S["w_cast"], 1)
            dve.wait_ge(S["w_tr"], 4)
            v.tensor_copy(wT[:, 0:4, :], psW).then_inc(S["w_done"], 1)
            dve.wait_ge(S["w_tr2"], 1)
            v.tensor_copy(wT[:, 4, :], psA[:, 0, :]).then_inc(S["w_done"], 1)
            dve.wait_ge(S["w_cast"], 7)

            def moments(c, xt, bn, mv, s_bn, s_mv, stage):
                if stage == 0:
                    wait(dve, s_mv, 2 * c)
                    for k in range(2):
                        v.bn_stats(bn[:, k, :], xt[:, k, :]).then_inc(s_bn, 1)
                if stage == 1:
                    dve.wait_ge(s_bn, 2 * c + 2)
                    settle(dve, S)
                    for k in range(2):
                        v.bn_aggr(mv[:, k, :], bn[:, k, :]).then_inc(s_mv, 1)

            def list_edges(b, t):
                c = t // 2
                dve.wait_ge(S["gc_d"], TILES // 2 * b.n + c + 1)
                if t in (0, 8):
                    wait(dve, S["y_mm"], TILES * (b.n - 4) + (TILES if t else 8))
                if t == 0:
                    wait(dve, S["et_d"], b.n - 3)
                v.scalar_tensor_tensor(Wsc[b.p4][:, t * P:(t + 1) * P], Ksb[:, (b.p2 + c) % 2, t % 2, :],
                                       tcol[:, t:t + 1], psT[:, bank(b, t), 1, :], ALU.is_equal, ALU.mult,
                                       accum_out=eT[b.p4][:, t:t + 1]).then_inc(S["w_d"], 1)

            def message(b, t, e, u):
                dve.wait_ge(S["gw_d"], TILES * e.n + u // 2 * 2 + 2)
                wait(dve, S["y_mm"], TILES * e.n + u - 4)
                v.scalar_tensor_tensor(msg[:, u % 5, :], psT[:, bank(b, t), 3, :], eT[e.p4][:, u:u + 1],
                                       Gsb[e.p4][:, u * P:(u + 1) * P], ALU.mult, ALU.mult)\
                 .then_inc(S["msg_d"], 1)

            def column_bounds(m, t):
                if t == 3:
                    if m.static and m.c == 0:
                        dve.wait_ge(S["iota_in"], 16)
                    dve.wait_ge(S["oo_d"], m.pair + 1)
                    wait(dve, S["Q_d"], 2 * m.n)
                    v.tensor_scalar(Qend[:, :], iota[:, :], oo[m.pp][:, 1, m.p2:m.p2 + 1], None, ALU.is_gt)\
                     .then_inc(S["Qe_d"], 1)
                if t == 3:
                    v.tensor_scalar(Qbeg[:, :], iota[:, :], oo[m.pp][:, 0, m.p2:m.p2 + 1], None, ALU.is_gt)\
                     .then_inc(S["Qb_d"], 1)

            def sum_out(e):
                dve.wait_ge(S["y_mm"], TILES * e.n + TILES)
                if e.p2 == 0:
                    wait(dve, S["dp"], e.pair)
                v.tensor_copy(yT[:, e.p2, :], psY[:, 0, :]).then_inc(S["yT_d"], 1)

            def silu(d, n, stage):
                at = 2 * d + n
                if stage == 0:
                    dve.wait_ge(S["z_p"], at)
                    dve.wait_ge(S["row_in"], 16)
                    wait(dve, S["st_d"], at - 1)
                    v.tensor_tensor(zs[:, :, :], psA, lb_bc, ALU.add).then_inc(S["zs_d"], 1)
                if stage == 1:
                    dve.wait_ge(S["zln_d"], at)
                    wait(dve, S["zgate_d"], at - 1)
                    v.scalar_tensor_tensor(zsig[:, :, :], zs[:, :, :], 0.0, zln[:, :, :], ALU.min, ALU.subtract)\
                     .then_inc(S["zsig_d"], 1)
                if stage == 2:
                    dve.wait_ge(S["zgate_d"], at)
                    wait(dve, S["hn_p2" if n == 1 else "res_d"], d)
                    v.tensor_tensor(hs[n][:, :, :], zs[:, :, :], zgate[:, :, :], ALU.mult).then_inc(S["st_d"], 1)

            def prep_vectors(b, t):
                q = rf_pair(b)
                c = q.pair
                if b.p2 == 0 and q.within(NB):
                    if t == 0:
                        dve.wait_ge(S[f"x_in{q.pp}"], 16 * q.half + 16)
                        moments(c, xin[q.pp], bn1, mv1, S["bn1_d"], S["mv1_d"], 0)
                    if t == 1:
                        wait(dve, S["nm1_d"], c)
                        moments(c, xin[q.pp], bn1, mv1, S["bn1_d"], S["mv1_d"], 1)
                q = prep_pair(b)
                c = q.pair
                if not q.within(NB):
                    return
                if b.p2 == 0:
                    if t == 4:
                        dve.wait_ge(S["adjTp"], c + 1)
                        wait(dve, S["adjL_d"], c - 1)
                        wait(dve, S["adjS_d"], c - 1)
                        wait(dve, S["adjQ_d"], c - 1)
                        wait(dve, S["maskT_d"], c - 1)
                        v.tensor_copy(adjT[q.pp][:, :, :], psA).then_inc(S["adjT_d"], 1)
                    if t == 6:
                        dve.wait_ge(S["rank_d"], c + 1)
                        wait(dve, S["key_d"], 2 * c)
                        v.tensor_copy(rank[:, :, :], psA).then_inc(S["rank_c"], 1)
                    if t == 7:
                        dve.wait_ge(S["rank_c"], c + 1)
                        wait(dve, S["offs_d"], c)
                        v.tensor_copy(deg[:, :], rank[:, :, P - 1]).then_inc(S["deg_d"], 1)
                else:
                    if t == 2:
                        dve.wait_ge(S["offs_d"], c + 1)
                        if (b + -1).within(NB):
                            dve.wait_ge(S["erow_d"], b.n)
                        wait(dve, S["key_d"], 2 * c - 2)
                        wait(dve, S["Qb_d"], 2 * c - 2)
                        wait(dve, S["Qe_d"], 2 * c - 2)
                        wait(dve, S["most_d"], c - 1)
                        v.tensor_copy(oo[q.pp][:, :, :], psO).then_inc(S["oo_d"], 1)
                    if t == 5:
                        dve.wait_ge(S["oo_d"], c + 1)
                        dve.wait_ge(S["maskT_d"], c + 1)
                        wait(dve, S["kx_d"], 2 * TILES * (c - 1))
                        for k in range(2):
                            v.scalar_tensor_tensor(parts[q.pp][:, k, 0, :], rank[:, k, :],
                                                   oo[q.pp][:, 0, k:k + 1], maskT[:, k, :],
                                                   ALU.add, ALU.mult).then_inc(S["key_d"], 1)
                    if t == 6:
                        wait(dve, S["most_d"], c)
                        v.tensor_tensor(most[:, :], most[:, :], oo[q.pp][:, 1, :], ALU.max)\
                         .then_inc(S["most_d"], 1)

            def rest_vectors(b, t):
                s, d = b + -D_STEP, (b + -D_STEP).pair
                if b.p2 == 1 and s.within(NB):
                    if t == 4:
                        dve.wait_ge(S["dp"], d + 1)
                        wait(dve, S["dsp_d"], d)
                        v.tensor_scalar(ds[:, :, :], psA, bd1c, None, ALU.add).then_inc(S["ds_d"], 1)
                    if t == 8:
                        dve.wait_ge(S["dln_d"], d + 1)
                        wait(dve, S["ep"], d)
                        v.scalar_tensor_tensor(dsp[:, :, :], ds[:, :, :], 0.0, dln[:, :, :], ALU.max, ALU.add)\
                         .then_inc(S["dsp_d"], 1)
                s, d = b + -E_STEP, (b + -E_STEP).pair
                if b.p2 == 0 and s.within(NB):
                    if t == 0:
                        dve.wait_ge(S["ep"], d + 1)
                        dve.wait_ge(S["xb_d"], d + 1)
                        wait(dve, S["res_d"], d - 1)
                        wait(dve, S["h2_d"], 2 * d - 2)
                        v.tensor_tensor(x2[s.pp][:, :, :], psA, xb[:, :, :], ALU.add)\
                         .then_inc(S["x2_d"], 1)
                    if t == 1:
                        dve.wait_ge(S["x2_d"], d + 1)
                        moments(d, x2[s.pp], bn2, mv2, S["bn2_d"], S["mv2_d"], 0)
                    if t == 2:
                        wait(dve, S["nm2_d"], d)
                        moments(d, x2[s.pp], bn2, mv2, S["bn2_d"], S["mv2_d"], 1)
                s = b + -Z1_STEP
                if b.p2 == 1 and s.within(NB) and t in SILU1_SLOT:
                    silu(s.pair, 1, SILU1_SLOT.index(t))
                s = b + -Z2_STEP
                if b.p2 == 0 and s.within(NB) and t in SILU2_SLOT:
                    silu(s.pair, 2, SILU2_SLOT.index(t))
                    if last_pair(s) and t == SILU2_SLOT[2]:
                        dve.wait_ge(S["st_d"], 2 * s.pair + 2)
                        dve.wait_ge(S[f"o_out{s.pp}"], 16 * s.half)
                        dve.wait_ge(S["res_d"], s.pair)
                        v.tensor_tensor(res[s.pp][:, :, :], x2[s.pp][:, :, :], hs[2][:, :, :], ALU.add)\
                         .then_inc(S["res_d"], 1)

            SILU1_SLOT, SILU2_SLOT = [0, 4, 5], [2, 4, 8]

            def find_flags():
                v.tensor_reduce(bound[:, 0:1], wraw[:, 0, 0:NG], AX.X, ALU.add, apply_absolute_value=True)\
                 .then_inc(S["bound_d"], 1)
                v.tensor_scalar(bound[:, 1:2], b1c, -1.0, None, ALU.mult).then_inc(S["bound_d"], 1)
                dve.wait_ge(S["bound_d"], 2)
                v.tensor_tensor(bound[:, 1:2], bound[:, 1:2], b1c, ALU.max).then_inc(S["bound_d"], 1)
                dve.wait_ge(S["bound_d"], 3)
                v.tensor_tensor(bound[:, 2:3], bound[:, 0:1], bound[:, 1:2], ALU.add).then_inc(S["bound_d"], 1)
                dve.wait_ge(S["most_d"], NB // 2)
                v.tensor_tensor(bound[:, 3:4], most[:, 0:1], most[:, 1:2], ALU.max).then_inc(S["bound_d"], 1)
                dve.wait_ge(S["bound_d"], 5)
                v.tensor_scalar(bound[:, 2:3], bound[:, 2:3], SAFE, None, ALU.is_gt).then_inc(S["bound_d"], 1)
                dve.wait_ge(S["bound_d"], 6)
                v.scalar_tensor_tensor(flags[:, :], bound[:, 3:4], float(LIMIT), bound[:, 2:3],
                                       ALU.is_gt, ALU.add).then_inc(S["flags_d"], 1)

            def step(b):
                if b.static and b.c == FLAGS_STEP:
                    find_flags()
                if b.static and b.c == FLAGS_STEP + 2:
                    dve.wait_ge(S["count_d"], 1)
                    v.tensor_copy(flag[:, :], psX[:, 0, 0:1]).then_inc(S["flag_d"], 1)
                for t in range(TILES):
                    e, u = filter_tile(b, t)
                    if t == 1 and (b + -4).within(NB):
                        sum_out(b + -4)
                    if t % 2 == 1:
                        for k in (1, 0):
                            if b.within(NB):
                                list_edges(b, t - k)
                        for k in (1, 0):
                            if e.within(NB):
                                message(b, t - k, e, u - k)
                    rest_vectors(b, t)
                    prep_vectors(b, t)
                    if (b + 1).within(NB):
                        column_bounds(b + 1, t)

            steps(dve, step)

        @block.scalar
        def _(act):
            a = nc.scalar.activation
            nc.scalar.preload_act_table_set("natural_log_exp_and_others")
            act.wait_ge(S["w_in"], 16)
            act.wait_ge(S["w_cast"], 7)

            def hidden(e, c, stage):
                part = ROUNDS[c]
                exp_at = ex[:, :].rearrange("p (s n) -> p s n", s=2)[:, :, part]
                hid_at = hid[e.p2][:, :].rearrange("p (s n) -> p s n", s=2)[:, :, part]
                if stage == 0:
                    act.wait_ge(S["x_d"], 4 * e.n + 2 * c + 2)
                    wait(act, S["hid_d"], 2 * e.n + c - 1)
                    a(exp_at, psX[:, :, 0:part.stop - part.start], ACT.Exp, bias=b1c).then_inc(S["ex_d"], 1)
                else:
                    act.wait_ge(S["ex_d"], 2 * e.n + c + 1)
                    wait(act, S["gw_d"], TILES * e.n - TILES)
                    a(hid_at, exp_at, ACT.Ln, bias=half_c[:, :], scale=0.5).then_inc(S["hid_d"], 1)

            def softplus_of_d(d, stage):
                if stage == 0:
                    act.wait_ge(S["ds_d"], d + 1)
                    a(dabs[:, :, :], ds[:, :, :], ACT.Abs).then_inc(S["abs_d"], 1)
                if stage == 1:
                    act.wait_ge(S["abs_d"], d + 1)
                    a(dexp[:, :, :], dabs[:, :, :], ACT.Exp, scale=-1.0).then_inc(S["dexp_d"], 1)
                if stage == 2:
                    act.wait_ge(S["dexp_d"], d + 1)
                    wait(act, S["dsp_d"], d)
                    a(dln[:, :, :], dexp[:, :, :], ACT.Ln, bias=half_c[:, :], scale=0.5).then_inc(S["dln_d"], 1)

            def silu(d, n, stage):
                at = 2 * d + n
                if stage == 0:
                    act.wait_ge(S["zs_d"], at)
                    a(zabs[:, :, :], zs[:, :, :], ACT.Abs).then_inc(S["zabs_d"], 1)
                    act.wait_ge(S["zabs_d"], at)
                    a(zexp[:, :, :], zabs[:, :, :], ACT.Exp, scale=-1.0).then_inc(S["zexp_d"], 1)
                    act.wait_ge(S["zexp_d"], at)
                    wait(act, S["zsig_d"], at - 1)
                    a(zln[:, :, :], zexp[:, :, :], ACT.Ln, bias=one_c[:, :]).then_inc(S["zln_d"], 1)
                if stage == 1:
                    act.wait_ge(S["zsig_d"], at)
                    wait(act, S["st_d"], at - 1)
                    a(zgate[:, :, :], zsig[:, :, :], ACT.Exp).then_inc(S["zgate_d"], 1)

            def normalized(dst, src, rs, nm, s_dst):
                for k in range(2):
                    a(dst[:, k, :], src[:, k, :], ACT.Relu, bias=nm[:, k:k + 1], scale=rs[:, k:k + 1])\
                        .then_inc(s_dst, 1)

            def chunk_copies(b, t):
                h, k = t // 2, bank(b, t - 1)
                if not b.within(NB):
                    return
                act.wait_ge(S["kx_d"], TILES * b.n + 2 * h + 2)
                e, u = filter_tile(b, t)
                if e.within(NB):
                    act.wait_ge(S["gw_d"], TILES * e.n + u + 1)
                wait(act, S["w_d"], TILES * b.n + 2 * (h - 1))
                a(Ksb[:, (b.p2 + h) % 2], psT[:, k:k + 2, 0, :], ACT.Copy)
                if t == 1:
                    wait(act, S["msg_d"], TILES * (b.n - 3))
                a(Gsb[b.p4][:, (t - 1) * P:(t + 1) * P].rearrange("p (k n) -> p k n", k=2), psT[:, k:k + 2, 2, :],
                  ACT.Copy).then_inc(S["gc_d"], 1)

            def step(b):
                q, p, m = rf_pair(b), prep_pair(b), b + -1
                c, prep = q.pair, q.within(NB)
                s_d, s_e, s_1, s_2 = (b + -n for n in (D_STEP, E_STEP, Z1_STEP, Z2_STEP))
                even, odd = b.p2 == 0, b.p2 == 1
                f, rounds = b + -2, (b + -2).within(NB)
                for t in range(TILES):
                    if t % 2 == 1:
                        chunk_copies(b, t)
                    if t == 1 and rounds:
                        act.wait_ge(S["dsq_d"], f.n + 1)
                        wait(act, S["x_d"], 4 * f.n)
                        a(gau[:, :], dsq[:, :], ACT.Exp, scale=COEFF).then_inc(S["gau_d"], 1)
                    if t == 2 and m.within(NB):
                        act.wait_ge(S["et_d"], m.n + 1)
                        if odd and p.within(NB):
                            act.wait_ge(S["offs_d"], p.pair + 1)
                        wait(act, S["e_out"], 16 * (m.n - 1))
                        a(erow[m.p2][:, :], psE, ACT.Copy).then_inc(S["erow_d"], 1)
                    if t == 2 and odd and prep:
                        act.wait_ge(S["h1Tp"], c + 1)
                        wait(act, S["rfp"], c)
                        a(h1T[:, :, :], psA, ACT.Copy).then_inc(S["h1T_d"], 1)
                    if t == 3 and odd and s_1.within(NB):
                        silu(s_1.pair, 1, 0)
                    if t == 3 and even and s_2.within(NB):
                        silu(s_2.pair, 2, 0)
                    if t == 4 and rounds:
                        hidden(f, 0, 0)
                    if t == 5 and even and s_e.within(NB):
                        act.wait_ge(S["nm2_d"], s_e.pair + 1)
                        wait(act, S["hn_p1"], s_e.pair)
                        normalized(hs[0], x2[s_e.pp], rs2, nm2, S["h2_d"])
                    if t == 5 and odd and s_1.within(NB):
                        silu(s_1.pair, 1, 1)
                    if t == 5 and odd and s_d.within(NB):
                        softplus_of_d(s_d.pair, 0)
                    if t == 5 and rounds:
                        hidden(f, 0, 1)
                    if t == 6 and odd and s_d.within(NB):
                        softplus_of_d(s_d.pair, 1)
                    if t == 6 and odd and rounds:
                        hidden(f, 1, 0)
                    if t == 7 and odd and prep:
                        act.wait_ge(S["rfp"], c + 1)
                        wait(act, S["rfS_d"], c - 1)
                        wait(act, S["rfhi"], c - 1)
                        wait(act, S["rfb_d"], c - 1)
                        a(rf[q.pp][:, :, :], psA, ACT.Copy).then_inc(S["rf_d"], 1)
                    if t == 7 and odd and s_d.within(NB):
                        softplus_of_d(s_d.pair, 2)
                    if t == 7 and even and rounds:
                        hidden(f, 1, 0)
                    if t == 7 and even and s_2.within(NB):
                        silu(s_2.pair, 2, 1)
                    if t == 7 and rounds:
                        hidden(f, 1, 1)
                    if t == 9:
                        s, n = (s_e, 1) if even else (s_1, 2)
                        if s.within(NB):
                            act.wait_ge(S[f"hn_p{n}"], s.pair + 1)
                            wait(act, S["z_p"], 2 * s.pair + n - 1)
                            a(hnT[:, :, :], psA, ACT.Copy).then_inc(S[f"hn_c{n}"], 1)
                    if t == 9 and even and prep:
                        act.wait_ge(S["nm1_d"], c + 1)
                        wait(act, S["h1Tp"], c)
                        normalized(h1, xin[q.pp], rs1, nm1, S["h1_d"])
                    if t == 9 and m.within(NB):
                        act.wait_ge(S[f"eb_in{m.p2}"], 32 * (2 * m.half + m.p4 // 2) + 32)
                        wait(act, S["gau_d"], m.n)
                        a(dsq[:, :], eb[m.p2][:, :], ACT.Square, bias=neg_off).then_inc(S["dsq_d"], 1)

            steps(act, step)

        @block.gpsimd
        def _(pool):
            g = nc.gpsimd
            pool.wait_ge(S["w_cast"], 7)

            def split(hi, lo, src, s_hi, s_all, c, read):
                read()
                settle(pool, S)
                g.tensor_copy(hi, src).then_inc(s_hi, 1)
                pool.wait_ge(s_hi, c + 1)
                g.tensor_tensor(lo, src, hi, ALU.subtract).then_inc(s_all, 1)

            def deviations(c, mv, tt, rs, nm, names, read):
                s_mv, s_ve, s_ng, s_rs, s_nm = (S[k] for k in names)
                pool.wait_ge(s_mv, 2 * c + 2)
                wait(pool, s_nm, c)
                settle(pool, S)
                g.tensor_scalar(tt[:, 0], mv[:, :, 1], EPS, None, ALU.add).then_inc(s_ve, 1)
                g.tensor_scalar(tt[:, 1], mv[:, :, 0], -1.0, None, ALU.mult).then_inc(s_ng, 1)
                pool.wait_ge(s_ve, c + 1)
                wait(pool, read, 2 * c)
                g.tensor_tensor(rs[:, :], tt[:, 0], mhalf[:, :], ALU.pow).then_inc(s_rs, 1)
                pool.wait_ge(s_ng, c + 1)
                pool.wait_ge(s_rs, c + 1)
                g.tensor_tensor(nm[:, :], tt[:, 1], rs[:, :], ALU.mult).then_inc(s_nm, 1)

            def owners(m):
                if not m.within(NB):
                    return
                pool.wait_ge(S["Qe_d"], m.n + 1)
                pool.wait_ge(S["Qb_d"], m.n + 1)
                for h in range(2):
                    part = slice(h * HALF, (h + 1) * HALF)
                    wait(pool, S["kx_d"], TILES * (m.n - 2) + (h + 1) * TILES // 2)
                    g.tensor_tensor(Q[m.p2][:, part], Qbeg[:, part], Qend[:, part], ALU.subtract)\
                     .then_inc(S["Q_d"], 1)

            def even_step(b):
                q = prep_pair(b)
                c = q.pair
                if q.within(NB):
                    pool.wait_ge(S[f"a_in{q.pp}"], 16 * q.half + 16)
                    wait(pool, S["rank_d"], c)
                    settle(pool, S)
                    g.tensor_scalar(maskN[:, :, :], adjin[q.pp][:, :, :], 0.0, 0.0, ALU.is_equal, ALU.is_equal)\
                     .then_inc(S["maskN_d"], 1)
                s = b + -E_STEP
                if s.within(NB):
                    deviations(s.pair, mv2, tt2, rs2, nm2, ("mv2_d", "ve2_d", "ng2_d", "rs2_d", "nm2_d"),
                               S["h2_d"])
                f = rf_pair(b)
                if f.within(NB):
                    deviations(f.pair, mv1, tt1, rs1, nm1, ("mv1_d", "ve1_d", "ng1_d", "rs1_d", "nm1_d"), S["h1_d"])
                owners(b + 1)
                if q.within(NB):
                    pool.wait_ge(S["adjT_d"], c + 1)
                    aT = adjT[q.pp][:, :, :]
                    wait(pool, S["key_d"], 2 * c)
                    settle(pool, S)
                    g.tensor_scalar(maskT[:, :, :], aT, 0.0, 0.0, ALU.is_equal, ALU.is_equal).then_inc(S["maskT_d"], 1)
                    split(parts[q.pp][:, :, 1, :], parts[q.pp][:, :, 3, :], aT, S["ahi"], S["adjS_d"], c,
                          lambda: wait(pool, S["kx_d"], 2 * TILES * (c - 1)))
                r = b + -4
                if r.within(NB):
                    pool.wait_ge(S["adjL_d"], r.pair + 1)
                    wait(pool, S["hn_p2"], r.pair - 1)
                    settle(pool, S)
                    g.tensor_copy(adjM[r.pp][:, :, :], adjL[r.pp][:, :, :]).then_inc(S["adjM_d"], 1)
                o = b + -Z2_STEP
                if o.within(NB) and not last_pair(o):
                    pool.wait_ge(S["st_d"], 2 * o.pair + 2)
                    wait(pool, S[f"o_out{o.pp}"], 16 * o.half)
                    g.tensor_tensor(res[o.pp][:, :, :], x2[o.pp][:, :, :], hs[2][:, :, :], ALU.add)\
                     .then_inc(S["res_d"], 1)

            def odd_step(b):
                q = prep_pair(b)
                if q.within(NB):
                    c = q.pair
                    pool.wait_ge(S["rf_d"], c + 1)
                    split(parts[q.pp][:, :, 2, :], parts[q.pp][:, :, 4, :], rf[q.pp][:, :, :], S["rfhi"],
                          S["rfS_d"], c, lambda: wait(pool, S["kx_d"], 2 * TILES * (c - 1)))
                r = b + -1
                if r.within(NB):
                    c = r.pair
                    pool.wait_ge(S["row_in"], 16)
                    wait(pool, S["y_mm"], 2 * TILES * (c - 1))
                    g.tensor_tensor(rfb[r.pp][:, :, :], rf[r.pp][:, :, :], b2_bc, ALU.mult)\
                     .then_inc(S["rfb_d"], 1)
                owners(b + 1)
                s = b + -D_STEP
                if s.within(NB):
                    pool.wait_ge(S[f"xp_in{s.pp}"], 16 * s.half + 16)
                    wait(pool, S["x2_d"], s.pair)
                    for k in range(2):
                        last = g.tensor_tensor(xb[:, k, :], xpost[s.pp][:, k, :], bd2_bc, ALU.add)
                    last.then_inc(S["xb_d"], 1)
                if r.within(NB):
                    g.tensor_tensor(adjQ[r.pp][:, :, :], adjT[r.pp][:, :, :], adjT[r.pp][:, :, :], ALU.mult)\
                     .then_inc(S["adjQ_d"], 1)
                    wait(pool, S["adjM_d"], c - 1)
                    settle(pool, S)
                    g.tensor_copy(adjL[r.pp][:, :, :], adjT[r.pp][:, :, :]).then_inc(S["adjL_d"], 1)

            def step(b):
                if b.p2 == 0:
                    even_step(b)
                else:
                    odd_step(b)

            steps(pool, step)

        block.__exit__(None, None, None)

        ORDER = {
            "pe": ("", "hT rf aT", "xp f y", "d e hn1 z1 hn2 z2"),
            "act": ("", "h hTc rfc", "dsq gau abs exp ln",
                    "dabs dexp dln h2 hc1 za1 ze1 zl1 zg1 hc2 za2 ze2 zl2 zg2"),
            "dve": ("", "bn mv aTc sq", "rel sum col filt msg ysb",
                    "ds dsp x2 bn2 mv2 zs1 zt1 st1 zs2 zt2 st2"),
            "pool": ("", "ve ng rs nm xb", "", "ve2 ng2 rs2 nm2 res"),
        }
        NQ = P // ROWS
        G = {k: sem("g_" + k) for k in ("pe", "act", "dve", "pool", "x", "adj", "eb", "out")}

        def after(eng, name, b=None, q=None):
            for owner, parts in ORDER.items():
                once, head, rows, tail = (p.split() for p in parts)
                graph = len(head) + NQ * len(rows) + len(tail)
                if name in once:
                    eng.wait_ge(G[owner], once.index(name) + 1)
                if name in head:
                    eng.wait_ge(G[owner], b * graph + (len(once) + head.index(name) + 1))
                if name in rows:
                    eng.wait_ge(G[owner], b * graph + q * len(rows) + (len(once) + len(head) + rows.index(name) + 1))
                if name in tail:
                    eng.wait_ge(G[owner], b * graph + (graph - len(tail) + len(once) + tail.index(name) + 1))

        gx, gadj, gsq = xin[0][:, 0, :], adjin[0][:, 0, :], xin[0][:, 1, :]
        geb, gdsq, ggau = eb[0][0:NG, 0:512], dsq[0:NG, 0:512], gau[0:NG, 0:512]
        gcol, gy, gmsg = cols2[:, :], yT[:, 0, :], msg[:, 0:ROWS, :]
        ps0, ps1, ps2, ps3 = psM[:, 0, :], psX[:, 0, :], psY[:, :, :], psX[:, 1, 0:ROWS]
        with nc.Block() as general:
            def needed(eng):
                return eng.value_load(flag[0:1, 0:1], min_val=0, max_val=2 * P)

            @general.sync
            def _(sp):
                sp.wait_ge(S["flag_d"], 1)
                with sp.If(needed(sp) > 0):
                    with sp.Fori(0, NB) as b:
                        sp.wait_ge(G["out"], 16 * b)
                        settle(sp, S)
                        sp.dma_start(gx, x[bass.ds(b, 1)].rearrange("b n d -> (b n) d")).then_inc(G["x"], 16)
                        sp.dma_start(gadj, adj[bass.ds(b, 1)].rearrange("b n d -> (b n) d"))\
                          .then_inc(G["adj"], 16)
                        with sp.Fori(0, NQ) as q:
                            n = b * NQ + q
                            once, head, rows, tail = (len(p.split()) for p in ORDER["dve"])
                            sp.wait_ge(G["dve"], b * (head + NQ * rows + tail) + q * rows + once + head)
                            settle(sp, S)
                            src = adj[bass.ds(b, 1), bass.ds(q * ROWS, ROWS), :].rearrange("b i j -> b (i j)")
                            sp.dma_start(geb, src.to_broadcast((NG, 512))).then_inc(G["eb"], 16)
                        after(sp, "res", b)
                        settle(sp, S)
                        sp.dma_start(out[bass.ds(b, 1)].rearrange("b n d -> (b n) d"), res[0][:, 0, :])\
                          .then_inc(G["out"], 16)
                    sp.wait_ge(G["out"], 16 * NB)

            @general.tensor
            def _(pe):
                def mm(o, a, b, start=True, stop=True):
                    return nc.tensor.matmul(o, a, b, start=start, stop=stop)

                pe.wait_ge(S["flag_d"], 1)
                with pe.If(needed(pe) > 0):
                    with pe.Fori(0, NB) as b:
                        after(pe, "h", b)
                        nc.tensor.transpose(ps0, h1[:, 0, :], ident).then_inc(G["pe"], 1)
                        after(pe, "hTc", b)
                        mm(ps0, h1T[:, 0, :], WaT).then_inc(G["pe"], 1)
                        after(pe, "rfc", b)
                        pe.wait_ge(G["adj"], 16 * b + 16)
                        nc.tensor.transpose(ps0, gadj, ident).then_inc(G["pe"], 1)
                        with pe.Fori(0, NQ) as q:
                            n = b * NQ + q
                            after(pe, "gau", b, q)
                            mm(ps1, W1T[0:NG, :], ggau).then_inc(G["pe"], 1)
                            after(pe, "sum", b, q)
                            for r in range(ROWS):
                                last = mm(ps2[:, r, :], hid[0][:, r * P:(r + 1) * P], W2T)
                            last.then_inc(G["pe"], 1)
                            after(pe, "msg", b, q)
                            after(pe, "col", b, q)
                            for r in range(ROWS):
                                last = mm(ps3[:, r:r + 1], gmsg[:, r, :], gcol[:, r:r + 1])
                            last.then_inc(G["pe"], 1)
                        after(pe, "ysb", b, NQ - 1)
                        mm(ps0, Wd1T, gy).then_inc(G["pe"], 1)
                        after(pe, "dsp", b)
                        mm(ps0, dsp[:, 0, :], Wd2T).then_inc(G["pe"], 1)
                        for k in (1, 2):
                            after(pe, "h2" if k == 1 else "st1", b)
                            mm(ps0, hs[k - 1][:, 0, :], adjT[0][:, 0, :]).then_inc(G["pe"], 1)
                            after(pe, f"hc{k}", b)
                            mm(ps0, hnT[:, 0, :], lw).then_inc(G["pe"], 1)

            @general.vector
            def _(dve):
                v = nc.vector
                dve.wait_ge(S["flag_d"], 1)
                with dve.If(needed(dve) > 0):
                    with dve.Fori(0, NB) as b:
                        dve.wait_ge(G["x"], 16 * b + 16)
                        v.bn_stats(bn1[:, 0, :], gx).then_inc(G["dve"], 1)
                        after(dve, "bn", b)
                        settle(dve, S)
                        v.bn_aggr(mv1[:, 0, :], bn1[:, 0, :]).then_inc(G["dve"], 1)
                        after(dve, "aT", b)
                        v.tensor_copy(adjT[0][:, 0, :], ps0).then_inc(G["dve"], 1)
                        after(dve, "aTc", b)
                        v.tensor_tensor(gsq, adjT[0][:, 0, :], adjT[0][:, 0, :], ALU.mult).then_inc(G["dve"], 1)
                        after(dve, "sq", b)
                        settle(dve, S)
                        with dve.Fori(0, NQ) as q:
                            n = b * NQ + q
                            after(dve, "ln", b, q)
                            v.tensor_scalar(ex[:, 512:1024], ps1, b1c, 0.0, ALU.add, ALU.max)\
                             .then_inc(G["dve"], 1)
                            after(dve, "rel", b, q)
                            v.tensor_tensor(hid[0][:, 0:512], ex[:, 0:512], ex[:, 512:1024], ALU.add)\
                             .then_inc(G["dve"], 1)
                            v.tensor_copy(gcol, xin[0][:, 1, bass.ds(q * ROWS, ROWS)]).then_inc(G["dve"], 1)
                            after(dve, "f", b, q)
                            for r in range(ROWS):
                                last = v.tensor_tensor(ex[:, r * P:(r + 1) * P], ps2[:, r, :], b2_bc[:, 0, :],
                                                       ALU.add)
                            last.then_inc(G["dve"], 1)
                            after(dve, "filt", b, q)
                            for r in range(ROWS):
                                last = v.tensor_tensor(gmsg[:, r, :], ex[:, r * P:(r + 1) * P], rf[0][:, 0, :],
                                                       ALU.mult)
                            last.then_inc(G["dve"], 1)
                            after(dve, "y", b, q)
                            v.tensor_copy(yT[:, 0, bass.ds(q * ROWS, ROWS)], ps3).then_inc(G["dve"], 1)
                        after(dve, "d", b)
                        v.tensor_scalar(ds[:, 0, :], ps0, bd1c, None, ALU.add).then_inc(G["dve"], 1)
                        after(dve, "dln", b)
                        v.scalar_tensor_tensor(dsp[:, 0, :], ds[:, 0, :], 0.0, dln[:, 0, :], ALU.max, ALU.add)\
                         .then_inc(G["dve"], 1)
                        after(dve, "xb", b)
                        after(dve, "e", b)
                        v.tensor_tensor(x2[0][:, 0, :], ps0, xb[:, 0, :], ALU.add).then_inc(G["dve"], 1)
                        after(dve, "x2", b)
                        v.bn_stats(bn2[:, 0, :], x2[0][:, 0, :]).then_inc(G["dve"], 1)
                        after(dve, "bn2", b)
                        settle(dve, S)
                        v.bn_aggr(mv2[:, 0, :], bn2[:, 0, :]).then_inc(G["dve"], 1)
                        for k in (1, 2):
                            after(dve, f"z{k}", b)
                            v.tensor_tensor(zs[:, 0, :], ps0, lb_bc[:, 0, :], ALU.add).then_inc(G["dve"], 1)
                            after(dve, f"zl{k}", b)
                            v.scalar_tensor_tensor(zsig[:, 0, :], zs[:, 0, :], 0.0, zln[:, 0, :], ALU.min,
                                                   ALU.subtract).then_inc(G["dve"], 1)
                            after(dve, f"zg{k}", b)
                            v.tensor_tensor(hs[k][:, 0, :], zs[:, 0, :], zgate[:, 0, :], ALU.mult)\
                             .then_inc(G["dve"], 1)

            @general.scalar
            def _(act):
                a = nc.scalar.activation
                act.wait_ge(S["flag_d"], 1)
                with act.If(needed(act) > 0):
                    nc.scalar.preload_act_table_set("natural_log_exp_and_others")
                    with act.Fori(0, NB) as b:
                        after(act, "nm", b)
                        a(h1[:, 0, :], gx, ACT.Relu, bias=nm1[:, 0:1], scale=rs1[:, 0:1]).then_inc(G["act"], 1)
                        after(act, "hT", b)
                        a(h1T[:, 0, :], ps0, ACT.Copy).then_inc(G["act"], 1)
                        after(act, "rf", b)
                        a(rf[0][:, 0, :], ps0, ACT.Copy).then_inc(G["act"], 1)
                        after(act, "sq", b)
                        with act.Fori(0, NQ) as q:
                            n = b * NQ + q
                            act.wait_ge(G["eb"], 16 * n + 16)
                            a(gdsq, geb, ACT.Square, bias=cst[0:NG, C_NO:C_NO + 1]).then_inc(G["act"], 1)
                            after(act, "dsq", b, q)
                            a(ggau, gdsq, ACT.Exp, scale=COEFF).then_inc(G["act"], 1)
                            after(act, "xp", b, q)
                            a(ex[:, 0:512], ps1, ACT.Abs, bias=b1c).then_inc(G["act"], 1)
                            after(act, "abs", b, q)
                            a(ex[:, 512:1024], ex[:, 0:512], ACT.Exp, scale=-1.0).then_inc(G["act"], 1)
                            after(act, "exp", b, q)
                            a(ex[:, 0:512], ex[:, 512:1024], ACT.Ln, bias=half_c[:, :], scale=0.5)\
                                .then_inc(G["act"], 1)
                        after(act, "ds", b)
                        a(dabs[:, 0, :], ds[:, 0, :], ACT.Abs).then_inc(G["act"], 1)
                        after(act, "dabs", b)
                        a(dexp[:, 0, :], dabs[:, 0, :], ACT.Exp, scale=-1.0).then_inc(G["act"], 1)
                        after(act, "dexp", b)
                        a(dln[:, 0, :], dexp[:, 0, :], ACT.Ln, bias=half_c[:, :], scale=0.5)\
                            .then_inc(G["act"], 1)
                        after(act, "nm2", b)
                        a(hs[0][:, 0, :], x2[0][:, 0, :], ACT.Relu, bias=nm2[:, 0:1], scale=rs2[:, 0:1])\
                            .then_inc(G["act"], 1)
                        for k in (1, 2):
                            after(act, f"hn{k}", b)
                            a(hnT[:, 0, :], ps0, ACT.Copy).then_inc(G["act"], 1)
                            after(act, f"zs{k}", b)
                            a(zabs[:, 0, :], zs[:, 0, :], ACT.Abs).then_inc(G["act"], 1)
                            after(act, f"za{k}", b)
                            a(zexp[:, 0, :], zabs[:, 0, :], ACT.Exp, scale=-1.0).then_inc(G["act"], 1)
                            after(act, f"ze{k}", b)
                            a(zln[:, 0, :], zexp[:, 0, :], ACT.Ln, bias=one_c[:, :]).then_inc(G["act"], 1)
                            after(act, f"zt{k}", b)
                            a(zgate[:, 0, :], zsig[:, 0, :], ACT.Exp).then_inc(G["act"], 1)

            @general.gpsimd
            def _(pool):
                g = nc.gpsimd

                def deviation(b, mv, tt, rs, nm, names):
                    s_mv, s_ve, s_ng, s_rs = names
                    after(pool, s_mv, b)
                    settle(pool, S)
                    g.tensor_scalar(tt[:, 0, 0:1], mv[:, 0, 1:2], EPS, None, ALU.add).then_inc(G["pool"], 1)
                    g.tensor_scalar(tt[:, 1, 0:1], mv[:, 0, 0:1], -1.0, None, ALU.mult).then_inc(G["pool"], 1)
                    after(pool, s_ve, b)
                    g.tensor_tensor(rs[:, 0:1], tt[:, 0, 0:1], mhalf[:, 0:1], ALU.pow).then_inc(G["pool"], 1)
                    after(pool, s_ng, b)
                    after(pool, s_rs, b)
                    g.tensor_tensor(nm[:, 0:1], tt[:, 1, 0:1], rs[:, 0:1], ALU.mult).then_inc(G["pool"], 1)

                pool.wait_ge(S["flag_d"], 1)
                with pool.If(needed(pool) > 0):
                    with pool.Fori(0, NB) as b:
                        deviation(b, mv1, tt1, rs1, nm1, ("mv", "ve", "ng", "rs"))
                        pool.wait_ge(G["x"], 16 * b + 16)
                        g.tensor_tensor(xb[:, 0, :], gx, bd2_bc, ALU.add).then_inc(G["pool"], 1)
                        deviation(b, mv2, tt2, rs2, nm2, ("mv2", "ve2", "ng2", "rs2"))
                        after(pool, "st2", b)
                        g.tensor_tensor(res[0][:, 0, :], x2[0][:, 0, :], hs[2][:, 0, :], ALU.add)\
                         .then_inc(G["pool"], 1)


def kernel(**inputs):
    import numpy as np
    import concourse.bacc as bacc
    from concourse.bass_utils import run_bass_kernel_spmd

    k, m = np.arange(P)[:, None], np.arange(P)[None, :]
    slot = k + P * np.arange(TILES)[None, :] + 1
    offsets = -np.tile(np.linspace(0.0, CUTOFF, NG, dtype=np.float32), P // NG)[:, None]
    w = {name[3:]: a for name, a in inputs.items() if name.startswith("L0")}
    constants = [c.astype(np.float32) for c in (k == m, k <= m, k < m, slot, offsets)]
    columns = [*constants, w["gnn_b1"][:, None], w["gnn_bd1"][:, None],
               w["gnn_W1"], w["gnn_W1"], w["gnn_W2"], w["gnn_Wa"], w["gnn_Wd1"], w["gnn_Wd2"],
               inputs["L1_gnn_W"]]
    rows = [w["gnn_bd2"], w["gnn_b2"], w["gnn_b2"], inputs["L1_gnn_b"], inputs["L1_gnn_b"]]
    given = {
        "x": inputs["x"],
        "adj": inputs["adj"],
        "packed": np.concatenate([np.asarray(c) for c in columns], axis=1),
        "rows": np.concatenate([np.asarray(r) for r in rows])[None, :],
        "slots": np.arange(1, T + 1, dtype=np.float16)[None, :],
    }
    given = {name: np.ascontiguousarray(a) for name, a in given.items()}

    nc = bacc.Bacc("TRN2", target_bir_lowering=False, num_devices=1)
    arrays = {f"in_{name}": a for name, a in given.items()}
    args = [nc.dram_tensor(f"in_{name}", a.shape, mybir.dt.from_np(a.dtype), kind="ExternalInput").ap()
            for name, a in given.items()]
    out = nc.dram_tensor("out", given["x"].shape, F32, kind="ExternalOutput").ap()
    build(nc, *args, out)
    r = run_bass_kernel_spmd(nc, [arrays], core_ids=[0])
    return r.results[0]["out"]
```
